# Optimizing a Trainium2 kernel written in Bass

```python
import numpy as np
import jax
import jax.numpy as jnp

def _softmax(x, axis=-1):
    return jax.nn.softmax(x, axis=axis)

def _gelu(x):
    return jax.nn.gelu(x, approximate=True)

def _silu(x):
    return jax.nn.silu(x)

def _sigmoid(x):
    return jax.nn.sigmoid(x)

def _layernorm(x, axis=-1, eps=1e-05):
    m = jnp.mean(x, axis=axis, keepdims=True)
    v = jnp.var(x, axis=axis, keepdims=True)
    return (x - m) / jnp.sqrt(v + eps)

def _scatter_add(tgt, idx, src, axis=0):
    return tgt.at[idx].add(src)

def _segment_sum(src, seg, n):
    return jax.ops.segment_sum(src, seg, n)
kernel_name = 'mk_xattn_ffn_d1_seqx_r4_9c85bd'

def setup_inputs(seed: int=0):
    np.random.seed(seed)
    _w = jnp.asarray

    def _rec_inputs():
        import jax
        import jax.numpy as jnp
        _rk = jax.random.key(seed)
        x = -0.0002928 + 1 * jax.random.normal(jax.random.fold_in(_rk, 1), (8, 512, 256), jnp.float32)
        _lenS = 512 - jax.random.randint(jax.random.fold_in(_rk, 7), (8,), 0, max(1, 512 // 4) + 1, jnp.int32)
        _lenS2 = 512 - jax.random.randint(jax.random.fold_in(_rk, 8), (8,), 0, max(1, 512 // 4) + 1, jnp.int32)
        _ctx_1024P = jax.random.normal(jax.random.fold_in(_rk, 11), (8, 16, 256), jnp.float32)
        _ctx_1024c = jax.random.dirichlet(jax.random.fold_in(_rk, 511), 0.3 * jnp.ones((16,), jnp.float32), (8, 512))
        _ctx_1024t = jnp.einsum('bsk,bkd->bsd', _ctx_1024c, _ctx_1024P)
        _ctx_1024t = _ctx_1024t * jax.lax.rsqrt(jnp.mean(jnp.square(_ctx_1024t)) + 1e-12) * 0.953939
        ctx_1024 = -1.39393e-06 + 0.999914 * (_ctx_1024t + 0.3 * jax.random.normal(jax.random.fold_in(_rk, 611), (8, 512, 256), jnp.float32))
        return (x, ctx_1024)
    x, ctx_1024 = _rec_inputs()

    def _L0_xattn_setup():
        import jax, jax.numpy as jnp
        import numpy as np
        E = 256
        H = 16
        D = E // H
        NUM_BUCKETS = 32
        MAX_DISTANCE = 128

        def _relative_position_bucket(rel, num_buckets=NUM_BUCKETS, max_distance=MAX_DISTANCE):
            nb = num_buckets // 2
            buckets = (rel > 0).astype(jnp.int32) * nb
            rel = jnp.abs(rel)
            max_exact = nb // 2
            is_small = rel < max_exact
            rel_f = jnp.maximum(rel, 1).astype(jnp.float32)
            large = max_exact + (jnp.log(rel_f / max_exact) / np.log(max_distance / max_exact) * (nb - max_exact)).astype(jnp.int32)
            large = jnp.minimum(large, nb - 1)
            return buckets + jnp.where(is_small, rel, large)
        key = jax.random.key(seed)
        ks = jax.random.split(key, 6)
        B, S, K = (2, 512, 512)
        w = 0.02
        return {'hidden_states': jax.random.normal(ks[0], (B, S, E), jnp.float32), 'key_value_states': jax.random.normal(ks[1], (B, K, E), jnp.float32), 'Wq': jax.random.normal(ks[2], (E, E), jnp.float32) * w, 'Wkv': jax.random.normal(ks[3], (E, 2 * E), jnp.float32) * w, 'Wo': jax.random.normal(ks[4], (E, E), jnp.float32) * w, 'rel_bias': jax.random.normal(ks[5], (NUM_BUCKETS, H), jnp.float32) * w}
    _L0_xattn_all = _L0_xattn_setup()
    _L0_xattn_in = {k: v for k, v in _L0_xattn_all.items() if k in ('Wq', 'Wkv', 'Wo', 'rel_bias')}
    del _L0_xattn_all

    def _L0_ffn_setup():
        import jax, jax.numpy as jnp
        import numpy as np
        H = 256
        I = 128
        E = 32
        TOP_K = 6
        N_GROUP = 8
        TOPK_GROUP = 4
        SCALE = 2.5
        N_SHARED = 2
        SI = I * N_SHARED
        B, S = (2, 256)
        key = jax.random.key(seed)
        ks = jax.random.split(key, 8)
        x = jax.random.normal(ks[0], (B, S, H), jnp.float32)
        gate_weight = jax.random.normal(ks[1], (E, H), jnp.float32) * 0.02
        e_score_correction_bias = jax.random.normal(ks[2], (E,), jnp.float32) * 0.01
        experts_gate_up = jax.random.normal(ks[3], (E, 2 * I, H), jnp.float32) * 0.02
        experts_down = jax.random.normal(ks[4], (E, H, I), jnp.float32) * 0.02
        shared_gate_w = jax.random.normal(ks[5], (SI, H), jnp.float32) * 0.02
        shared_up_w = jax.random.normal(ks[6], (SI, H), jnp.float32) * 0.02
        shared_down_w = jax.random.normal(ks[7], (H, SI), jnp.float32) * 0.02
        return {'x': x, 'gate_weight': gate_weight, 'e_score_correction_bias': e_score_correction_bias, 'experts_gate_up': experts_gate_up, 'experts_down': experts_down, 'shared_gate_w': shared_gate_w, 'shared_up_w': shared_up_w, 'shared_down_w': shared_down_w}
    _L0_ffn_all = _L0_ffn_setup()
    _L0_ffn_in = {k: v for k, v in _L0_ffn_all.items() if k in ('gate_weight', 'e_score_correction_bias', 'experts_gate_up', 'experts_down', 'shared_gate_w', 'shared_up_w', 'shared_down_w')}
    del _L0_ffn_all
    return {'x': x, 'ctx_1024': ctx_1024, 'L0_xattn_Wq': _L0_xattn_in['Wq'], 'L0_xattn_Wkv': _L0_xattn_in['Wkv'], 'L0_xattn_Wo': _L0_xattn_in['Wo'], 'L0_xattn_rel_bias': _L0_xattn_in['rel_bias'], 'L0_ffn_gate_weight': _L0_ffn_in['gate_weight'], 'L0_ffn_e_score_correction_bias': _L0_ffn_in['e_score_correction_bias'], 'L0_ffn_experts_gate_up': _L0_ffn_in['experts_gate_up'], 'L0_ffn_experts_down': _L0_ffn_in['experts_down'], 'L0_ffn_shared_gate_w': _L0_ffn_in['shared_gate_w'], 'L0_ffn_shared_up_w': _L0_ffn_in['shared_up_w'], 'L0_ffn_shared_down_w': _L0_ffn_in['shared_down_w']}

def reference(x, ctx_1024, L0_xattn_Wq, L0_xattn_Wkv, L0_xattn_Wo, L0_xattn_rel_bias, L0_ffn_gate_weight, L0_ffn_e_score_correction_bias, L0_ffn_experts_gate_up, L0_ffn_experts_down, L0_ffn_shared_gate_w, L0_ffn_shared_up_w, L0_ffn_shared_down_w):
    import jax
    import jax.numpy as jnp

    def _L0_xattn_ref(hidden_states, key_value_states, Wq, Wkv, Wo, rel_bias):
        import jax, jax.numpy as jnp
        import numpy as np
        E = 256
        H = 16
        D = E // H
        NUM_BUCKETS = 32
        MAX_DISTANCE = 128

        def _relative_position_bucket(rel, num_buckets=NUM_BUCKETS, max_distance=MAX_DISTANCE):
            nb = num_buckets // 2
            buckets = (rel > 0).astype(jnp.int32) * nb
            rel = jnp.abs(rel)
            max_exact = nb // 2
            is_small = rel < max_exact
            rel_f = jnp.maximum(rel, 1).astype(jnp.float32)
            large = max_exact + (jnp.log(rel_f / max_exact) / np.log(max_distance / max_exact) * (nb - max_exact)).astype(jnp.int32)
            large = jnp.minimum(large, nb - 1)
            return buckets + jnp.where(is_small, rel, large)
        B, S, _ = hidden_states.shape
        K = key_value_states.shape[1]
        q = (hidden_states @ Wq).reshape(B, S, H, D).transpose(0, 2, 1, 3)
        kv = (key_value_states @ Wkv).reshape(B, K, 2, H, D)
        k = kv[:, :, 0].transpose(0, 2, 1, 3)
        v = kv[:, :, 1].transpose(0, 2, 1, 3)
        scores = jnp.einsum('bhsd,bhkd->bhsk', q, k)
        rel = jnp.arange(K)[None, :] - jnp.arange(S)[:, None]
        buckets = _relative_position_bucket(rel)
        bias = rel_bias[buckets].transpose(2, 0, 1)[None]
        scores = scores + bias
        attn = jax.nn.softmax(scores.astype(jnp.float32), axis=-1).astype(scores.dtype)
        out = jnp.einsum('bhsk,bhkd->bshd', attn, v).reshape(B, S, E)
        return out @ Wo

    def _L0_ffn_ref(x, gate_weight, e_score_correction_bias, experts_gate_up, experts_down, shared_gate_w, shared_up_w, shared_down_w):
        import jax, jax.numpy as jnp
        import numpy as np
        H = 256
        I = 128
        E = 32
        TOP_K = 6
        N_GROUP = 8
        TOPK_GROUP = 4
        SCALE = 2.5
        N_SHARED = 2
        SI = I * N_SHARED
        B, S = (2, 256)
        b, s, h = x.shape
        xf = x.reshape(-1, h)
        T = xf.shape[0]
        logits = xf.astype(jnp.float32) @ gate_weight.astype(jnp.float32).T
        scores = jax.nn.sigmoid(logits)
        sfc = scores + e_score_correction_bias[None, :]
        gs = E // N_GROUP
        group_scores = sfc.reshape(T, N_GROUP, gs).max(axis=-1)
        _, gidx = jax.lax.top_k(group_scores, TOPK_GROUP)
        gmask = jnp.zeros((T, N_GROUP), bool).at[jnp.arange(T)[:, None], gidx].set(True)
        smask = jnp.repeat(gmask, gs, axis=1)
        masked = jnp.where(smask, sfc, 0.0)
        _, topk_idx = jax.lax.top_k(masked, TOP_K)
        tw = jnp.take_along_axis(scores, topk_idx, axis=1)
        tw = tw / (tw.sum(-1, keepdims=True) + 1e-20)
        tw = (tw * SCALE).astype(xf.dtype)
        combine = jnp.zeros((T, E), xf.dtype).at[jnp.arange(T)[:, None], topk_idx].add(tw)

        def expert_step(acc, inp):
            gu, dn, c = inp
            g = xf @ gu[:I].T
            u = xf @ gu[I:].T
            o = jax.nn.silu(g) * u @ dn.T
            return (acc + c[:, None] * o, None)
        routed, _ = jax.lax.scan(expert_step, jnp.zeros_like(xf), (experts_gate_up, experts_down, combine.T))
        sh = jax.nn.silu(xf @ shared_gate_w.T) * (xf @ shared_up_w.T)
        shared_out = sh @ shared_down_w.T
        return (routed + shared_out).reshape(b, s, h)
    x = x + _L0_xattn_ref(_layernorm(x, axis=-1), ctx_1024, L0_xattn_Wq, L0_xattn_Wkv, L0_xattn_Wo, L0_xattn_rel_bias)
    x = x + _L0_ffn_ref(_layernorm(x, axis=-1), L0_ffn_gate_weight, L0_ffn_e_score_correction_bias, L0_ffn_experts_gate_up, L0_ffn_experts_down, L0_ffn_shared_gate_w, L0_ffn_shared_up_w, L0_ffn_shared_down_w)
    return x

_drawn_inputs = setup_inputs


def setup_inputs(seed=0):
    import zlib

    import numpy as np

    out = dict(_drawn_inputs(seed))
    spreads = {}
    factors = {'L0_xattn_Wq': 7.24,
     'L0_xattn_rel_bias': 8.0,
     'L0_ffn_gate_weight': 5.124,
     'L0_ffn_e_score_correction_bias': 8.0,
     'L0_ffn_experts_gate_up': 4.622,
     'L0_ffn_experts_down': 4.615,
     'L0_ffn_shared_gate_w': 3.384,
     'L0_ffn_shared_up_w': 3.348,
     'L0_ffn_shared_down_w': 3.352}
    for name, (base, spread) in spreads.items():
        noise = np.random.default_rng([zlib.crc32(name.encode()), seed]).standard_normal(out[name].shape)
        drawn = base * np.exp(spread * noise) if base else spread * noise
        out[name] = jnp.asarray(drawn.astype(out[name].dtype))
    for name, factor in factors.items():
        out[name] = (out[name] * factor).astype(out[name].dtype)
    return out
```

```python
import numpy as np
import concourse.bass as bass
import concourse.mybir as mybir
from contextlib import ExitStack

F32 = mybir.dt.float32
BF16 = mybir.dt.bfloat16
I32 = mybir.dt.int32
U32 = mybir.dt.uint32
ALU = mybir.AluOpType
ACT = mybir.ActivationFunctionType
X = mybir.AxisListType.X

P = 128
B, S, E = 8, 512, 256
H, D = 16, 16
TB = S // P
EC = E // P
NT = B * TB
EPS = 1e-5

BUCKETS = 32
BUCKET_STARTS = [0, 1, 2, 3, 4, 5, 6, 7, 8, 12, 16, 23, 32, 46, 64, 91]
FAR = BUCKET_STARTS[-1]
NEAR_LO = -(FAR - 1)
NEAR_W = P + 2 * (FAR - 1)
DIAG = NEAR_W + P - 1

TERMS = [(0, 0), (0, 1), (1, 0), (1, 1), (0, 2), (2, 0)]
KQ = len(TERMS) * D
ROW_MAX = KQ
ROW_FAR = KQ + 3
KS = ROW_FAR + 3 * TB
VW = 32
CH = 2 * TB * 4
NS = H * TB

NE, TOPK, NG, TOPG, SCALE = 32, 6, 8, 4, 2.5
GS = NE // NG
FI, SI = 128, 256
REG = B * S + P
PADS = NE * REG
ROWW = E + 4
TILES = 224
NY = TOPK * B * S
SENT = -1e30


class Count:

    def __init__(self, sem, per=1, ahead=2):
        self.sem, self.per, self.ahead = sem, per, ahead

    def value(self, n, part=None):
        return (n + self.ahead) * self.per + (self.per if part is None else part)


def stand_alone(eng, passed):
    eng.sem_inc(passed, 1)


def build(nc, a, out):
    ctx = ExitStack()
    counts = []

    def sem(name):
        return ctx.enter_context(nc.semaphore(name))

    def count(name, per=1, ahead=2):
        c = Count(sem(name), per, ahead)
        counts.append(c)
        return c

    def dram(name, shape, dt):
        return nc.dram_tensor(name, shape, dt, kind="Internal").ap()

    with ctx:
        sc = dict(
            parts=dram("parts", [B, 2, E, 3, S], BF16),
            v=dram("v", [B, P, TB, H, VW], F32),
            diag=dram("diag", [H, P, DIAG + P], F32),
            krows=dram("krows", [KS - ROW_MAX, S], BF16),
            far=dram("far", [3, TB, H, S], BF16),
            negmax=dram("negmax", [B, 3, NS, P], BF16),
            x1=dram("x1", [B, P, TB, E], F32),
            base=dram("base", [B, P, TB, E], F32),
            slots=dram("slots", [PADS + P, ROWW], F32),
            tiletab=dram("tiletab", [2, P, 2], I32),
            y=dram("y", [NY, E], F32),
        )
        passed = sem("passed")
        c1, c2 = project_counts(count, sem), attend_counts(count, sem)
        c3, c4, c5 = route_counts(count, sem), expert_counts(count, sem), combine_counts(count, sem)
        with ExitStack() as held:
            ident = held.enter_context(nc.sbuf_tensor("ident", [P, P], F32))
            identb = held.enter_context(nc.sbuf_tensor("identb", [P, P], BF16))
            with nc.sbuf_tensor("near", [P, H, NEAR_W], F32) as near:
                prepare(nc, a, sc, counts, sem, passed, ident, identb, near)
                project(nc, a, sc, c1, passed, ident)
                attend(nc, a, sc, c2, passed, ident, identb, near)
            with nc.sbuf_tensor("tiles", [1, 2, 2 * P], I32) as tiles:
                route(nc, a, sc, c3, passed, ident, tiles)
                experts(nc, a, sc, c4, passed, ident, tiles)
            combine(nc, a, sc, c5, out)


def prepare(nc, a, sc, counts, sem, passed, ident, identb, near):
    loaded, dve, pe, act, far_out, far_in = (sem("prep_" + n) for n in ("loaded", "dve", "pe", "act", "out", "in"))
    with (
        nc.sbuf_tensor("rel", [H, BUCKETS], F32) as rel,
        nc.sbuf_tensor("relmax", [H, 1], F32) as relmax,
        nc.sbuf_tensor("relT", [BUCKETS, H], F32) as relT,
        nc.sbuf_tensor("oh_diag", [BUCKETS, DIAG], F32) as oh_diag,
        nc.sbuf_tensor("oh_far", [BUCKETS, TB * S], F32) as oh_far,
        nc.sbuf_tensor("ediag", [H, DIAG], F32) as ediag,
        nc.sbuf_tensor("krows32", [KS - ROW_MAX, S], F32) as krows32,
        nc.sbuf_tensor("krows16", [KS - ROW_MAX, S], BF16) as krows16,
        nc.sbuf_tensor("fparts", [H, 3, TB * S], BF16) as fparts,
        nc.sbuf_tensor("frest", [H, 2, TB * S], F32) as frest,
        nc.psum_tensor("pt", [BUCKETS, H], F32) as pt,
        nc.psum_tensor("pd", [H, 512], F32) as pd,
        nc.psum_tensor("pf", [H, TB * S], F32) as pf,
        nc.Block() as block,
    ):
        @block.sync
        def _(sp):
            for c in counts:
                if c.ahead:
                    sp.sem_inc(c.sem, c.ahead * c.per)
            sp.dma_start(ident[:, :], a["eye"]).then_inc(loaded, 16)
            sp.dma_start(rel[:, :], a["rel_bias"]).then_inc(loaded, 16)
            sp.dma_start(oh_diag[:, :], a["onehot_diag"]).then_inc(loaded, 16)
            sp.dma_start(oh_far[:, :], a["onehot_far"]).then_inc(loaded, 16)
            sp.dma_start(krows32[:, :], a["krows"]).then_inc(loaded, 16)
            sp.wait_ge(act, 1)
            skewed = bass.AP(tensor=sc["diag"].tensor, offset=0, ap=[[P * (DIAG + P), H], [DIAG + P + 1, P], [1, DIAG]])
            sp.dma_start(skewed, ediag[:, :].rearrange("h (o i) -> h o i", o=1).to_broadcast([H, P, DIAG])).then_inc(far_out, 16)
            sp.wait_ge(dve, 10)
            for p in range(3):
                sp.dma_start(sc["far"][p].rearrange("k h s -> h k s"),
                             fparts[:, p, :].rearrange("h (k s) -> h k s", k=TB)).then_inc(far_out, 16)
            sp.dma_start(sc["krows"], krows16[:, :]).then_inc(far_out, 16)
            sp.wait_ge(far_out, 80)
            sp.dma_start(near[:, :, :], sc["diag"][:, :, P - 1:P - 1 + NEAR_W].rearrange("h k j -> k h j")).then_inc(far_in, 16)
            sp.wait_ge(far_in, 16)

        @block.vector
        def _(v):
            v.wait_ge(loaded, 80)
            v.tensor_copy(identb[:, :], ident[:, :]).then_inc(dve, 1)
            v.reduce_max(relmax[:, :], rel[:, :], X).then_inc(dve, 1)
            v.wait_ge(dve, 2)
            v.tensor_scalar(frest[:, 0, 0:BUCKETS], rel[:, :], relmax[:, 0:1], None, ALU.subtract).then_inc(dve, 1)
            v.wait_ge(pe, 1)
            v.tensor_copy(relT[:, :], pt[:, :]).then_inc(dve, 1)
            v.wait_ge(pe, 2)
            v.tensor_copy(fparts[:, 0, :], pf[:, :]).then_inc(dve, 1)
            v.wait_ge(dve, 5)
            v.tensor_sub(frest[:, 0, :], pf[:, :], fparts[:, 0, :]).then_inc(dve, 1)
            v.wait_ge(dve, 6)
            v.tensor_copy(fparts[:, 1, :], frest[:, 0, :]).then_inc(dve, 1)
            v.wait_ge(dve, 7)
            v.tensor_sub(frest[:, 1, :], frest[:, 0, :], fparts[:, 1, :]).then_inc(dve, 1)
            v.wait_ge(dve, 8)
            v.tensor_copy(fparts[:, 2, :], frest[:, 1, :]).then_inc(dve, 1)
            v.tensor_copy(krows16[:, :], krows32[:, :]).then_inc(dve, 1)

        @block.scalar
        def _(s):
            s.wait_ge(pe, 2)
            s.activation(ediag[:, :], pd[:, 0:DIAG], ACT.Exp).then_inc(act, 1)

        @block.tensor
        def _(t):
            t.wait_ge(dve, 3)
            t.transpose(pt[:, :], frest[:, 0, 0:BUCKETS], ident[0:H, 0:H]).then_inc(pe, 1)
            t.wait_ge(dve, 4)
            t.matmul(pd[:, 0:DIAG], relT[:, :], oh_diag[:, :], start=True, stop=True)
            for k in range(TB):
                last = t.matmul(pf[:, k * S:(k + 1) * S], relT[:, :], oh_far[:, k * S:(k + 1) * S], start=True, stop=True)
            last.then_inc(pe, 1)


def project_counts(count, sem):
    return dict(
        weights=sem("pr_weights"), ones=sem("pr_ones"),
        x_in=[count(f"pr_x_in{u}", 16) for u in range(2)], c_in=[count(f"pr_c_in{u}", 16) for u in range(2)],
        parts_out=[count(f"pr_parts_out{u}", 16) for u in range(2)], v_out=[count(f"pr_v_out{u}", 16) for u in range(2)],
        stats=count("pr_stats", 8), rstd=count("pr_rstd", 2), xn=count("pr_xn", TB),
        tp=count("pr_tp", 2), xnT=count("pr_xnT", 2), mm=count("pr_mm", 4), part1=count("pr_part1", 4),
        rest=count("pr_rest", 4), part2=count("pr_part2", 4), part3=count("pr_part3", 4),
        vmm=count("pr_vmm", 2), v=count("pr_v", 2),
    )


def project(nc, a, sc, c, passed, ident):
    def pair(name, shape, dt=F32):
        return [es.enter_context(nc.sbuf_tensor(f"pr_{name}{u}", shape, dt)) for u in range(2)]

    with ExitStack() as es:
        wq = es.enter_context(nc.sbuf_tensor("wq", [P, EC, E], F32))
        wkv = es.enter_context(nc.sbuf_tensor("wkv", [P, EC, 2 * E], F32))
        half = es.enter_context(nc.sbuf_tensor("half", [P, TB], F32))
        x, xn, xnT, cT = pair("x", [P, TB, E]), pair("xn", [P, TB, E]), pair("xnT", [P, EC, S]), pair("cT", [P, EC, S])
        st, mv, var, rstd = pair("st", [P, TB, 6]), pair("mv", [P, TB, 2]), pair("var", [P, TB]), pair("rstd", [P, TB])
        parts, vt, rest = pair("parts", [P, 4, 3, S], BF16), pair("vt", [P, TB, H, VW]), pair("rest", [P, S])
        tp = [es.enter_context(nc.psum_tensor(f"pr_tp{i}", [P, S], F32)) for i in range(EC)]
        qk = [es.enter_context(nc.psum_tensor(f"pr_qk{i}", [P, S], F32)) for i in range(4)]
        vp = [es.enter_context(nc.psum_tensor(f"pr_vp{i}", [P, 2, E], F32)) for i in range(2)]
        block = es.enter_context(nc.Block())
        x_rows = a["x"].rearrange("(b t p) e -> b p t e", b=B, t=TB)
        cT_cols = a["ctxT"].rearrange("(c p) (b s) -> b p c s", p=P, b=B)
        parts_d = sc["parts"].rearrange("b k (m p) t s -> b p (k m) (t s)", p=P)

        @block.sync
        def _(sp):
            sp.dma_start(wq[:, :, :], a["wq"].rearrange("(c p) e -> p c e", p=P)).then_inc(c["weights"], 16)
            sp.dma_start(wkv[:, :, :], a["wkv"].rearrange("(c p) e -> p c e", p=P)).then_inc(c["weights"], 16)

            def load(n, u, it):
                sp.dma_start(x[u][:, :, :], x_rows[n]).then_inc(c["x_in"][u].sem, 16)
                sp.dma_start(cT[u][:, :, :], cT_cols[n]).then_inc(c["c_in"][u].sem, 16)

            def body(n, u, first, last, it):
                if first:
                    load(n, u, it)
                sp.wait_ge(c["part3"].sem, c["part3"].value(n))
                sp.dma_start(parts_d[bass.ds(n, 1)].rearrange("o p w s -> (o p) w s"),
                             parts[u][:, :, :, :].rearrange("p w t s -> p w (t s)")).then_inc(c["parts_out"][u].sem, 16)
                sp.wait_ge(c["v"].sem, c["v"].value(n))
                sp.dma_start(sc["v"][bass.ds(n, 1)].rearrange("o p k h w -> (o p) (k h w)"),
                             vt[u][:, :, :, :].rearrange("p k h w -> p (k h w)")).then_inc(c["v_out"][u].sem, 16)

            load(0, 0, 0)
            load(1, 1, 0)

            def step(n, u, it, last):
                body(n, u, False, last, it)
                if not last:
                    sp.wait_ge(c["xn"].sem, c["xn"].value(n))
                    sp.dma_start(x[u][:, :, :], x_rows[bass.ds(n + 2, 1)].rearrange("o p t e -> (o p) t e")).then_inc(c["x_in"][u].sem, 16)
                    sp.dma_start(cT[u][:, :, :], cT_cols[bass.ds(n + 2, 1)].rearrange("o p c s -> (o p) c s")).then_inc(c["c_in"][u].sem, 16)

            with sp.Fori(0, B // 2 - 1) as it:
                for u in range(2):
                    step(it * 2 + u, u, it, False)
            for u in range(2):
                step(B - 2 + u, u, B // 2 - 1, True)
            for u in range(2):
                sp.wait_ge(c["parts_out"][u].sem, c["parts_out"][u].value(B // 2 - 1))
                sp.wait_ge(c["v_out"][u].sem, c["v_out"][u].value(B // 2 - 1))

        @block.gpsimd
        def _(g):
            for u in range(2):
                g.memset(vt[u][:, :, :, :], 0.0).then_inc(c["ones"], 1)
            g.memset(half[:, :], -0.5).then_inc(c["ones"], 1)
            g.wait_ge(c["ones"], 3)
            for u in range(2):
                g.memset(vt[u][:, :, :, D:D + 1], 1.0).then_inc(c["ones"], 1)

            def body(n, u):
                g.wait_ge(c["stats"].sem, c["stats"].value(n))
                stand_alone(g, passed)
                g.tensor_scalar(var[u][:, :], mv[u][:, :, 1], EPS, None, ALU.add).then_inc(c["rstd"].sem, 1)
                g.wait_ge(c["rstd"].sem, c["rstd"].value(n, 1))
                g.tensor_tensor(rstd[u][:, :], var[u][:, :], half[:, :], ALU.pow).then_inc(c["rstd"].sem, 1)

            with g.Fori(0, B // 2) as it:
                for u in range(2):
                    body(it * 2 + u, u)

        @block.vector
        def _(v):
            def stats(n, u, it):
                v.wait_ge(c["x_in"][u].sem, c["x_in"][u].value(it))
                v.wait_ge(c["rstd"].sem, c["rstd"].value(n - 2))
                v.wait_ge(c["xn"].sem, c["xn"].value(n - 2))
                for t in range(TB):
                    v.bn_stats(st[u][:, t, :], x[u][:, t, :]).then_inc(c["stats"].sem, 1)
                v.wait_ge(c["stats"].sem, c["stats"].value(n, TB))
                stand_alone(v, passed)
                for t in range(TB):
                    v.bn_aggr(mv[u][:, t, :], st[u][:, t, :]).then_inc(c["stats"].sem, 1)

            def normalise(n, u):
                v.wait_ge(c["rstd"].sem, c["rstd"].value(n))
                v.wait_ge(c["tp"].sem, c["tp"].value(n - 2))
                for t in range(TB):
                    v.tensor_scalar(xn[u][:, t, :], x[u][:, t, :], mv[u][:, t, 0:1], rstd[u][:, t:t + 1],
                                    ALU.subtract, ALU.mult).then_inc(c["xn"].sem, 1)

            def split(n, u, it):
                v.wait_ge(c["parts_out"][u].sem, c["parts_out"][u].value(it - 1))
                for w in range(4 + 1):
                    if w < 4:
                        v.wait_ge(c["part1"].sem, c["part1"].value(n, w + 1))
                        v.wait_ge(c["part3"].sem, c["part3"].value(n, w - 1))
                        v.tensor_sub(rest[w % 2][:, :], qk[w][:, :], parts[u][:, w, 0, :]).then_inc(c["rest"].sem, 1)
                    if w >= 1:
                        v.wait_ge(c["part2"].sem, c["part2"].value(n, w))
                        v.tensor_sub(parts[u][:, w - 1, 2, :], rest[(w - 1) % 2][:, :], parts[u][:, w - 1, 1, :]).then_inc(c["part3"].sem, 1)

            v.wait_ge(c["ones"], 5)
            stats(0, 0, 0)
            normalise(0, 0)

            def body(n, u, it, last):
                if not last:
                    stats(n + 1, 1 - u, it + u)
                split(n, u, it)
                if not last:
                    normalise(n + 1, 1 - u)

            with v.Fori(0, B // 2 - 1) as it:
                for u in range(2):
                    body(it * 2 + u, u, it, False)
            body(B - 2, 0, B // 2 - 1, False)
            body(B - 1, 1, B // 2 - 1, True)

        @block.scalar
        def _(s):
            def xnT_out(n, u):
                for i in range(EC):
                    s.wait_ge(c["tp"].sem, c["tp"].value(n, i + 1))
                    s.wait_ge(c["mm"].sem, c["mm"].value(n - 2, 2))
                    s.copy(xnT[u][:, i, :], tp[i][:, :]).then_inc(c["xnT"].sem, 1)

            def body(n, u, it, last):
                s.wait_ge(c["parts_out"][u].sem, c["parts_out"][u].value(it - 1))
                for w in range(4 + 1):
                    if w < 4:
                        s.wait_ge(c["mm"].sem, c["mm"].value(n, w + 1))
                        s.copy(parts[u][:, w, 0, :], qk[w][:, :]).then_inc(c["part1"].sem, 1)
                    if w >= 1:
                        s.wait_ge(c["rest"].sem, c["rest"].value(n, w))
                        s.copy(parts[u][:, w - 1, 1, :], rest[(w - 1) % 2][:, :]).then_inc(c["part2"].sem, 1)
                if not last:
                    xnT_out(n + 1, 1 - u)
                s.wait_ge(c["v_out"][u].sem, c["v_out"][u].value(it - 1))
                for i in range(2):
                    s.wait_ge(c["vmm"].sem, c["vmm"].value(n, i + 1))
                    s.copy(vt[u][:, 2 * i:2 * i + 2, :, 0:D],
                           vp[i][:, :, :].rearrange("p k (h d) -> p k h d", h=H)).then_inc(c["v"].sem, 1)

            s.wait_ge(c["ones"], 5)
            xnT_out(0, 0)
            with s.Fori(0, B // 2 - 1) as it:
                for u in range(2):
                    body(it * 2 + u, u, it, False)
            body(B - 2, 0, B // 2 - 1, False)
            body(B - 1, 1, B // 2 - 1, True)

        @block.tensor
        def _(t_):
            def transposes(n, u):
                for i in range(EC):
                    t_.wait_ge(c["xn"].sem, c["xn"].value(n))
                    t_.wait_ge(c["xnT"].sem, c["xnT"].value(n - 1, i + 1))
                    for t in range(TB):
                        last = t_.transpose(tp[i][:, t * P:(t + 1) * P], xn[u][:, t, i * P:(i + 1) * P], ident[:, :])
                    last.then_inc(c["tp"].sem, 1)

            def body(n, u, it, last):
                for w in range(4):
                    m = w % 2
                    if w == 0:
                        t_.wait_ge(c["xnT"].sem, c["xnT"].value(n))
                    if w == 2:
                        t_.wait_ge(c["c_in"][u].sem, c["c_in"][u].value(it))
                    t_.wait_ge(c["rest"].sem, c["rest"].value(n - 1, w + 1))
                    for i in range(EC):
                        lhsT = wq[:, i, m * P:(m + 1) * P] if w < 2 else wkv[:, i, m * P:(m + 1) * P]
                        rhs = xnT[u][:, i, :] if w < 2 else cT[u][:, i, :]
                        mm = t_.matmul(qk[w][:, :], lhsT, rhs, start=(i == 0), stop=(i == EC - 1))
                    mm.then_inc(c["mm"].sem, 1)
                if not last:
                    transposes(n + 1, 1 - u)
                for k2 in range(2):
                    t_.wait_ge(c["v"].sem, c["v"].value(n - 1, k2 + 1))
                    for k in range(2):
                        kb = 2 * k2 + k
                        for i in range(EC):
                            mm = t_.matmul(vp[k2][:, k, :], cT[u][:, i, kb * P:(kb + 1) * P], wkv[:, i, E:2 * E],
                                           start=(i == 0), stop=(i == EC - 1))
                    mm.then_inc(c["vmm"].sem, 1)

            t_.wait_ge(c["weights"], 32)
            transposes(0, 0)
            with t_.Fori(0, B // 2 - 1) as it:
                for u in range(2):
                    body(it * 2 + u, u, it, False)
            body(B - 2, 0, B // 2 - 1, False)
            body(B - 1, 1, B // 2 - 1, True)


def attend_counts(count, sem):
    return dict(
        once=sem("at_once"), rows=sem("at_rows"), v0=[sem(f"at_v0{g}") for g in range(4)],
        stack=count("at_stack", 16 * 2 * len(TERMS)), res=count("at_res", 16),
        nm_out=count("at_nm_out", 16), nm_in=count("at_nm_in", 16), x1_out=count("at_x1_out", 16),
        v_in=[count(f"at_v_in{g}", 16) for g in range(4)],
        s=count("at_s", NS), mx=count("at_mx", NS), nm=count("at_nm", 5), nmp=count("at_nmp"), nmT=count("at_nmT"),
        st=count("at_st", CH), ex=count("at_ex", CH), mul=count("at_mul", CH), pv=count("at_pv", CH // 2),
        o=count("at_o", 4), op=count("at_op", 4), rc=count("at_rc", 4), on=count("at_on", 4),
        onp=count("at_onp", EC), onT=count("at_onT", EC), wo=count("at_wo", 2), x1=count("at_x1", 2),
    )


S_FROM, S_TO = 5, 30
S_AT = [(max(0, min(NS, (k - S_FROM + 1) * NS // (S_TO - S_FROM))) - max(0, min(NS, (k - S_FROM) * NS // (S_TO - S_FROM))))
        for k in range(CH)]
S_BEFORE = [sum(S_AT[:k]) for k in range(CH)]
AT_O_LAST, AT_ON0, AT_ON1, AT_WO0, AT_WO1 = 4, 6, 8, 10, 11
AT_O = [12, 20, 28]


def near_range(kb):
    lo, hi = kb * P + NEAR_LO, kb * P + NEAR_LO + NEAR_W
    return max(lo, 0), min(hi, S), max(lo, 0) - lo


def attend(nc, a, sc, c, passed, ident, identb, near):
    with ExitStack() as es:
        def sb(name, shape, dt=F32):
            return es.enter_context(nc.sbuf_tensor("at_" + name, shape, dt))

        def ps(name, shape, dt=F32):
            return es.enter_context(nc.psum_tensor("at_" + name, shape, dt))

        qs, ks = sb("qs", [P, 2, H, S], BF16), sb("ks", [P, 2, H, S], BF16)
        wo = sb("wo", [P, EC, E])
        vt = sb("vt", [P, TB, H, VW])
        pr = [sb(f"pr{i}", [P, 2, S]) for i in range(4)]
        o_sb = [sb(f"o{i}", [P, S]) for i in range(2)]
        rc = sb("rc", [P, TB, 4])
        on = sb("on", [P, TB, E])
        onT = sb("onT", [P, EC, S])
        res, x1 = sb("res", [P, TB, E]), sb("x1", [P, TB, E])
        nm, nmr, nmb, nmT = sb("nm", [P, NS]), sb("nmr", [P, 2, NS]), sb("nmb", [P, 3, NS], BF16), sb("nmT", [NS, 3, P], BF16)
        sp_ = [ps(f"s{i}", [P, S]) for i in range(2)]
        st_ = [ps(f"st{i}", [P, 2, S]) for i in range(2)]
        op = ps("o", [P, S])
        mp = ps("m", [P, TB, P])
        mpb = mp[:, :, :].rearrange("p a b -> p (a b)").bitcast(BF16)
        block = es.enter_context(nc.Block())
        x_rows = a["x"].rearrange("(b t p) e -> b p t e", b=B, t=TB)

        def par(n):
            return n % 2

        def put(n):
            return bass.ds(par(n), 1)

        @block.sync
        def _(sp):
            sp.dma_start(wo[:, :, :], a["wo"].rearrange("(c p) e -> p c e", p=P)).then_inc(c["once"], 16)
            for u in range(2):
                sp.dma_start(ks[ROW_MAX:KS, u, :, :], sc["krows"].rearrange("r (o s) -> r o s", o=1).to_broadcast([KS - ROW_MAX, H, S])).then_inc(c["rows"], 16)
                sp.dma_start(qs[ROW_FAR:KS, u, :, :], sc["far"].rearrange("p k h s -> (p k) h s")).then_inc(c["rows"], 16)

            def stacks(n):
                for i, (qi, ki) in enumerate(TERMS):
                    for k, dst, part in ((0, qs, qi), (1, ks, ki)):
                        src = sc["parts"][bass.ds(n, 1), k, :, part, :].rearrange("o (h d) s -> (o d) h s", d=D)
                        sp.dma_start(dst[i * D:(i + 1) * D, put(n), :, :].rearrange("p o h s -> p (o h) s"), src).then_inc(c["stack"].sem, 16)

            def maxima(n):
                sp.wait_ge(c["nmT"].sem, c["nmT"].value(n))
                sp.dma_start(sc["negmax"][bass.ds(n, 1)].rearrange("o t c q -> (o c) t q"), nmT[:, :, :]).then_inc(c["nm_out"].sem, 16)
                sp.wait_ge(c["nm_out"].sem, c["nm_out"].value(n))
                sp.dma_start(qs[ROW_MAX:ROW_FAR, put(n), :, :].rearrange("t o h s -> t (o h s)"),
                             sc["negmax"][bass.ds(n, 1)].rearrange("o t c q -> (o t) (c q)")).then_inc(c["nm_in"].sem, 16)

            def v_group(n, g):
                sp.dma_start(vt[:, :, 4 * g:4 * g + 4, :].rearrange("p k h w -> p k (h w)"),
                             sc["v"][bass.ds(n, 1), :, :, 4 * g:4 * g + 4, :].rearrange("o p k h w -> (o p) k (h w)")).then_inc(c["v_in"][g].sem, 16)

            def store(n):
                sp.wait_ge(c["x1"].sem, c["x1"].value(n))
                sp.dma_start(sc["x1"][bass.ds(n, 1)].rearrange("o p t e -> (o p) t e"), x1[:, :, :]).then_inc(c["x1_out"].sem, 16)

            def residual(n):
                sp.wait_ge(c["x1"].sem, c["x1"].value(n - 1))
                sp.dma_start(res[:, :, :], x_rows[bass.ds(n, 1)].rearrange("o p t e -> (o p) t e")).then_inc(c["res"].sem, 16)

            def batch(n, first, last):
                if not last:
                    sp.wait_ge(c["st"].sem, c["st"].value(n - 1))
                    stacks(n + 1)
                if not first:
                    store(n - 1)
                residual(n)
                if not last:
                    for g in range(4):
                        sp.wait_ge(c["pv"].sem, c["pv"].value(n, 4 * g + 4))
                        v_group(n + 1, g)
                        if g == 3:
                            break
                        if g == 2:
                            maxima(n + 1)

            stacks(0)
            for g in range(4):
                v_group(0, g)
            maxima(0)
            batch(0, True, False)
            with sp.Fori(1, B - 1) as n:
                batch(n, False, False)
            batch(B - 1, False, True)
            store(B - 1)
            sp.wait_ge(c["x1_out"].sem, c["x1_out"].value(B - 1))

        def score_units(n, unit, k):
            for j in range(S_BEFORE[k], S_BEFORE[k] + S_AT[k]):
                unit(n, j)

        @block.vector
        def _(v):
            def row_max(n, j):
                v.wait_ge(c["s"].sem, c["s"].value(n, j + 1))
                if j == 0:
                    v.wait_ge(c["nm"].sem, c["nm"].value(n - 1))
                v.reduce_max(nm[:, j:j + 1], sp_[j % 2][:, :], X, negate=True).then_inc(c["mx"].sem, 1)

            def split_max(n):
                k = c["nm"]
                v.wait_ge(c["mx"].sem, c["mx"].value(n))
                v.wait_ge(c["nmp"].sem, c["nmp"].value(n - 1))
                v.tensor_copy(nmb[:, 0, :], nm[:, :]).then_inc(k.sem, 1)
                v.wait_ge(k.sem, k.value(n, 1))
                v.tensor_sub(nmr[:, 0, :], nm[:, :], nmb[:, 0, :]).then_inc(k.sem, 1)
                v.wait_ge(k.sem, k.value(n, 2))
                v.tensor_copy(nmb[:, 1, :], nmr[:, 0, :]).then_inc(k.sem, 1)
                v.wait_ge(k.sem, k.value(n, 3))
                v.tensor_sub(nmr[:, 1, :], nmr[:, 0, :], nmb[:, 1, :]).then_inc(k.sem, 1)
                v.wait_ge(k.sem, k.value(n, 4))
                v.tensor_copy(nmb[:, 2, :], nmr[:, 1, :]).then_inc(k.sem, 1)

            def normalise(n, g):
                v.wait_ge(c["op"].sem, c["op"].value(n, g + 1))
                heads = mp[:, :, :].rearrange("p t (h w) -> p t h w", w=VW)
                v.wait_ge(c["on"].sem, c["on"].value(n, g))
                v.reciprocal(rc[:, :, :], heads[:, :, :, D]).then_inc(c["rc"].sem, 1)
                v.wait_ge(c["rc"].sem, c["rc"].value(n, g + 1))
                v.wait_ge(c["onp"].sem, c["onp"].value(n - 1))
                v.tensor_tensor(on[:, :, 4 * g * D:4 * (g + 1) * D].rearrange("p t (h d) -> p t h d", d=D), heads[:, :, :, 0:D],
                                rc[:, :, :].rearrange("p t (h o) -> p t h o", o=1).to_broadcast([P, TB, 4, D]), ALU.mult).then_inc(c["on"].sem, 1)

            def add_residual(n, i):
                v.wait_ge(c["wo"].sem, c["wo"].value(n, i + 1))
                if i == 0:
                    v.wait_ge(c["res"].sem, c["res"].value(n))
                    v.wait_ge(c["x1_out"].sem, c["x1_out"].value(n - 1))
                v.tensor_add(x1[:, 2 * i:2 * i + 2, :], mp[:, :, :].rearrange("p a b -> p (a b)").rearrange("p (t e) -> p t e", e=E),
                             res[:, 2 * i:2 * i + 2, :]).then_inc(c["x1"].sem, 1)

            def batch(n, first, last):
                for k in range(CH):
                    if not last:
                        score_units(n + 1, row_max, k)
                    if not first and k == AT_O_LAST:
                        normalise(n - 1, 3)
                    if not first and k in (AT_WO0, AT_WO1):
                        add_residual(n - 1, (AT_WO0, AT_WO1).index(k))
                    if k in AT_O:
                        normalise(n, AT_O.index(k))
                if not last:
                    split_max(n + 1)

            for j in range(NS):
                row_max(0, j)
            split_max(0)
            batch(0, True, False)
            with v.Fori(1, B - 1) as n:
                batch(n, False, False)
            batch(B - 1, False, True)
            normalise(B - 1, 3)
            for i in range(2):
                add_residual(B - 1, i)

        @block.scalar
        def _(s):
            def exp(n, k):
                s.wait_ge(c["st"].sem, c["st"].value(n, k + 1))
                s.wait_ge(c["pv"].sem, c["pv"].value(n, (k - 4) // 2 + 1))
                s.activation(pr[k % 4][:, :, :], st_[k % 2][:, :, :], ACT.Exp).then_inc(c["ex"].sem, 1)

            def o_out(n, g):
                s.wait_ge(c["pv"].sem, c["pv"].value(n, 4 * g + 4))
                s.wait_ge(c["op"].sem, c["op"].value(n, g - 1))
                s.copy(o_sb[g % 2][:, :], op[:, :]).then_inc(c["o"].sem, 1)

            def onT_out(n, i):
                s.wait_ge(c["onp"].sem, c["onp"].value(n, i + 1))
                s.wait_ge(c["wo"].sem, c["wo"].value(n - 1))
                s.copy(onT[:, i, :], mp[:, :, :].rearrange("p a b -> p (a b)")).then_inc(c["onT"].sem, 1)

            def nmT_out(n):
                s.wait_ge(c["nmp"].sem, c["nmp"].value(n))
                s.wait_ge(c["nm_out"].sem, c["nm_out"].value(n - 1))
                s.copy(nmT[:, :, :].rearrange("c t q -> c (t q)"), mpb[0:NS, 0:3 * P]).then_inc(c["nmT"].sem, 1)

            def batch(n, first, last):
                for k in range(CH):
                    if not first and k == 2:
                        o_out(n - 1, 3)
                    if not first and k in (AT_ON0 + 1, AT_ON1 + 1):
                        onT_out(n - 1, (AT_ON0 + 1, AT_ON1 + 1).index(k))
                    if k in (10, 18, 26):
                        o_out(n, (10, 18, 26).index(k))
                    exp(n, k)
                if not last:
                    nmT_out(n + 1)

            nmT_out(0)
            batch(0, True, False)
            with s.Fori(1, B - 1) as n:
                batch(n, False, False)
            batch(B - 1, False, True)
            o_out(B - 1, 3)
            for i in range(EC):
                onT_out(B - 1, i)

        @block.gpsimd
        def _(g_):
            def batch(n):
                for k in range(CH):
                    g, kb, two = k // 8, k // 2 % TB, k % 2
                    lo, hi, at = near_range(kb)
                    h = 4 * g + 2 * two
                    g_.wait_ge(c["ex"].sem, c["ex"].value(n, k + 1))
                    g_.tensor_tensor(pr[k % 4][:, :, lo:hi], pr[k % 4][:, :, lo:hi], near[:, h:h + 2, at:at + hi - lo],
                                     ALU.mult).then_inc(c["mul"].sem, 1)

            with g_.Fori(0, B) as n:
                batch(n)

        @block.tensor
        def _(t):
            def scores(n, j):
                h, qb = j // TB, j % TB
                t.wait_ge(c["mx"].sem, c["mx"].value(n, j - 1))
                if j == 0:
                    t.wait_ge(c["stack"].sem, c["stack"].value(n))
                t.matmul(sp_[j % 2][:, :], qs[0:KQ, put(n), h, qb * P:(qb + 1) * P].rearrange("p o q -> p (o q)"),
                         ks[0:KQ, put(n), h, :].rearrange("p o q -> p (o q)"), start=True, stop=True).then_inc(c["s"].sem, 1)

            def chunk(n, k):
                g, kb, two = k // 8, k // 2 % TB, k % 2
                t.wait_ge(c["ex"].sem, c["ex"].value(n, k - 1))
                if k == 0:
                    t.wait_ge(c["nm_in"].sem, c["nm_in"].value(n))
                for j in range(2):
                    h = 4 * g + 2 * two + j
                    last = t.matmul(st_[k % 2][:, j, :], ks[0:KS, put(n), h, kb * P:(kb + 1) * P].rearrange("p o q -> p (o q)"),
                                    qs[0:KS, put(n), h, :].rearrange("p o q -> p (o q)"), start=True, stop=True)
                last.then_inc(c["st"].sem, 1)

            def values(n, i):
                g, kb = i // TB, i % TB
                t.wait_ge(c["mul"].sem, c["mul"].value(n, 2 * i + 2))
                if kb == 0:
                    t.wait_ge(c["v_in"][g].sem, c["v_in"][g].value(n))
                    t.wait_ge(c["o"].sem, c["o"].value(n, g))
                for hh in range(4):
                    k = 2 * i + hh // 2
                    last = t.matmul(op[32 * hh:32 * hh + VW, :], vt[:, kb, 4 * g + hh, :], pr[k % 4][:, hh % 2, :],
                                    start=(kb == 0), stop=(kb == TB - 1))
                last.then_inc(c["pv"].sem, 1)

            def o_back(n, g, misc_free):
                t.wait_ge(c["o"].sem, c["o"].value(n, g + 1))
                misc_free()
                for q in range(TB):
                    last = t.transpose(mp[:, q, :], o_sb[g % 2][:, q * P:(q + 1) * P], ident[:, :])
                last.then_inc(c["op"].sem, 1)

            def on_back(n, i):
                if i == 0:
                    t.wait_ge(c["on"].sem, c["on"].value(n))
                else:
                    t.wait_ge(c["onT"].sem, c["onT"].value(n, 1))
                for q in range(TB):
                    last = t.transpose(mp[:, q, :], on[:, q, i * P:(i + 1) * P], ident[:, :])
                last.then_inc(c["onp"].sem, 1)

            def project_out(n, i):
                if i == 0:
                    t.wait_ge(c["onT"].sem, c["onT"].value(n))
                else:
                    t.wait_ge(c["x1"].sem, c["x1"].value(n, 1))
                out = mp[:, :, :].rearrange("p a b -> p (a b)")
                for q in range(2):
                    for i2 in range(EC):
                        last = t.matmul(out[:, q * E:(q + 1) * E], onT[:, i2, (2 * i + q) * P:(2 * i + q + 1) * P], wo[:, i2, :],
                                        start=(i2 == 0), stop=(i2 == EC - 1))
                last.then_inc(c["wo"].sem, 1)

            def maxima_back(n, misc_free):
                t.wait_ge(c["nm"].sem, c["nm"].value(n))
                misc_free()
                stand_alone(t, passed)
                for p in range(3):
                    last = t.transpose(mpb[0:NS, p * P:(p + 1) * P], nmb[:, p, :], identb[:, :])
                last.then_inc(c["nmp"].sem, 1)

            def batch(n, first, last):
                for k in range(CH):
                    chunk(n, k)
                    if not last:
                        score_units(n + 1, scores, k)
                    if k == 1 and not first:
                        values(n - 1, CH // 2 - 1)
                    if k % 2 and k >= 3:
                        values(n, (k - 3) // 2)
                    if not first:
                        if k == AT_O_LAST:
                            o_back(n - 1, 3, lambda: (t.wait_ge(c["nmT"].sem, c["nmT"].value(n)),
                                                      t.wait_ge(c["on"].sem, c["on"].value(n - 1, 3))))
                        if k in (AT_ON0, AT_ON1):
                            on_back(n - 1, (AT_ON0, AT_ON1).index(k))
                        if k in (AT_WO0, AT_WO1):
                            project_out(n - 1, (AT_WO0, AT_WO1).index(k))
                    if k in AT_O:
                        g = AT_O.index(k)
                        o_back(n, g, lambda: (t.wait_ge(c["x1"].sem, c["x1"].value(n - 1)) if g == 0 else
                                              t.wait_ge(c["on"].sem, c["on"].value(n, g))))
                if not last:
                    maxima_back(n + 1, lambda: t.wait_ge(c["on"].sem, c["on"].value(n, 3)))

            t.wait_ge(c["once"], 16)
            t.wait_ge(c["rows"], 64)
            for j in range(NS):
                scores(0, j)
            maxima_back(0, lambda: None)
            batch(0, True, False)
            with t.Fori(1, B - 1) as n:
                batch(n, False, False)
            batch(B - 1, False, True)
            values(B - 1, CH // 2 - 1)
            o_back(B - 1, 3, lambda: t.wait_ge(c["on"].sem, c["on"].value(B - 1, 3)))
            for i in range(EC):
                on_back(B - 1, i)
            for i in range(2):
                project_out(B - 1, i)


def route_counts(count, sem):
    return dict(
        once=sem("rt_once"), init=sem("rt_init"), end=sem("rt_end"), pads=sem("rt_pads"), padrow=sem("rt_padrow"),
        tab=sem("rt_tab"), tiles=sem("rt_tiles"), dummy=sem("rt_dummy"),
        x_in=[count(f"rt_x_in{u}", 16) for u in range(2)], base_out=[count(f"rt_base_out{u}", 16) for u in range(2)],
        scat=[count(f"rt_scat{u}", 16 * TB * TOPK, 0) for u in range(2)],
        stats=count("rt_stats", 8), rstd=count("rt_rstd", 2), xn=count("rt_xn", TB), tp=count("rt_tp", 2),
        xT=count("rt_xT", 2), lg=count("rt_lg"), ex=count("rt_ex"), r=count("rt_r", R_STEPS),
        cnt=count("rt_cnt"), up=count("rt_up", TB), silu=count("rt_silu", TB), h=count("rt_h", TB),
        ht=count("rt_ht", TB), hT=count("rt_hT", TB), dn=count("rt_dn", TB), base=count("rt_base", TB),
    )


R_STEPS = 46


def route(nc, a, sc, c, passed, ident, tiles):
    with ExitStack() as es:
        def sb(name, shape, dt=F32):
            return es.enter_context(nc.sbuf_tensor("rt_" + name, shape, dt))

        def pair(name, shape, dt=F32):
            return [sb(f"{name}{u}", shape, dt) for u in range(2)]

        def ps(name, shape, dt=F32):
            return es.enter_context(nc.psum_tensor("rt_" + name, shape, dt))

        gate, wsh, wsd = sb("gate", [P, EC, NE]), sb("wsh", [P, EC, 2 * SI]), sb("wsd", [P, SI // P, E])
        ebias, earlier, regions = sb("ebias", [P, NE]), sb("earlier", [P, NG, NG]), sb("regions", [P, NE])
        before, ones = sb("before", [P, P], BF16), sb("ones", [P, P], BF16)
        before32, half = sb("before32", [P, P]), sb("half", [P, TB])
        x, rows, xT = pair("x", [P, TB, E]), pair("rows", [P, TB, TOPK, ROWW]), pair("xT", [P, EC, S])
        st, mv, var, rstd = pair("st", [P, TB, 6]), pair("mv", [P, TB, 2]), pair("var", [P, TB]), pair("rstd", [P, TB])
        base = pair("base", [P, TB, E])
        slots = pair("slots", [P, TB, TOPK], U32)
        ex, sig, sfc = sb("ex", [P, TB, NE]), sb("sig", [P, TB, NE]), sb("sfc", [P, TB, NE])
        gmax, gcmp, geq, rank = sb("gmax", [P, TB, NG]), sb("gcmp", [P, TB, NG, NG]), sb("geq", [P, TB, NG, NG]), sb("rank", [P, TB, NG])
        cand, left, top = sb("cand", [P, TB, NE + 8]), sb("left", [P, TB, NE + 8]), sb("top", [P, TB, 8])
        sel, selb, wgt = sb("sel", [P, TB, NE]), sb("selb", [P, TB, NE], BF16), sb("wgt", [P, TB, NE])
        wsum, winv = sb("wsum", [P, TB]), sb("winv", [P, TB])
        cnt, key, ktop = sb("cnt", [P, TB + 1, NE]), sb("key", [P, TB, NE]), sb("ktop", [P, TB, 8])
        hit, dst = sb("hit", [P, TB, TOPK, NE]), sb("dst", [P, TB, TOPK], I32)
        sg, h, hT = pair("sg", [P, SI]), pair("h", [P, SI]), pair("hT", [P, SI // P, P])
        padrow, padidx = sb("padrow", [P, ROWW]), sb("padidx", [P, NE], U32)
        ends, starts, ntile = sb("ends", [P, NE]), sb("starts", [P, NE]), sb("ntile", [P, NE])
        nti, zero = sb("nti", [P, NE], I32), sb("zero", [P, NE])
        index, ind, ind2 = sb("index", [P, 2]), sb("ind", [P, 2, NE]), sb("ind2", [P, 2, NE])
        num, start, tab_i = sb("num", [P, 2]), sb("start", [P, 2]), sb("tab_i", [P, 2, 2], I32)
        tp = [ps(f"tp{i}", [P, S]) for i in range(EC)]
        lp = ps("l", [P, 4, TB, NE])
        up = [ps(f"up{i}", [P, 2, SI]) for i in range(2)]
        hp = ps("h", [P, 2 * SI // P, P])
        dp = [ps(f"d{i}", [P, 2 * E]) for i in range(2)]
        block = es.enter_context(nc.Block())

        @block.sync
        def _(sp):
            for dst_, src in ((gate, a["gateT"].rearrange("(c p) e -> p c e", p=P)), (wsh, a["shared"]), (wsd, a["shared_dn"]),
                              (ebias, a["ebias"].to_broadcast([P, NE])), (earlier, a["earlier"].rearrange("p (i j) -> p i j", j=NG)),
                              (regions, a["regions"]), (before32, a["before"])):
                sp.dma_start(dst_[tuple(slice(None) for _ in dst_.shape)], src).then_inc(c["once"], 16)

            def load(n, u):
                sp.dma_start(x[u][:, :, :], sc["x1"][bass.ds(n, 1)].rearrange("o p t e -> (o p) t e")).then_inc(c["x_in"][u].sem, 16)

            def step(n, u, last):
                sp.wait_ge(c["base"].sem, c["base"].value(n))
                sp.dma_start(sc["base"][bass.ds(n, 1)].rearrange("o p t e -> (o p) t e"), base[u][:, :, :]).then_inc(c["base_out"][u].sem, 16)
                if not last:
                    sp.wait_ge(c["xn"].sem, c["xn"].value(n))
                    load(n + 2, u)

            load(0, 0)
            load(1, 1)
            with sp.Fori(0, B // 2 - 1) as it:
                for u in range(2):
                    step(it * 2 + u, u, False)
            for u in range(2):
                step(B - 2 + u, u, True)
            for u in range(2):
                sp.wait_ge(c["base_out"][u].sem, c["base_out"][u].value(B // 2 - 1))
            sp.wait_ge(c["end"], T_LAST)
            sp.dma_start(sc["tiletab"].rearrange("w p c -> p w c"), tab_i[:, :, :]).then_inc(c["tab"], 16)
            sp.wait_ge(c["tab"], 16)
            sp.dma_start(tiles[:, :, :], sc["tiletab"].rearrange("w p c -> (w p c)").rearrange("(o w i) -> o w i", o=1, w=2)).then_inc(c["tiles"], 16)
            sp.wait_ge(c["padrow"], 1)
            sp.dma_start(sc["slots"][PADS:PADS + P, :], padrow[:, :]).then_inc(c["dummy"], 16)
            sp.wait_ge(c["tiles"], 16)
            sp.wait_ge(c["dummy"], 16)

        @block.gpsimd
        def _(g):
            init = c["init"]
            g.memset(half[:, :], -0.5).then_inc(init, 1)
            g.memset(ones[:, :], 1.0).then_inc(init, 1)
            g.memset(cand[:, :, :], SENT).then_inc(init, 1)
            g.memset(cnt[:, :, :], 0.0).then_inc(init, 1)
            g.memset(zero[:, :], 0.0).then_inc(init, 1)
            for u in range(2):
                g.memset(rows[u][:, :, :, :], 0.0).then_inc(init, 1)
            g.memset(padrow[:, :], 0.0).then_inc(init, 1)
            g.iota(dst[:, :, :], [[P, TB], [B * S, TOPK]], base=0, channel_multiplier=1).then_inc(init, 1)
            g.iota(index[:, :], [[1, 2]], base=0, channel_multiplier=2, allow_small_or_imprecise_dtypes=True).then_inc(init, 1)
            g.wait_ge(init, 10)
            g.memset(padrow[:, E + 1:E + 2].bitcast(I32), 1 << 20).then_inc(c["padrow"], 1)

            def norm(n, u):
                g.wait_ge(c["stats"].sem, c["stats"].value(n))
                stand_alone(g, passed)
                g.tensor_scalar(var[u][:, :], mv[u][:, :, 1], EPS, None, ALU.add).then_inc(c["rstd"].sem, 1)
                g.wait_ge(c["rstd"].sem, c["rstd"].value(n, 1))
                g.tensor_tensor(rstd[u][:, :], var[u][:, :], half[:, :], ALU.pow).then_inc(c["rstd"].sem, 1)

            def body(n, u, last):
                if not last:
                    norm(n + 1, 1 - u)
                g.wait_ge(c["r"].sem, c["r"].value(n))
                stand_alone(g, passed)
                for t in range(TB):
                    for j in range(TOPK):
                        g.indirect_dma_start(sc["slots"], bass.IndirectOffsetOnAxis(ap=slots[u][:, t, j:j + 1], axis=0),
                                             rows[u][:, t, j, :], None).then_inc(c["scat"][u].sem, 16)

            norm(0, 0)
            with g.Fori(0, B // 2 - 1) as it:
                for u in range(2):
                    body(it * 2 + u, u, False)
            body(B - 2, 0, False)
            body(B - 1, 1, True)
            g.wait_ge(c["end"], 1)
            g.wait_ge(c["padrow"], 1)
            for e in range(NE):
                g.indirect_dma_start(sc["slots"], bass.IndirectOffsetOnAxis(ap=padidx[:, e:e + 1], axis=0),
                                     padrow[:, :], None).then_inc(c["pads"], 16)
            for u in range(2):
                g.wait_ge(c["scat"][u].sem, c["scat"][u].value(B // 2 - 1))
            g.wait_ge(c["pads"], 16 * NE)

        def over_experts(ap):
            return ap

        @block.vector
        def _(v):
            def scattered(u, it):
                if not isinstance(it, int) or it:
                    v.wait_ge(c["scat"][u].sem, c["scat"][u].value(it - 1))

            def stats(n, u, it):
                v.wait_ge(c["x_in"][u].sem, c["x_in"][u].value(it))
                v.wait_ge(c["xn"].sem, c["xn"].value(n - 2))
                for t in range(TB):
                    v.bn_stats(st[u][:, t, :], x[u][:, t, :]).then_inc(c["stats"].sem, 1)
                v.wait_ge(c["stats"].sem, c["stats"].value(n, TB))
                stand_alone(v, passed)
                for t in range(TB):
                    v.bn_aggr(mv[u][:, t, :], st[u][:, t, :]).then_inc(c["stats"].sem, 1)

            def normalise(n, u, it):
                v.wait_ge(c["rstd"].sem, c["rstd"].value(n))
                scattered(u, it)
                v.wait_ge(c["tp"].sem, c["tp"].value(n - 2))
                for t in range(TB):
                    v.tensor_scalar(rows[u][:, t, :, 0:E], x[u][:, t:t + 1, :].to_broadcast([P, TOPK, E]), mv[u][:, t, 0:1],
                                    rstd[u][:, t:t + 1], ALU.subtract, ALU.mult).then_inc(c["xn"].sem, 1)

            def choose(n, u, it):
                k = c["r"]
                done = [0]

                def step(*ops):
                    if done[0]:
                        v.wait_ge(k.sem, k.value(n, done[0]))
                    if len(ops) == TB:
                        stand_alone(v, passed)
                    for op in ops:
                        op().then_inc(k.sem, 1)
                        done[0] += 1

                v.wait_ge(k.sem, k.value(n - 1))
                v.wait_ge(c["ex"].sem, c["ex"].value(n))
                groups = lambda ap: ap.rearrange("p t (g s) -> p t g s", s=GS)
                last1 = lambda ap: ap.rearrange("p t (g o) -> p t g o", o=1)
                step(lambda: v.tensor_scalar(sig[:, :, :], ex[:, :, :], 1.0, None, ALU.add))
                step(lambda: v.reciprocal(sig[:, :, :], sig[:, :, :]))
                step(lambda: v.tensor_tensor(sfc[:, :, :], sig[:, :, :],
                                             ebias[:, :].rearrange("p (o e) -> p o e", o=1).to_broadcast([P, TB, NE]), ALU.add))
                step(lambda: v.tensor_reduce(gmax[:, :, :], groups(sfc[:, :, :]), X, ALU.max))
                gi = last1(gmax[:, :, :]).to_broadcast([P, TB, NG, NG])
                gj = gmax[:, :, :].rearrange("p t (o g) -> p t o g", o=1).to_broadcast([P, TB, NG, NG])
                step(lambda: v.tensor_tensor(gcmp[:, :, :, :], gj, gi, ALU.is_gt),
                     lambda: v.tensor_tensor(geq[:, :, :, :], gj, gi, ALU.is_equal))
                step(lambda: v.tensor_tensor(geq[:, :, :, :], geq[:, :, :, :],
                                             earlier[:, :, :].rearrange("p (o i) j -> p o i j", o=1).to_broadcast([P, TB, NG, NG]), ALU.mult))
                step(lambda: v.tensor_tensor(gcmp[:, :, :, :], gcmp[:, :, :, :], geq[:, :, :, :], ALU.add))
                step(lambda: v.tensor_reduce(rank[:, :, :], gcmp[:, :, :, :], X, ALU.add))
                step(lambda: v.tensor_scalar(rank[:, :, :], rank[:, :, :], float(TOPG), None, ALU.is_lt))
                step(lambda: v.tensor_tensor(cand[:, :, 0:NE].rearrange("p t (g s) -> p t g s", s=GS), groups(sfc[:, :, :]),
                                             last1(rank[:, :, :]).to_broadcast([P, TB, NG, GS]), ALU.mult))
                step(*[lambda t=t: v.max(top[:, t, :], cand[:, t, :]) for t in range(TB)])
                step(lambda: v.memset(top[:, :, TOPK:8], SENT))
                step(*[lambda t=t: v.match_replace(left[:, t, :], top[:, t, :], cand[:, t, :], 2 * SENT) for t in range(TB)])
                step(lambda: v.tensor_scalar(sel[:, :, :], left[:, :, 0:NE], 1.5 * SENT, None, ALU.is_lt))
                step(lambda: v.tensor_copy(selb[:, :, :], sel[:, :, :]),
                     lambda: v.tensor_tensor(wgt[:, :, :], sel[:, :, :], sig[:, :, :], ALU.mult))
                step(lambda: v.tensor_reduce(wsum[:, :], wgt[:, :, :], X, ALU.add))
                step(lambda: v.tensor_scalar(wsum[:, :], wsum[:, :], 1e-20, None, ALU.add))
                step(lambda: v.reciprocal(winv[:, :], wsum[:, :]))
                step(lambda: v.tensor_scalar(winv[:, :], winv[:, :], SCALE, None, ALU.mult))
                step(lambda: v.tensor_tensor(wgt[:, :, :], wgt[:, :, :],
                                             winv[:, :].rearrange("p (t o) -> p t o", o=1).to_broadcast([P, TB, NE]), ALU.mult),
                     lambda: v.tensor_copy(cnt[:, 0, :], cnt[:, TB, :]))
                v.wait_ge(c["cnt"].sem, c["cnt"].value(n))
                for t in range(TB):
                    step(lambda: v.tensor_tensor(cnt[:, t + 1, :], cnt[:, t, :], lp[:, 2, t, :], ALU.add))
                step(lambda: v.tensor_tensor(key[:, :, :], lp[:, 1, :, :], cnt[:, 0:TB, :], ALU.add))
                step(lambda: v.scalar_tensor_tensor(key[:, :, :], key[:, :, :], 1.0,
                                                    regions[:, :].rearrange("p (o e) -> p o e", o=1).to_broadcast([P, TB, NE]), ALU.add, ALU.add))
                step(lambda: v.tensor_tensor(key[:, :, :], key[:, :, :], sel[:, :, :], ALU.mult))
                step(*[lambda t=t: v.max(ktop[:, t, :], key[:, t, :]) for t in range(TB)])
                scattered(u, it)
                step(lambda: v.tensor_scalar(slots[u][:, :, :], ktop[:, :, 0:TOPK], -1.0, None, ALU.add),
                     lambda: v.tensor_tensor(hit[:, :, :, :], key[:, :, :].rearrange("p t (o e) -> p t o e", o=1).to_broadcast([P, TB, TOPK, NE]),
                                             last1(ktop[:, :, 0:TOPK]).to_broadcast([P, TB, TOPK, NE]), ALU.is_equal),
                     lambda: v.tensor_copy(rows[u][:, :, :, E + 1].bitcast(I32), dst[:, :, :]))
                step(lambda: v.tensor_tensor(hit[:, :, :, :], hit[:, :, :, :],
                                             wgt[:, :, :].rearrange("p t (o e) -> p t o e", o=1).to_broadcast([P, TB, TOPK, NE]), ALU.mult),
                     lambda: v.tensor_scalar(dst[:, :, :], dst[:, :, :], float(S), None, ALU.add))
                step(lambda: v.tensor_reduce(rows[u][:, :, :, E], hit[:, :, :, :], X, ALU.add))
                assert done[0] == R_STEPS, done

            def shared(n, u, it):
                v.wait_ge(c["base_out"][u].sem, c["base_out"][u].value(it - 1))
                for t in range(TB + 1):
                    if t < TB:
                        v.wait_ge(c["silu"].sem, c["silu"].value(n, t + 1))
                        v.wait_ge(c["ht"].sem, c["ht"].value(n, t - 1))
                        v.tensor_tensor(h[t % 2][:, :], sg[t % 2][:, :], up[t % 2][:, 1, :], ALU.mult).then_inc(c["h"].sem, 1)
                    if t:
                        v.wait_ge(c["dn"].sem, c["dn"].value(n, t))
                        v.tensor_tensor(base[u][:, t - 1, :], dp[(t - 1) % 2][:, 0:E], x[u][:, t - 1, :], ALU.add).then_inc(c["base"].sem, 1)

            v.wait_ge(c["init"], 10)
            v.wait_ge(c["once"], 7 * 16)
            v.tensor_copy(before[:, :], before32[:, :]).then_inc(c["init"], 1)
            stats(0, 0, 0)
            normalise(0, 0, 0)

            def body(n, u, it, last):
                choose(n, u, it)
                if not last:
                    stats(n + 1, 1 - u, it + u)
                shared(n, u, it)
                if not last:
                    normalise(n + 1, 1 - u, it + u)

            body(0, 0, 0, False)
            body(1, 1, 0, False)
            with v.Fori(1, B // 2 - 1) as it:
                for u in range(2):
                    body(it * 2 + u, u, it, False)
            body(B - 2, 0, B // 2 - 1, False)
            body(B - 1, 1, B // 2 - 1, True)

            end = c["end"]
            last = cnt[:, TB, :]
            v.wait_ge(c["r"].sem, c["r"].value(B - 1))
            done = [0]

            def step(op):
                if done[0]:
                    v.wait_ge(end, done[0])
                op().then_inc(end, 1)
                done[0] += 1

            v.tensor_scalar(num[:, :], index[:, :], 0.5, None, ALU.mult).then_inc(c["init"], 1)
            v.wait_ge(c["init"], 12)
            step(lambda: v.scalar_tensor_tensor(padidx[:, :], last, num[:, 0:1], regions[:, :], ALU.add, ALU.add))
            step(lambda: v.tensor_scalar(nti[:, :], last, float(P - 1), None, ALU.add))
            step(lambda: v.tensor_scalar(nti[:, :], nti[:, :], 7, None, ALU.logical_shift_right))
            step(lambda: v.tensor_copy(ntile[:, :], nti[:, :]))
            step(lambda: v.tensor_tensor_scan(ends[:, :], ntile[:, :], zero[:, :], 0.0, ALU.add, ALU.add))
            e3 = lambda ap: ap.rearrange("p (o e) -> p o e", o=1).to_broadcast([P, 2, NE])
            i3 = lambda ap: ap.rearrange("p (c o) -> p c o", o=1).to_broadcast([P, 2, NE])
            step(lambda: v.tensor_tensor(ind[:, :, :], i3(index[:, :]), e3(ends[:, :]), ALU.is_ge))
            step(lambda: v.tensor_reduce(num[:, :], ind[:, :, :], X, ALU.add))
            step(lambda: v.tensor_tensor(ind2[:, :, :], ind[:, :, :], e3(ntile[:, :]), ALU.mult))
            step(lambda: v.tensor_reduce(start[:, :], ind2[:, :, :], X, ALU.add))
            step(lambda: v.tensor_scalar(tab_i[:, 1, :], num[:, :], float(NE - 1), None, ALU.min))
            step(lambda: v.tensor_sub(start[:, :], index[:, :], start[:, :]))
            step(lambda: v.tensor_scalar(start[:, :], start[:, :], float(P), None, ALU.mult))
            step(lambda: v.scalar_tensor_tensor(start[:, :], num[:, :], float(REG), start[:, :], ALU.mult, ALU.add))
            step(lambda: v.tensor_scalar(tab_i[:, 0, :], start[:, :], float(PADS), None, ALU.min))
            assert done[0] == T_LAST

        @block.scalar
        def _(s):
            def xT_out(n, u):
                for i in range(EC):
                    s.wait_ge(c["tp"].sem, c["tp"].value(n, i + 1))
                    s.wait_ge(c["up"].sem, c["up"].value(n - 2))
                    s.copy(xT[u][:, i, :], tp[i][:, :]).then_inc(c["xT"].sem, 1)

            def body(n, u, last):
                s.wait_ge(c["lg"].sem, c["lg"].value(n))
                s.wait_ge(c["r"].sem, c["r"].value(n - 1))
                s.activation(ex[:, :, :], lp[:, 0, :, :], ACT.Exp, scale=-1.0).then_inc(c["ex"].sem, 1)
                for t in range(TB + 1):
                    if t < TB:
                        s.wait_ge(c["up"].sem, c["up"].value(n, t + 1))
                        s.wait_ge(c["h"].sem, c["h"].value(n, t - 1))
                        s.activation(sg[t % 2][:, :], up[t % 2][:, 0, :], ACT.Silu).then_inc(c["silu"].sem, 1)
                    if t:
                        s.wait_ge(c["ht"].sem, c["ht"].value(n, t))
                        s.wait_ge(c["dn"].sem, c["dn"].value(n, t - 2))
                        s.copy(hT[(t - 1) % 2][:, :, :], hp[:, 0:SI // P, :]).then_inc(c["hT"].sem, 1)
                if not last:
                    xT_out(n + 1, 1 - u)

            xT_out(0, 0)
            with s.Fori(0, B // 2 - 1) as it:
                for u in range(2):
                    body(it * 2 + u, u, False)
            body(B - 2, 0, False)
            body(B - 1, 1, True)

        @block.tensor
        def _(t_):
            def transposes(n, u):
                t_.wait_ge(c["xn"].sem, c["xn"].value(n))
                for i in range(EC):
                    t_.wait_ge(c["xT"].sem, c["xT"].value(n - 1, i + 1))
                    for t in range(TB):
                        last = t_.transpose(tp[i][:, t * P:(t + 1) * P], rows[u][:, t, 0, i * P:(i + 1) * P], ident[:, :])
                    last.then_inc(c["tp"].sem, 1)

            def logits(n, u):
                t_.wait_ge(c["xT"].sem, c["xT"].value(n))
                t_.wait_ge(c["r"].sem, c["r"].value(n - 1))
                for t in range(TB):
                    for i in range(EC):
                        last = t_.matmul(lp[:, 0, t, :], xT[u][:, i, t * P:(t + 1) * P], gate[:, i, :], start=(i == 0), stop=(i == EC - 1))
                last.then_inc(c["lg"].sem, 1)

            def shared_up(n, u, t):
                t_.wait_ge(c["h"].sem, c["h"].value(n, t - 1))
                for i in range(EC):
                    last = t_.matmul(up[t % 2][:, :, :].rearrange("p a b -> p (a b)"), xT[u][:, i, t * P:(t + 1) * P], wsh[:, i, :],
                                     start=(i == 0), stop=(i == EC - 1))
                last.then_inc(c["up"].sem, 1)

            def hidden_back(n, t):
                t_.wait_ge(c["h"].sem, c["h"].value(n, t + 1))
                t_.wait_ge(c["hT"].sem, c["hT"].value(n, t))
                for i in range(SI // P):
                    last = t_.transpose(hp[:, i, :], h[t % 2][:, i * P:(i + 1) * P], ident[:, :])
                last.then_inc(c["ht"].sem, 1)

            def shared_down(n, t):
                t_.wait_ge(c["hT"].sem, c["hT"].value(n, t + 1))
                t_.wait_ge(c["base"].sem, c["base"].value(n, t - 1))
                for i in range(SI // P):
                    last = t_.matmul(dp[t % 2][:, 0:E], hT[t % 2][:, i, :], wsd[:, i, :], start=(i == 0), stop=(i == SI // P - 1))
                last.then_inc(c["dn"].sem, 1)

            def counts(n):
                t_.wait_ge(c["r"].sem, c["r"].value(n, R_SELECTED))
                flat = selb[:, :, :].rearrange("p t e -> p (t e)")
                t_.matmul(lp[:, 1, :, :].rearrange("p t e -> p (t e)"), before[:, :], flat, start=True, stop=True)
                t_.matmul(lp[:, 2, :, :].rearrange("p t e -> p (t e)"), ones[:, :], flat, start=True, stop=True).then_inc(c["cnt"].sem, 1)

            def body(n, u, last):
                logits(n, u)
                for t in range(TB):
                    shared_up(n, u, t)
                    if t == 0:
                        counts(n)
                    else:
                        hidden_back(n, t - 1)
                        shared_down(n, t - 1)
                hidden_back(n, TB - 1)
                shared_down(n, TB - 1)
                if not last:
                    transposes(n + 1, 1 - u)

            t_.wait_ge(c["once"], 7 * 16)
            t_.wait_ge(c["init"], 11)
            transposes(0, 0)
            with t_.Fori(0, B // 2 - 1) as it:
                for u in range(2):
                    body(it * 2 + u, u, False)
            body(B - 2, 0, False)
            body(B - 1, 1, True)


T_LAST = 14
R_SELECTED = 22


XR = 8


def expert_counts(count, sem):
    return dict(
        weights=sem("ex_weights"), x_in=[count(f"ex_x_in{u}", 16) for u in range(XR)],
        y_out=[count(f"ex_y_out{u}", 16, 0) for u in range(XR)], all_out=sem("ex_all_out"),
        tp=count("ex_tp"), xT=count("ex_xT"), up=count("ex_up"), silu=count("ex_silu"), h=count("ex_h"),
        ht=count("ex_ht"), hT=count("ex_hT"), dn=count("ex_dn"), y=count("ex_y"),
    )


def experts(nc, a, sc, c, passed, ident, tiles):
    with ExitStack() as es:
        def ring(k, name, shape, dt=F32):
            return [es.enter_context(nc.sbuf_tensor(f"ex_{name}{u}", shape, dt)) for u in range(k)]

        def banks(name):
            return [es.enter_context(nc.psum_tensor(f"ex_{name}{u}", [P, 512], F32)) for u in range(2)]

        gu = es.enter_context(nc.sbuf_tensor("gu", [P, NE, EC, 2 * FI], F32))
        dn = es.enter_context(nc.sbuf_tensor("dn", [P, NE, E], F32))
        x, xT = ring(XR, "x", [P, ROWW]), ring(2, "xT", [P, EC, P])
        sg, h, hT, y = ring(2, "sg", [P, FI]), ring(2, "h", [P, FI]), ring(2, "hT", [FI, P]), ring(XR, "y", [P, E])
        tp, up, hp, dp = banks("tp"), banks("up"), banks("hp"), banks("dp")
        tp_, up_ = [b[:, 0:E].rearrange("p (c q) -> p c q", c=EC) for b in tp], [b[:, 0:2 * FI].rearrange("p (c i) -> p c i", c=2) for b in up]
        block = es.enter_context(nc.Block())
        U = XR

        def loop(eng, body, peel=1):
            for n in range(peel * U):
                body(n, n % U, n // U, n < U, False)
            with eng.Fori(peel, TILES // U - 1) as it:
                for u in range(U):
                    body(it * U + u, u, it, False, False)
            for u in range(U):
                body(TILES - U + u, u, TILES // U - 1, False, True)

        @block.sync
        def _(sp):
            def load(n, u):
                at = sp.value_load(tiles[0:1, 0, bass.ds(n, 1)], min_val=0, max_val=PADS)
                sp.dma_start(x[u][:, :], sc["slots"][bass.ds(at, P), :]).then_inc(c["x_in"][u].sem, 16)

            for u in range(U):
                load(u, u)
            for e in range(0, NE, 4):
                sp.dma_start(gu[:, e:e + 4, :, :], a["gu"][:, e:e + 4, :, :]).then_inc(c["weights"], 16)
                sp.dma_start(dn[:, e:e + 4, :], a["dn"][:, e:e + 4, :]).then_inc(c["weights"], 16)

            def body(n, u, it, first, last):
                if not last:
                    sp.wait_ge(c["y"].sem, c["y"].value(n))
                    sp.wait_ge(c["y_out"][u].sem, c["y_out"][u].value(it))
                    load(n + U, u)

            loop(sp, body)

        @block.gpsimd
        def _(g):
            def body(n, u, it, first, last):
                g.wait_ge(c["y"].sem, c["y"].value(n))
                stand_alone(g, passed)
                g.indirect_dma_start(sc["y"], bass.IndirectOffsetOnAxis(ap=x[u][:, E + 1:E + 2].bitcast(U32), axis=0),
                                     y[u][:, :], None, bounds_check=NY - 1, oob_is_err=False).then_inc(c["y_out"][u].sem, 16)

            loop(g, body)
            for u in range(U):
                g.wait_ge(c["y_out"][u].sem, c["y_out"][u].value(TILES // U - 1))

        @block.scalar
        def _(s):
            def xT_out(n, u):
                s.wait_ge(c["tp"].sem, c["tp"].value(n))
                s.wait_ge(c["up"].sem, c["up"].value(n - 2))
                s.copy(xT[u % 2][:, :, :], tp_[u % 2]).then_inc(c["xT"].sem, 1)

            def body(n, u, it, first, last):
                s.wait_ge(c["up"].sem, c["up"].value(n))
                s.wait_ge(c["h"].sem, c["h"].value(n - 2))
                s.activation(sg[u % 2][:, :], up_[u % 2][:, 0, :], ACT.Silu).then_inc(c["silu"].sem, 1)
                if not (last and u >= U - 2):
                    xT_out(n + 2, u + 2)
                s.wait_ge(c["ht"].sem, c["ht"].value(n))
                s.wait_ge(c["dn"].sem, c["dn"].value(n - 2))
                s.copy(hT[u % 2][:, :], hp[u % 2][:, 0:P]).then_inc(c["hT"].sem, 1)

            xT_out(0, 0)
            xT_out(1, 1)
            loop(s, body)

        @block.vector
        def _(v):
            def weigh(n, u, it, first):
                v.wait_ge(c["dn"].sem, c["dn"].value(n))
                if not first:
                    v.wait_ge(c["y_out"][u].sem, c["y_out"][u].value(it - 1))
                v.tensor_scalar(y[u][:, :], dp[u % 2][:, 0:E], x[u][:, E:E + 1], None, ALU.mult).then_inc(c["y"].sem, 1)

            def body(n, u, it, first, last):
                v.wait_ge(c["silu"].sem, c["silu"].value(n))
                v.wait_ge(c["ht"].sem, c["ht"].value(n - 2))
                v.tensor_tensor(h[u % 2][:, :], sg[u % 2][:, :], up_[u % 2][:, 1, :], ALU.mult).then_inc(c["h"].sem, 1)
                if u:
                    weigh(n - 1, u - 1, it, first)
                elif not first:
                    weigh(n - 1, U - 1, it - 1, isinstance(it, int) and it == 1)

            loop(v, body, 2)
            weigh(TILES - 1, U - 1, TILES // U - 1, False)

        @block.tensor
        def _(t):
            def x_back(n, u, it):
                t.wait_ge(c["x_in"][u].sem, c["x_in"][u].value(it))
                t.wait_ge(c["xT"].sem, c["xT"].value(n - 2))
                for i in range(EC):
                    last = t.transpose(tp_[u % 2][:, i, :], x[u][:, i * P:(i + 1) * P], ident[:, :])
                last.then_inc(c["tp"].sem, 1)

            def expert_of(n):
                return t.value_load(tiles[0:1, 1, bass.ds(n, 1)], min_val=0, max_val=NE - 1)

            def down(n, u, e):
                t.wait_ge(c["hT"].sem, c["hT"].value(n))
                t.wait_ge(c["y"].sem, c["y"].value(n - 2))
                t.matmul(dp[u % 2][:, 0:E], hT[u % 2][:, :], dn[:, bass.ds(e, 1), :].rearrange("p o h -> p (o h)"),
                         start=True, stop=True).then_inc(c["dn"].sem, 1)

            def body(n, u, it, first, last):
                e = expert_of(n)
                t.wait_ge(c["xT"].sem, c["xT"].value(n))
                t.wait_ge(c["h"].sem, c["h"].value(n - 2))
                for i in range(EC):
                    mm = t.matmul(up[u % 2][:, 0:2 * FI], xT[u % 2][:, i, :],
                                  gu[:, bass.ds(e, 1), i, :].rearrange("p o h -> p (o h)"), start=(i == 0), stop=(i == EC - 1))
                mm.then_inc(c["up"].sem, 1)
                if not (last and u >= U - 2):
                    x_back(n + 2, (u + 2) % U, it + (u + 2) // U)
                if not (first and u == 0):
                    down(n - 1, (u - 1) % U, expert_of(n - 1))
                t.wait_ge(c["h"].sem, c["h"].value(n))
                t.wait_ge(c["hT"].sem, c["hT"].value(n - 2))
                t.transpose(hp[u % 2][:, 0:P], h[u % 2][:, :], ident[:, :]).then_inc(c["ht"].sem, 1)

            x_back(0, 0, 0)
            x_back(1, 1, 0)
            t.wait_ge(c["weights"], 16 * NE // 2)
            loop(t, body)
            down(TILES - 1, U - 1, expert_of(TILES - 1))


def combine_counts(count, sem):
    return dict(b_in=[count(f"co_b_in{u}", 16) for u in range(4)], y_in=[count(f"co_y_in{u}", 16) for u in range(4)],
                out=[count(f"co_out{u}", 16) for u in range(4)],
                add=count("co_add", TOPK), addp=count("co_addp", TOPK))


def combine(nc, a, sc, c, out):
    U = 4
    with ExitStack() as es:
        acc = [es.enter_context(nc.sbuf_tensor(f"acc{u}", [P, E], F32)) for u in range(U)]
        y = [es.enter_context(nc.sbuf_tensor(f"yy{u}", [P, TOPK, E], F32)) for u in range(U)]
        block = es.enter_context(nc.Block())
        base = sc["base"].rearrange("b p t e -> (b t) p e") if False else sc["base"]
        y_rows = sc["y"].rearrange("(j n p) e -> n p j e", j=TOPK, p=P)
        out_rows = out.rearrange("(n p) e -> n p e", p=P)

        def sum_sem(u):
            return c["add"] if u % 2 == 0 else c["addp"]

        @block.sync
        def _(sp):
            def load(it, u):
                sp.dma_start(acc[u][:, :], sc["base"][bass.ds(it, 1), :, u, :].rearrange("o p e -> (o p) e")).then_inc(c["b_in"][u].sem, 16)
                sp.dma_start(y[u][:, :, :], y_rows[bass.ds(it * TB + u, 1)].rearrange("o p j e -> (o p) j e")).then_inc(c["y_in"][u].sem, 16)

            for u in range(U):
                load(0, u)
            with sp.Fori(1, B) as it:
                for u in range(U):
                    sp.wait_ge(c["out"][u].sem, c["out"][u].value(it - 1))
                    load(it, u)

        @block.scalar
        def _(s):
            with s.Fori(0, B) as it:
                for u in range(U):
                    k = sum_sem(u)
                    s.wait_ge(k.sem, k.value(it * 2 + u // 2))
                    s.dma_start(out_rows[bass.ds(it * TB + u, 1)].rearrange("o p e -> (o p) e"), acc[u][:, :]).then_inc(c["out"][u].sem, 16)
            for u in range(U):
                s.wait_ge(c["out"][u].sem, c["out"][u].value(B - 1))

        def sums(eng, k, odd):
            with eng.Fori(0, B) as it:
                for half in range(2):
                    u, m = 2 * half + odd, it * 2 + half
                    eng.wait_ge(c["b_in"][u].sem, c["b_in"][u].value(it))
                    eng.wait_ge(c["y_in"][u].sem, c["y_in"][u].value(it))
                    for j in range(TOPK):
                        if j:
                            eng.wait_ge(k.sem, k.value(m, j))
                        eng.tensor_tensor(acc[u][:, :], acc[u][:, :], y[u][:, j, :], ALU.add).then_inc(k.sem, 1)

        @block.vector
        def _(v):
            sums(v, c["add"], 0)

        @block.gpsimd
        def _(g):
            sums(g, c["addp"], 1)


def shape_constants():
    bucket = np.searchsorted(BUCKET_STARTS, np.arange(S), side="right") - 1
    rel = P - 1 - NEAR_LO - np.arange(DIAG)
    of = np.where(rel > 0, BUCKETS // 2, 0) + bucket[np.abs(rel)]
    onehot_diag = (of[None, :] == np.arange(BUCKETS)[:, None]).astype(np.float32)
    u = np.arange(S)[None, :] - P * np.arange(TB)[:, None]
    far = np.where(u < NEAR_LO, BUCKETS - 1, np.where(u >= NEAR_LO + NEAR_W, BUCKETS // 2 - 1, -1)).reshape(-1)
    onehot_far = (far[None, :] == np.arange(BUCKETS)[:, None]).astype(np.float32)
    blocks = (np.arange(S)[None, :] // P == np.arange(TB)[:, None]).astype(np.float32)
    krows = np.concatenate([np.ones((3, S), np.float32), blocks, blocks, blocks])
    g = np.arange(NG)
    return dict(
        eye=np.eye(P, dtype=np.float32), onehot_diag=onehot_diag, onehot_far=onehot_far, krows=krows,
        before=np.triu(np.ones((P, P), np.float32), 1),
        earlier=np.broadcast_to((g[None, :] < g[:, None]).astype(np.float32).reshape(1, -1), (P, NG * NG)).copy(),
        regions=np.broadcast_to(np.arange(NE, dtype=np.float32)[None, :] * REG, (P, NE)).copy(),
    )


def arrays_of(i):
    n = lambda k: np.asarray(i[k])
    t = np.ascontiguousarray
    gu = n("L0_ffn_experts_gate_up")
    shared = np.concatenate([n("L0_ffn_shared_gate_w"), n("L0_ffn_shared_up_w")])
    return dict(
        x=t(n("x").reshape(B * S, E)), ctxT=t(n("ctx_1024").reshape(B * S, E).T),
        wq=t(n("L0_xattn_Wq")), wkv=t(n("L0_xattn_Wkv")), wo=t(n("L0_xattn_Wo")),
        rel_bias=t(n("L0_xattn_rel_bias").T), gateT=t(n("L0_ffn_gate_weight").T),
        ebias=t(n("L0_ffn_e_score_correction_bias").reshape(1, NE)),
        gu=t(gu.reshape(NE, 2 * FI, EC, P).transpose(3, 0, 2, 1)),
        dn=t(n("L0_ffn_experts_down").transpose(2, 0, 1)),
        shared=t(shared.reshape(2 * SI, EC, P).transpose(2, 1, 0)),
        shared_dn=t(n("L0_ffn_shared_down_w").reshape(E, SI // P, P).transpose(2, 1, 0)),
        **shape_constants(),
    )


def kernel(**inputs):
    import concourse.bacc as bacc
    from concourse.bass_utils import run_bass_kernel_spmd

    nc = bacc.Bacc("TRN2", target_bir_lowering=False, num_devices=1)
    arrays = arrays_of(inputs)
    a = {k: nc.dram_tensor("in_" + k, v.shape, mybir.dt.from_np(v.dtype), kind="ExternalInput").ap() for k, v in arrays.items()}
    out = nc.dram_tensor("out", (B * S, E), F32, kind="ExternalOutput").ap()
    build(nc, a, out)
    r = run_bass_kernel_spmd(nc, [{"in_" + k: v for k, v in arrays.items()}], core_ids=[0])
    return r.results[0]["out"].reshape(B, S, E)
```

```python
import numpy as np
import concourse.bass as bass
import concourse.mybir as mybir
from contextlib import ExitStack

F32 = mybir.dt.float32
BF16 = mybir.dt.bfloat16
I32 = mybir.dt.int32
U32 = mybir.dt.uint32
ALU = mybir.AluOpType
ACT = mybir.ActivationFunctionType
X = mybir.AxisListType.X

P = 128
B, S, E = 8, 512, 256
H, D = 16, 16
TB = S // P
EC = E // P
NT = B * TB
EPS = 1e-5

BUCKETS = 32
BUCKET_STARTS = [0, 1, 2, 3, 4, 5, 6, 7, 8, 12, 16, 23, 32, 46, 64, 91]
FAR = BUCKET_STARTS[-1]
NEAR_LO = -(FAR - 1)
NEAR_W = P + 2 * (FAR - 1)
DIAG = NEAR_W + P - 1

TERMS = [(0, 0), (0, 1), (1, 0), (1, 1), (0, 2), (2, 0)]
KQ = len(TERMS) * D
ROW_MAX = KQ
ROW_FAR = KQ + 3
KS = ROW_FAR + 3 * TB
VW = 32
CH = 2 * TB * 4
NS = H * TB

NE, TOPK, NG, TOPG, SCALE = 32, 6, 8, 4, 2.5
GS = NE // NG
FI, SI = 128, 256
REG = B * S + P
PADS = NE * REG
ROWW = E + 4
TILES = 224
NY = TOPK * B * S
SENT = -1e30


class Count:

    def __init__(self, sem, per=1, ahead=2):
        self.sem, self.per, self.ahead = sem, per, ahead

    def value(self, n, part=None):
        return (n + self.ahead) * self.per + (self.per if part is None else part)


def stand_alone(eng, passed):
    eng.sem_inc(passed, 1)


def build(nc, a, out):
    ctx = ExitStack()
    counts = []

    def sem(name):
        return ctx.enter_context(nc.semaphore(name))

    def count(name, per=1, ahead=2):
        c = Count(sem(name), per, ahead)
        counts.append(c)
        return c

    def dram(name, shape, dt):
        return nc.dram_tensor(name, shape, dt, kind="Internal").ap()

    with ctx:
        sc = dict(
            parts=dram("parts", [B, 2, E, 3, S], BF16),
            v=dram("v", [B, P, TB, H, VW], F32),
            diag=dram("diag", [H, P, DIAG + P], F32),
            krows=dram("krows", [KS - ROW_MAX, S], BF16),
            far=dram("far", [3, TB, H, S], BF16),
            negmax=dram("negmax", [B, 3, NS, P], BF16),
            x1=dram("x1", [B, P, TB, E], F32),
            base=dram("base", [B, P, TB, E], F32),
            slots=dram("slots", [PADS + P, ROWW], F32),
            tiletab=dram("tiletab", [2, P, 2], I32),
            y=dram("y", [NY, E], F32),
        )
        passed = sem("passed")
        c1, c2 = project_counts(count, sem), attend_counts(count, sem)
        c3, c4, c5 = route_counts(count, sem), expert_counts(count, sem), combine_counts(count, sem)
        with ExitStack() as held:
            ident = held.enter_context(nc.sbuf_tensor("ident", [P, P], F32))
            identb = held.enter_context(nc.sbuf_tensor("identb", [P, P], BF16))
            with nc.sbuf_tensor("near", [P, H, NEAR_W], F32) as near:
                tables_out, tables_in = sem("tables_out"), sem("tables_in")
                with (
                    nc.sbuf_tensor("ediag", [H, DIAG], F32) as ediag,
                    nc.sbuf_tensor("krows16", [KS - ROW_MAX, S], BF16) as krows16,
                    nc.sbuf_tensor("fparts", [H, 3, TB * S], BF16) as fparts,
                ):
                    prepare(nc, a, sc, counts, sem, ident, identb, ediag, krows16, fparts, tables_out)
                    project(nc, a, sc, c1, passed, ident, near, tables_out, tables_in)
                attend(nc, a, sc, c2, passed, ident, identb, near)
            with nc.sbuf_tensor("tiles", [1, 2, 2 * P], I32) as tiles:
                with nc.sbuf_tensor("weights", [P, NE * WE], F32) as weights:
                    route(nc, a, sc, c3, passed, ident, tiles, weights, c4["weights"])
                    experts(nc, a, sc, c4, passed, ident, tiles, weights)
            combine(nc, a, sc, c5, out)


def prepare(nc, a, sc, counts, sem, ident, identb, ediag, krows16, fparts, tables_out):
    loaded, dve, pe, act = (sem("prep_" + n) for n in ("loaded", "dve", "pe", "act"))
    with (
        nc.sbuf_tensor("rel", [H, BUCKETS], F32) as rel,
        nc.sbuf_tensor("relmax", [H, 1], F32) as relmax,
        nc.sbuf_tensor("relT", [BUCKETS, H], F32) as relT,
        nc.sbuf_tensor("oh_diag", [BUCKETS, DIAG], F32) as oh_diag,
        nc.sbuf_tensor("oh_far", [BUCKETS, TB * S], F32) as oh_far,
        nc.sbuf_tensor("krows32", [KS - ROW_MAX, S], F32) as krows32,
        nc.sbuf_tensor("frest", [H, 2, TB * S], F32) as frest,
        nc.psum_tensor("pt", [BUCKETS, H], F32) as pt,
        nc.psum_tensor("pd", [H, 512], F32) as pd,
        nc.psum_tensor("pf", [H, TB * S], F32) as pf,
        nc.Block() as block,
    ):
        @block.sync
        def _(sp):
            for c in counts:
                if c.ahead:
                    sp.sem_inc(c.sem, c.ahead * c.per)
            sp.dma_start(ident[:, :], a["eye"]).then_inc(loaded, 16)
            sp.dma_start(rel[:, :], a["rel_bias"]).then_inc(loaded, 16)
            sp.dma_start(oh_diag[:, :], a["onehot_diag"]).then_inc(loaded, 16)
            sp.dma_start(oh_far[:, :], a["onehot_far"]).then_inc(loaded, 16)
            sp.dma_start(krows32[:, :], a["krows"]).then_inc(loaded, 16)
            sp.wait_ge(act, 1)
            skewed = bass.AP(tensor=sc["diag"].tensor, offset=0, ap=[[P * (DIAG + P), H], [DIAG + P + 1, P], [1, DIAG]])
            sp.dma_start(skewed, ediag[:, :].rearrange("h (o i) -> h o i", o=1).to_broadcast([H, P, DIAG])).then_inc(tables_out, 16)
            sp.wait_ge(dve, 10)
            for p in range(3):
                sp.dma_start(sc["far"][p].rearrange("k h s -> h k s"),
                             fparts[:, p, :].rearrange("h (k s) -> h k s", k=TB)).then_inc(tables_out, 16)
            sp.dma_start(sc["krows"], krows16[:, :]).then_inc(tables_out, 16)

        @block.vector
        def _(v):
            v.wait_ge(loaded, 80)
            v.tensor_copy(identb[:, :], ident[:, :]).then_inc(dve, 1)
            v.reduce_max(relmax[:, :], rel[:, :], X).then_inc(dve, 1)
            v.wait_ge(dve, 2)
            v.tensor_scalar(frest[:, 0, 0:BUCKETS], rel[:, :], relmax[:, 0:1], None, ALU.subtract).then_inc(dve, 1)
            v.wait_ge(pe, 1)
            v.tensor_copy(relT[:, :], pt[:, :]).then_inc(dve, 1)
            v.wait_ge(pe, 2)
            v.tensor_copy(fparts[:, 0, :], pf[:, :]).then_inc(dve, 1)
            v.wait_ge(dve, 5)
            v.tensor_sub(frest[:, 0, :], pf[:, :], fparts[:, 0, :]).then_inc(dve, 1)
            v.wait_ge(dve, 6)
            v.tensor_copy(fparts[:, 1, :], frest[:, 0, :]).then_inc(dve, 1)
            v.wait_ge(dve, 7)
            v.tensor_sub(frest[:, 1, :], frest[:, 0, :], fparts[:, 1, :]).then_inc(dve, 1)
            v.wait_ge(dve, 8)
            v.tensor_copy(fparts[:, 2, :], frest[:, 1, :]).then_inc(dve, 1)
            v.tensor_copy(krows16[:, :], krows32[:, :]).then_inc(dve, 1)

        @block.scalar
        def _(s):
            s.wait_ge(pe, 2)
            s.activation(ediag[:, :], pd[:, 0:DIAG], ACT.Exp).then_inc(act, 1)

        @block.tensor
        def _(t):
            t.wait_ge(dve, 3)
            t.transpose(pt[:, :], frest[:, 0, 0:BUCKETS], ident[0:H, 0:H]).then_inc(pe, 1)
            t.wait_ge(dve, 4)
            t.matmul(pd[:, 0:DIAG], relT[:, :], oh_diag[:, :], start=True, stop=True)
            for k in range(TB):
                last = t.matmul(pf[:, k * S:(k + 1) * S], relT[:, :], oh_far[:, k * S:(k + 1) * S], start=True, stop=True)
            last.then_inc(pe, 1)


def project_counts(count, sem):
    return dict(
        weights=sem("pr_weights"), ones=sem("pr_ones"),
        x_in=[count(f"pr_x_in{u}", 16) for u in range(2)], c_in=[count(f"pr_c_in{u}", 16) for u in range(2)],
        parts_out=[count(f"pr_parts_out{u}", 16) for u in range(2)], v_out=[count(f"pr_v_out{u}", 16) for u in range(2)],
        stats=count("pr_stats", 8), rstd=count("pr_rstd", 2), xn=count("pr_xn", TB),
        tp=count("pr_tp", 2), xnT=count("pr_xnT", 2), mm=count("pr_mm", 4), part1=count("pr_part1", 4),
        rest=count("pr_rest", 4), part2=count("pr_part2", 4), part3=count("pr_part3", 4),
        vmm=count("pr_vmm", 2), v=count("pr_v", 2),
    )


def project(nc, a, sc, c, passed, ident, near, tables_out, tables_in):
    def pair(name, shape, dt=F32):
        return [es.enter_context(nc.sbuf_tensor(f"pr_{name}{u}", shape, dt)) for u in range(2)]

    with ExitStack() as es:
        wq = es.enter_context(nc.sbuf_tensor("wq", [P, EC, E], F32))
        wkv = es.enter_context(nc.sbuf_tensor("wkv", [P, EC, 2 * E], F32))
        half = es.enter_context(nc.sbuf_tensor("half", [P, TB], F32))
        x, xn, xnT, cT = pair("x", [P, TB, E]), pair("xn", [P, TB, E]), pair("xnT", [P, EC, S]), pair("cT", [P, EC, S])
        st, mv, var, rstd = pair("st", [P, TB, 6]), pair("mv", [P, TB, 2]), pair("var", [P, TB]), pair("rstd", [P, TB])
        parts, vt, rest = pair("parts", [P, 4, 3, S], BF16), pair("vt", [P, TB, H, VW]), pair("rest", [P, S])
        tp = [es.enter_context(nc.psum_tensor(f"pr_tp{i}", [P, S], F32)) for i in range(EC)]
        qk = [es.enter_context(nc.psum_tensor(f"pr_qk{i}", [P, S], F32)) for i in range(4)]
        vp = [es.enter_context(nc.psum_tensor(f"pr_vp{i}", [P, 2, E], F32)) for i in range(2)]
        block = es.enter_context(nc.Block())
        x_rows = a["x"].rearrange("(b t p) e -> b p t e", b=B, t=TB)
        cT_cols = a["ctxT"].rearrange("(c p) (b s) -> b p c s", p=P, b=B)
        parts_d = sc["parts"].rearrange("b k (m p) t s -> b p (k m) (t s)", p=P)

        @block.sync
        def _(sp):
            def load_x(n, u):
                sp.dma_start(x[u][:, :, :], x_rows[bass.ds(n, 1)].rearrange("o p t e -> (o p) t e")).then_inc(c["x_in"][u].sem, 16)

            def load_c(n, u):
                sp.dma_start(cT[u][:, :, :], cT_cols[bass.ds(n, 1)].rearrange("o p c s -> (o p) c s")).then_inc(c["c_in"][u].sem, 16)

            def step(n, u, last):
                if not last:
                    sp.wait_ge(c["xn"].sem, c["xn"].value(n))
                    load_x(n + 2, u)
                sp.wait_ge(c["part3"].sem, c["part3"].value(n))
                sp.dma_start(parts_d[bass.ds(n, 1)].rearrange("o p w s -> (o p) w s"),
                             parts[u][:, :, :, :].rearrange("p w t s -> p w (t s)")).then_inc(c["parts_out"][u].sem, 16)
                sp.wait_ge(c["v"].sem, c["v"].value(n))
                sp.dma_start(sc["v"][bass.ds(n, 1)].rearrange("o p k h w -> (o p) (k h w)"),
                             vt[u][:, :, :, :].rearrange("p k h w -> p (k h w)")).then_inc(c["v_out"][u].sem, 16)
                if not last:
                    load_c(n + 2, u)

            load_x(0, 0)
            sp.dma_start(wq[:, :, :], a["wq"].rearrange("(c p) e -> p c e", p=P)).then_inc(c["weights"], 16)
            sp.dma_start(wkv[:, :, :], a["wkv"].rearrange("(c p) e -> p c e", p=P)).then_inc(c["weights"], 16)
            load_c(0, 0)
            load_x(1, 1)
            load_c(1, 1)
            sp.wait_ge(tables_out, 80)
            sp.dma_start(near[:, :, :], sc["diag"][:, :, P - 1:P - 1 + NEAR_W].rearrange("h k j -> k h j")).then_inc(tables_in, 16)
            with sp.Fori(0, B // 2 - 1) as it:
                for u in range(2):
                    step(it * 2 + u, u, False)
            for u in range(2):
                step(B - 2 + u, u, True)
            sp.wait_ge(tables_in, 16)
            for u in range(2):
                sp.wait_ge(c["parts_out"][u].sem, c["parts_out"][u].value(B // 2 - 1))
                sp.wait_ge(c["v_out"][u].sem, c["v_out"][u].value(B // 2 - 1))

        @block.gpsimd
        def _(g):
            for u in range(2):
                g.memset(vt[u][:, :, :, :], 0.0).then_inc(c["ones"], 1)
            g.memset(half[:, :], -0.5).then_inc(c["ones"], 1)
            g.wait_ge(c["ones"], 3)
            for u in range(2):
                g.memset(vt[u][:, :, :, D:D + 1], 1.0).then_inc(c["ones"], 1)

            def body(n, u):
                g.wait_ge(c["stats"].sem, c["stats"].value(n))
                stand_alone(g, passed)
                g.tensor_scalar(var[u][:, :], mv[u][:, :, 1], EPS, None, ALU.add).then_inc(c["rstd"].sem, 1)
                g.wait_ge(c["rstd"].sem, c["rstd"].value(n, 1))
                g.tensor_tensor(rstd[u][:, :], var[u][:, :], half[:, :], ALU.pow).then_inc(c["rstd"].sem, 1)

            with g.Fori(0, B // 2) as it:
                for u in range(2):
                    body(it * 2 + u, u)

        @block.vector
        def _(v):
            def stats(n, u, it):
                v.wait_ge(c["x_in"][u].sem, c["x_in"][u].value(it))
                v.wait_ge(c["rstd"].sem, c["rstd"].value(n - 2))
                v.wait_ge(c["xn"].sem, c["xn"].value(n - 2))
                for t in range(TB):
                    v.bn_stats(st[u][:, t, :], x[u][:, t, :]).then_inc(c["stats"].sem, 1)
                v.wait_ge(c["stats"].sem, c["stats"].value(n, TB))
                stand_alone(v, passed)
                for t in range(TB):
                    v.bn_aggr(mv[u][:, t, :], st[u][:, t, :]).then_inc(c["stats"].sem, 1)

            def normalise(n, u):
                v.wait_ge(c["rstd"].sem, c["rstd"].value(n))
                v.wait_ge(c["tp"].sem, c["tp"].value(n - 2))
                for t in range(TB):
                    v.tensor_scalar(xn[u][:, t, :], x[u][:, t, :], mv[u][:, t, 0:1], rstd[u][:, t:t + 1],
                                    ALU.subtract, ALU.mult).then_inc(c["xn"].sem, 1)

            def split(n, u, it, last):
                v.wait_ge(c["parts_out"][u].sem, c["parts_out"][u].value(it - 1))
                for w in range(4 + 1):
                    if w < 4:
                        v.wait_ge(c["part1"].sem, c["part1"].value(n, w + 1))
                        v.wait_ge(c["part3"].sem, c["part3"].value(n, w - 1))
                        v.tensor_sub(rest[w % 2][:, :], qk[w][:, :], parts[u][:, w, 0, :]).then_inc(c["rest"].sem, 1)
                    if w >= 1:
                        v.wait_ge(c["part2"].sem, c["part2"].value(n, w))
                        v.tensor_sub(parts[u][:, w - 1, 2, :], rest[(w - 1) % 2][:, :], parts[u][:, w - 1, 1, :]).then_inc(c["part3"].sem, 1)
                    if w == 2 and not last:
                        normalise(n + 1, 1 - u)

            v.wait_ge(c["ones"], 5)
            stats(0, 0, 0)
            normalise(0, 0)

            def body(n, u, it, last):
                if not last:
                    stats(n + 1, 1 - u, it + u)
                split(n, u, it, last)

            with v.Fori(0, B // 2 - 1) as it:
                for u in range(2):
                    body(it * 2 + u, u, it, False)
            body(B - 2, 0, B // 2 - 1, False)
            body(B - 1, 1, B // 2 - 1, True)

        @block.scalar
        def _(s):
            def xnT_out(n, u):
                for i in range(EC):
                    s.wait_ge(c["tp"].sem, c["tp"].value(n, i + 1))
                    s.wait_ge(c["mm"].sem, c["mm"].value(n - 2, 2))
                    s.copy(xnT[u][:, i, :], tp[i][:, :]).then_inc(c["xnT"].sem, 1)

            def body(n, u, it, last):
                s.wait_ge(c["parts_out"][u].sem, c["parts_out"][u].value(it - 1))
                for w in range(4 + 1):
                    if w < 4:
                        s.wait_ge(c["mm"].sem, c["mm"].value(n, w + 1))
                        s.copy(parts[u][:, w, 0, :], qk[w][:, :]).then_inc(c["part1"].sem, 1)
                    if w >= 1:
                        s.wait_ge(c["rest"].sem, c["rest"].value(n, w))
                        s.copy(parts[u][:, w - 1, 1, :], rest[(w - 1) % 2][:, :]).then_inc(c["part2"].sem, 1)
                s.wait_ge(c["v_out"][u].sem, c["v_out"][u].value(it - 1))
                for i in range(2):
                    s.wait_ge(c["vmm"].sem, c["vmm"].value(n, i + 1))
                    s.copy(vt[u][:, 2 * i:2 * i + 2, :, 0:D],
                           vp[i][:, :, :].rearrange("p k (h d) -> p k h d", h=H)).then_inc(c["v"].sem, 1)
                if not last:
                    xnT_out(n + 1, 1 - u)

            s.wait_ge(c["ones"], 5)
            xnT_out(0, 0)
            with s.Fori(0, B // 2 - 1) as it:
                for u in range(2):
                    body(it * 2 + u, u, it, False)
            body(B - 2, 0, B // 2 - 1, False)
            body(B - 1, 1, B // 2 - 1, True)

        @block.tensor
        def _(t_):
            def transposes(n, u):
                for i in range(EC):
                    t_.wait_ge(c["xn"].sem, c["xn"].value(n))
                    t_.wait_ge(c["xnT"].sem, c["xnT"].value(n - 1, i + 1))
                    for t in range(TB):
                        last = t_.transpose(tp[i][:, t * P:(t + 1) * P], xn[u][:, t, i * P:(i + 1) * P], ident[:, :])
                    last.then_inc(c["tp"].sem, 1)

            def body(n, u, it, last):
                for w in range(4):
                    m = w % 2
                    if w == 0:
                        t_.wait_ge(c["xnT"].sem, c["xnT"].value(n))
                    if w == 2:
                        t_.wait_ge(c["c_in"][u].sem, c["c_in"][u].value(it))
                    t_.wait_ge(c["rest"].sem, c["rest"].value(n - 1, w + 1))
                    for i in range(EC):
                        lhsT = wq[:, i, m * P:(m + 1) * P] if w < 2 else wkv[:, i, m * P:(m + 1) * P]
                        rhs = xnT[u][:, i, :] if w < 2 else cT[u][:, i, :]
                        mm = t_.matmul(qk[w][:, :], lhsT, rhs, start=(i == 0), stop=(i == EC - 1))
                    mm.then_inc(c["mm"].sem, 1)
                for k2 in range(2):
                    t_.wait_ge(c["v"].sem, c["v"].value(n - 1, k2 + 1))
                    for k in range(2):
                        kb = 2 * k2 + k
                        for i in range(EC):
                            mm = t_.matmul(vp[k2][:, k, :], cT[u][:, i, kb * P:(kb + 1) * P], wkv[:, i, E:2 * E],
                                           start=(i == 0), stop=(i == EC - 1))
                    mm.then_inc(c["vmm"].sem, 1)
                if not last:
                    transposes(n + 1, 1 - u)

            t_.wait_ge(c["weights"], 32)
            transposes(0, 0)
            with t_.Fori(0, B // 2 - 1) as it:
                for u in range(2):
                    body(it * 2 + u, u, it, False)
            body(B - 2, 0, B // 2 - 1, False)
            body(B - 1, 1, B // 2 - 1, True)


def attend_counts(count, sem):
    return dict(
        once=sem("at_once"), rows=sem("at_rows"),
        stack=[count(f"at_stack{i}", 16 * 2 * len(TERMS)) for i in range(2)], res=count("at_res", 16),
        nm_out=[count(f"at_nm_out{i}", 16) for i in range(2)], nm_in=[count(f"at_nm_in{i}", 16) for i in range(2)], x1_out=count("at_x1_out", 16),
        v_in=[count(f"at_v_in{g}", 16) for g in range(4)],
        s=count("at_s", NS), mx=count("at_mx", NS, 3), nm=count("at_nm", 10), nmp=count("at_nmp", 2), nmT=count("at_nmT", 2),
        st=count("at_st", 2 * CH), ex=count("at_ex", 2 * CH), mul=count("at_mul", CH), pv=count("at_pv", CH // 2),
        o=count("at_o", 4), op=count("at_op", 4), rc=count("at_rc", 4), on=count("at_on", 4),
        onp=count("at_onp", EC), onT=count("at_onT", EC), wo=count("at_wo", 2), x1=count("at_x1", 2),
    )


NH2 = NS // 2


def score_tiles(k, first):
    if not first:
        return [(1, 2 * k), (1, 2 * k + 1)]
    if k < CH // 4:
        return [(0, NH2 + 4 * k + i) for i in range(4)]
    if k < CH // 2:
        return [(1, 4 * (k - CH // 4) + i) for i in range(4)]
    return [(1, 2 * k), (1, 2 * k + 1)]


AT_MAX, AT_MAX_BACK = CH // 2 - 1, CH // 2 + 1


def second_half_at(first):
    return (CH // 4, CH // 4 + 1, CH // 4 + 2) if first else (0, 2, 3)


AT_O_LAST, AT_ON0, AT_ON1, AT_WO0, AT_WO1 = 4, 6, 8, 10, 11
AT_O = [12, 20, 28]


def near_range(kb):
    lo, hi = kb * P + NEAR_LO, kb * P + NEAR_LO + NEAR_W
    return max(lo, 0), min(hi, S), max(lo, 0) - lo


def attend(nc, a, sc, c, passed, ident, identb, near):
    with ExitStack() as es:
        def sb(name, shape, dt=F32):
            return es.enter_context(nc.sbuf_tensor("at_" + name, shape, dt))

        def ps(name, shape, dt=F32):
            return es.enter_context(nc.psum_tensor("at_" + name, shape, dt))

        qs, ks = sb("qs", [P, 2, H, S], BF16), sb("ks", [P, 2, H, S], BF16)
        wo = sb("wo", [P, EC, E])
        vt = sb("vt", [P, TB, H, VW])
        pr = [sb(f"pr{i}", [P, 2, S]) for i in range(4)]
        o_sb = [sb(f"o{i}", [P, S]) for i in range(2)]
        rc = sb("rc", [P, TB, 4])
        on = sb("on", [P, TB, E])
        onT = sb("onT", [P, EC, S])
        res, x1 = sb("res", [P, TB, E]), sb("x1", [P, TB, E])
        nm, nmr, nmb, nmT = sb("nm", [P, NS]), sb("nmr", [P, 2, NS]), sb("nmb", [P, 3, NS], BF16), sb("nmT", [NH2, 2, 3, P], BF16)
        sp_ = [ps(f"s{i}", [P, S]) for i in range(3)]
        st_ = [ps(f"st{i}", [P, S]) for i in range(3)]
        op = ps("o", [P, S])
        mp = ps("m", [P, TB, P])
        mpb = mp[:, :, :].rearrange("p a b -> p (a b)").bitcast(BF16)
        block = es.enter_context(nc.Block())
        x_rows = a["x"].rearrange("(b t p) e -> b p t e", b=B, t=TB)

        @block.sync
        def _(sp):
            def rows(u):
                sp.dma_start(ks[ROW_MAX:KS, u, :, :], sc["krows"].rearrange("r (o s) -> r o s", o=1).to_broadcast([KS - ROW_MAX, H, S])).then_inc(c["rows"], 16)
                sp.dma_start(qs[ROW_FAR:KS, u, :, :], sc["far"].rearrange("p k h s -> (p k) h s")).then_inc(c["rows"], 16)

            def stacks(n, odd, half):
                heads = slice(H // 2 * half, H // 2 * (half + 1))
                for i, (qi, ki) in enumerate(TERMS):
                    for k, dst, part in ((0, qs, qi), (1, ks, ki)):
                        src = sc["parts"][bass.ds(n, 1), k, heads.start * D:heads.stop * D, part, :].rearrange("o (h d) s -> (o d) h s", d=D)
                        sp.dma_start(dst[i * D:(i + 1) * D, odd, heads, :], src).then_inc(c["stack"][half].sem, 16)

            def maxima(n, odd, i):
                sp.wait_ge(c["nmT"].sem, c["nmT"].value(n, i + 1))
                sp.dma_start(sc["negmax"][bass.ds(n, 1), :, NH2 * i:NH2 * (i + 1)].rearrange("o t c q -> (o c) t q"),
                             nmT[:, i, :, :]).then_inc(c["nm_out"][i].sem, 16)
                sp.wait_ge(c["nm_out"][i].sem, c["nm_out"][i].value(n))
                sp.dma_start(qs[ROW_MAX:ROW_FAR, odd, H // 2 * i:H // 2 * (i + 1), :].rearrange("t h s -> t (h s)"),
                             sc["negmax"][bass.ds(n, 1), :, NH2 * i:NH2 * (i + 1)].rearrange("o t c q -> (o t) (c q)")).then_inc(c["nm_in"][i].sem, 16)

            def v_group(n, g):
                sp.dma_start(vt[:, :, 4 * g:4 * g + 4, :].rearrange("p k h w -> p k (h w)"),
                             sc["v"][bass.ds(n, 1), :, :, 4 * g:4 * g + 4, :].rearrange("o p k h w -> (o p) k (h w)")).then_inc(c["v_in"][g].sem, 16)

            def store(n):
                sp.wait_ge(c["x1"].sem, c["x1"].value(n))
                sp.dma_start(sc["x1"][bass.ds(n, 1)].rearrange("o p t e -> (o p) t e"), x1[:, :, :]).then_inc(c["x1_out"].sem, 16)

            def residual(n):
                sp.wait_ge(c["x1"].sem, c["x1"].value(n - 1))
                sp.dma_start(res[:, :, :], x_rows[bass.ds(n, 1)].rearrange("o p t e -> (o p) t e")).then_inc(c["res"].sem, 16)

            def batch(n, odd, first, last, before_last=False):
                maxima(n, odd, 1)
                if not last:
                    sp.wait_ge(c["st"].sem, c["st"].value(n - 1))
                    stacks(n + 1, 1 - odd, 1)
                if not first:
                    store(n - 1)
                residual(n)
                if not last:
                    for g in range(4):
                        sp.wait_ge(c["pv"].sem, c["pv"].value(n, 4 * g + 4))
                        v_group(n + 1, g)
                        if g == 2:
                            maxima(n + 1, 1 - odd, 0)
                        if g == 1 and not before_last:
                            sp.wait_ge(c["st"].sem, c["st"].value(n, CH))
                            stacks(n + 2, odd, 0)

            stacks(0, 0, 0)
            stacks(0, 0, 1)
            rows(0)
            sp.dma_start(wo[:, :, :], a["wo"].rearrange("(c p) e -> p c e", p=P)).then_inc(c["once"], 16)
            for g in range(4):
                v_group(0, g)
            rows(1)
            maxima(0, 0, 0)
            stacks(1, 1, 0)
            batch(0, 0, True, False)
            with sp.Fori(0, B // 2 - 2) as it:
                for u in range(2):
                    batch(it * 2 + (1 + u), 1 - u, False, False)
            batch(B - 3, 1, False, False)
            batch(B - 2, 0, False, False, True)
            batch(B - 1, 1, False, True)
            store(B - 1)
            sp.wait_ge(c["x1_out"].sem, c["x1_out"].value(B - 1))

        @block.vector
        def _(v):
            def row_max(n, j):
                v.wait_ge(c["s"].sem, c["s"].value(n, j + 1))
                if j == 0:
                    v.wait_ge(c["nm"].sem, c["nm"].value(n - 1))
                v.reduce_max(nm[:, j:j + 1], sp_[j % 3][:, :], X, negate=True).then_inc(c["mx"].sem, 1)

            def split_max(n, i):
                k, at = c["nm"], slice(NH2 * i, NH2 * (i + 1))
                v.wait_ge(c["mx"].sem, c["mx"].value(n, NH2 * (i + 1)))
                v.wait_ge(c["nmp"].sem, c["nmp"].value(n - 1, i + 1))
                v.tensor_copy(nmb[:, 0, at], nm[:, at]).then_inc(k.sem, 1)
                v.wait_ge(k.sem, k.value(n, 5 * i + 1))
                v.tensor_sub(nmr[:, 0, at], nm[:, at], nmb[:, 0, at]).then_inc(k.sem, 1)
                v.wait_ge(k.sem, k.value(n, 5 * i + 2))
                v.tensor_copy(nmb[:, 1, at], nmr[:, 0, at]).then_inc(k.sem, 1)
                v.wait_ge(k.sem, k.value(n, 5 * i + 3))
                v.tensor_sub(nmr[:, 1, at], nmr[:, 0, at], nmb[:, 1, at]).then_inc(k.sem, 1)
                v.wait_ge(k.sem, k.value(n, 5 * i + 4))
                v.tensor_copy(nmb[:, 2, at], nmr[:, 1, at]).then_inc(k.sem, 1)

            def normalise(n, g):
                v.wait_ge(c["op"].sem, c["op"].value(n, g + 1))
                heads = mp[:, :, :].rearrange("p t (h w) -> p t h w", w=VW)
                v.wait_ge(c["on"].sem, c["on"].value(n, g))
                v.reciprocal(rc[:, :, :], heads[:, :, :, D]).then_inc(c["rc"].sem, 1)
                v.wait_ge(c["rc"].sem, c["rc"].value(n, g + 1))
                v.wait_ge(c["onp"].sem, c["onp"].value(n - 1))
                v.tensor_tensor(on[:, :, 4 * g * D:4 * (g + 1) * D].rearrange("p t (h d) -> p t h d", d=D), heads[:, :, :, 0:D],
                                rc[:, :, :].rearrange("p t (h o) -> p t h o", o=1).to_broadcast([P, TB, 4, D]), ALU.mult).then_inc(c["on"].sem, 1)

            def add_residual(n, i):
                v.wait_ge(c["wo"].sem, c["wo"].value(n, i + 1))
                if i == 0:
                    v.wait_ge(c["res"].sem, c["res"].value(n))
                    v.wait_ge(c["x1_out"].sem, c["x1_out"].value(n - 1))
                v.tensor_add(x1[:, 2 * i:2 * i + 2, :], mp[:, :, :].rearrange("p a b -> p (a b)").rearrange("p (t e) -> p t e", e=E),
                             res[:, 2 * i:2 * i + 2, :]).then_inc(c["x1"].sem, 1)

            def batch(n, first, last):
                for k in range(CH):
                    if k == second_half_at(first)[0]:
                        split_max(n, 1)
                    if not last:
                        for ahead, j in score_tiles(k, first):
                            row_max(n + ahead, j)
                        if k == AT_MAX:
                            split_max(n + 1, 0)
                    if not first and k == AT_O_LAST + 1:
                        normalise(n - 1, 3)
                    if not first and k in (AT_WO0, AT_WO1):
                        add_residual(n - 1, (AT_WO0, AT_WO1).index(k))
                    if k - 1 in AT_O:
                        normalise(n, AT_O.index(k - 1))

            for j in range(NH2):
                row_max(0, j)
            split_max(0, 0)
            batch(0, True, False)
            with v.Fori(1, B - 1) as n:
                batch(n, False, False)
            batch(B - 1, False, True)
            normalise(B - 1, 3)
            for i in range(2):
                add_residual(B - 1, i)

        @block.scalar
        def _(s):
            def exp(n, k):
                s.wait_ge(c["pv"].sem, c["pv"].value(n, (k - 4) // 2 + 1))
                for j in range(2):
                    m = 2 * k + j
                    s.wait_ge(c["st"].sem, c["st"].value(n, m + 1))
                    s.activation(pr[k % 4][:, j, :], st_[m % 3][:, :], ACT.Exp).then_inc(c["ex"].sem, 1)

            def o_out(n, g):
                s.wait_ge(c["pv"].sem, c["pv"].value(n, 4 * g + 4))
                s.wait_ge(c["op"].sem, c["op"].value(n, g - 1))
                s.copy(o_sb[g % 2][:, :], op[:, :]).then_inc(c["o"].sem, 1)

            def onT_out(n, i):
                s.wait_ge(c["onp"].sem, c["onp"].value(n, i + 1))
                s.wait_ge(c["wo"].sem, c["wo"].value(n - 1))
                s.copy(onT[:, i, :], mp[:, :, :].rearrange("p a b -> p (a b)")).then_inc(c["onT"].sem, 1)

            def nmT_out(n, i):
                s.wait_ge(c["nmp"].sem, c["nmp"].value(n, i + 1))
                s.wait_ge(c["nm_out"][i].sem, c["nm_out"][i].value(n - 1))
                s.copy(nmT[:, i, :, :].rearrange("c t q -> c (t q)"), mpb[0:NH2, 0:3 * P]).then_inc(c["nmT"].sem, 1)

            def batch(n, first, last):
                for k in range(CH):
                    if not first and k == 2:
                        o_out(n - 1, 3)
                    if not first and k in (AT_ON0 + 1, AT_ON1 + 1):
                        onT_out(n - 1, (AT_ON0 + 1, AT_ON1 + 1).index(k))
                    if k in (10, 18, 26):
                        o_out(n, (10, 18, 26).index(k))
                    if k == second_half_at(first)[2]:
                        nmT_out(n, 1)
                    if not last and k == AT_MAX_BACK + 1:
                        nmT_out(n + 1, 0)
                    exp(n, k)

            nmT_out(0, 0)
            batch(0, True, False)
            with s.Fori(1, B - 1) as n:
                batch(n, False, False)
            batch(B - 1, False, True)
            o_out(B - 1, 3)
            for i in range(EC):
                onT_out(B - 1, i)

        @block.gpsimd
        def _(g_):
            def batch(n):
                for k in range(CH):
                    g, kb, two = k // 8, k // 2 % TB, k % 2
                    lo, hi, at = near_range(kb)
                    h = 4 * g + 2 * two
                    g_.wait_ge(c["ex"].sem, c["ex"].value(n, 2 * k + 2))
                    g_.tensor_tensor(pr[k % 4][:, :, lo:hi], pr[k % 4][:, :, lo:hi], near[:, h:h + 2, at:at + hi - lo],
                                     ALU.mult).then_inc(c["mul"].sem, 1)

            with g_.Fori(0, B) as n:
                batch(n)

        @block.tensor
        def _(t):
            def scores(n, odd, j):
                h, qb = j // TB, j % TB
                if j == 0 or j >= 3:
                    t.wait_ge(c["mx"].sem, c["mx"].value(n, max(j - 2, 0)))
                if j in (0, NH2):
                    stack = c["stack"][j // NH2]
                    t.wait_ge(stack.sem, stack.value(n))
                t.matmul(sp_[j % 3][:, :], qs[0:KQ, odd, h, qb * P:(qb + 1) * P], ks[0:KQ, odd, h, :], start=True, stop=True).then_inc(c["s"].sem, 1)

            def chunk(n, odd, k, between):
                g, kb, two = k // 8, k // 2 % TB, k % 2
                if k in (0, CH // 2):
                    nm_in = c["nm_in"][k // (CH // 2)]
                    t.wait_ge(nm_in.sem, nm_in.value(n))
                for j in range(2):
                    h = 4 * g + 2 * two + j
                    if j:
                        between()
                    m = 2 * k + j
                    if m == 0 or m >= 3:
                        t.wait_ge(c["ex"].sem, c["ex"].value(n, max(m - 2, 0)))
                    t.matmul(st_[m % 3][:, :], ks[0:KS, odd, h, kb * P:(kb + 1) * P], qs[0:KS, odd, h, :],
                             start=True, stop=True).then_inc(c["st"].sem, 1)

            def values(n, i):
                g, kb = i // TB, i % TB
                t.wait_ge(c["mul"].sem, c["mul"].value(n, 2 * i + 2))
                if kb == 0:
                    t.wait_ge(c["v_in"][g].sem, c["v_in"][g].value(n))
                    t.wait_ge(c["o"].sem, c["o"].value(n, g))
                for hh in range(4):
                    k = 2 * i + hh // 2
                    last = t.matmul(op[32 * hh:32 * hh + VW, :], vt[:, kb, 4 * g + hh, :], pr[k % 4][:, hh % 2, :],
                                    start=(kb == 0), stop=(kb == TB - 1))
                last.then_inc(c["pv"].sem, 1)

            def o_back(n, g, misc_free):
                t.wait_ge(c["o"].sem, c["o"].value(n, g + 1))
                misc_free()
                for q in range(TB):
                    last = t.transpose(mp[:, q, :], o_sb[g % 2][:, q * P:(q + 1) * P], ident[:, :])
                last.then_inc(c["op"].sem, 1)

            def on_back(n, i):
                if i == 0:
                    t.wait_ge(c["on"].sem, c["on"].value(n))
                else:
                    t.wait_ge(c["onT"].sem, c["onT"].value(n, 1))
                for q in range(TB):
                    last = t.transpose(mp[:, q, :], on[:, q, i * P:(i + 1) * P], ident[:, :])
                last.then_inc(c["onp"].sem, 1)

            def project_out(n, i):
                if i == 0:
                    t.wait_ge(c["onT"].sem, c["onT"].value(n))
                else:
                    t.wait_ge(c["x1"].sem, c["x1"].value(n, 1))
                out = mp[:, :, :].rearrange("p a b -> p (a b)")
                for q in range(2):
                    for i2 in range(EC):
                        last = t.matmul(out[:, q * E:(q + 1) * E], onT[:, i2, (2 * i + q) * P:(2 * i + q + 1) * P], wo[:, i2, :],
                                        start=(i2 == 0), stop=(i2 == EC - 1))
                last.then_inc(c["wo"].sem, 1)

            def maxima_back(n, i, misc_free):
                t.wait_ge(c["nm"].sem, c["nm"].value(n, 5 * (i + 1)))
                misc_free()
                stand_alone(t, passed)
                for p in range(3):
                    last = t.transpose(mpb[0:NH2, p * P:(p + 1) * P], nmb[:, p, NH2 * i:NH2 * (i + 1)], identb[:, :])
                last.then_inc(c["nmp"].sem, 1)

            def batch(n, odd, first, last):
                for k in range(CH):
                    todo = [] if last else score_tiles(k, first)

                    def one():
                        if todo:
                            ahead, j = todo.pop(0)
                            scores(n + ahead, (odd + ahead) % 2, j)

                    chunk(n, odd, k, one)
                    one()
                    if k == 1 and not first:
                        values(n - 1, CH // 2 - 1)
                    if k % 2 and k >= 3:
                        values(n, (k - 3) // 2)
                    while todo:
                        one()
                    if k == second_half_at(first)[1]:
                        maxima_back(n, 1, lambda: t.wait_ge(c["nmT"].sem, c["nmT"].value(n, 1)) if first else
                                    t.wait_ge(c["on"].sem, c["on"].value(n - 1, 3)))
                    if not first:
                        if k == AT_O_LAST:
                            o_back(n - 1, 3, lambda: (t.wait_ge(c["nmT"].sem, c["nmT"].value(n)),
                                                      t.wait_ge(c["on"].sem, c["on"].value(n - 1, 3))))
                        if k in (AT_ON0, AT_ON1):
                            on_back(n - 1, (AT_ON0, AT_ON1).index(k))
                        if k in (AT_WO0, AT_WO1):
                            project_out(n - 1, (AT_WO0, AT_WO1).index(k))
                    if k == AT_MAX_BACK and not last:
                        maxima_back(n + 1, 0, lambda: t.wait_ge(c["on"].sem, c["on"].value(n, 1)))
                    if k in AT_O:
                        g = AT_O.index(k)

                        def read():
                            if g == 0 and first:
                                t.wait_ge(c["nmT"].sem, c["nmT"].value(n))
                            elif g == 0:
                                t.wait_ge(c["x1"].sem, c["x1"].value(n - 1))
                            elif g == 1 and not last:
                                t.wait_ge(c["nmT"].sem, c["nmT"].value(n + 1, 1))
                            else:
                                t.wait_ge(c["on"].sem, c["on"].value(n, g))

                        o_back(n, g, read)

            for j in range(NH2):
                scores(0, 0, j)
            t.wait_ge(c["once"], 16)
            t.wait_ge(c["rows"], 64)
            maxima_back(0, 0, lambda: None)
            batch(0, 0, True, False)
            with t.Fori(0, B // 2 - 1) as it:
                for u in range(2):
                    batch(it * 2 + (1 + u), 1 - u, False, False)
            batch(B - 1, 1, False, True)
            values(B - 1, CH // 2 - 1)
            o_back(B - 1, 3, lambda: t.wait_ge(c["on"].sem, c["on"].value(B - 1, 3)))
            for i in range(EC):
                on_back(B - 1, i)
            for i in range(2):
                project_out(B - 1, i)


def route_counts(count, sem):
    return dict(
        once=sem("rt_once"), init=sem("rt_init"), end=sem("rt_end"), pads=sem("rt_pads"), padrow=sem("rt_padrow"),
        tab=sem("rt_tab"), tiles=sem("rt_tiles"), dummy=sem("rt_dummy"),
        x_in=[count(f"rt_x_in{u}", 16) for u in range(2)], base_in=[count(f"rt_base_in{u}", 16) for u in range(2)], base_out=[count(f"rt_base_out{u}", 16) for u in range(2)],
        scat=[count(f"rt_scat{u}", 16 * TB * TOPK, 0) for u in range(2)],
        stats=count("rt_stats", 8), rstd=count("rt_rstd", 2), xn=count("rt_xn", TB), tp=count("rt_tp", 2),
        xT=count("rt_xT", 2), lg=count("rt_lg"), ex=count("rt_ex"), r=count("rt_r", R_STEPS),
        cnt=count("rt_cnt"), up=count("rt_up", TB), silu=count("rt_silu", TB), h=count("rt_h", TB),
        ht=count("rt_ht", TB), hT=count("rt_hT", TB), dn=count("rt_dn", TB), base=count("rt_base", TB), rows=count("rt_rows", TB),
    )


R_STEPS = 46


def route(nc, a, sc, c, passed, ident, tiles, weights, weights_in):
    with ExitStack() as es:
        def sb(name, shape, dt=F32):
            return es.enter_context(nc.sbuf_tensor("rt_" + name, shape, dt))

        def pair(name, shape, dt=F32):
            return [sb(f"{name}{u}", shape, dt) for u in range(2)]

        def ps(name, shape, dt=F32):
            return es.enter_context(nc.psum_tensor("rt_" + name, shape, dt))

        gate, wsh, wsd = sb("gate", [P, EC, NE]), sb("wsh", [P, EC, 2 * SI]), sb("wsd", [P, SI // P, E])
        ebias, earlier, regions = sb("ebias", [P, NE]), sb("earlier", [P, NG, NG]), sb("regions", [P, NE])
        before, ones = sb("before", [P, P], BF16), sb("ones", [P, P], BF16)
        before32, half = sb("before32", [P, P]), sb("half", [P, TB])
        x, xn, rows, xT = pair("x", [P, TB, E]), pair("xn", [P, TB, E]), pair("rows", [P, TB, TOPK, ROWW]), pair("xT", [P, EC, S])
        st, mv, var, rstd = pair("st", [P, TB, 6]), pair("mv", [P, TB, 2]), pair("var", [P, TB]), pair("rstd", [P, TB])
        base = pair("base", [P, TB, E])
        slots = pair("slots", [P, TB, TOPK], U32)
        ex, sig, sfc = sb("ex", [P, TB, NE]), sb("sig", [P, TB, NE]), sb("sfc", [P, TB, NE])
        gmax, gcmp, geq, rank = sb("gmax", [P, TB, NG]), sb("gcmp", [P, TB, NG, NG]), sb("geq", [P, TB, NG, NG]), sb("rank", [P, TB, NG])
        cand, left, top = sb("cand", [P, TB, NE + 8]), sb("left", [P, TB, NE + 8]), sb("top", [P, TB, 8])
        sel, selb, wgt = sb("sel", [P, TB, NE]), sb("selb", [P, TB, NE], BF16), sb("wgt", [P, TB, NE])
        wsum, winv = sb("wsum", [P, TB]), sb("winv", [P, TB])
        cnt, key, ktop = sb("cnt", [P, TB + 1, NE]), sb("key", [P, TB, NE]), sb("ktop", [P, TB, 8])
        hit, dst = sb("hit", [P, TB, TOPK, NE]), sb("dst", [P, TB, TOPK], I32)
        sg, h, hT = pair("sg", [P, SI]), pair("h", [P, SI]), pair("hT", [P, SI // P, P])
        padrow, padidx = sb("padrow", [P, ROWW]), sb("padidx", [P, NE], I32)
        ends, starts, ntile = sb("ends", [P, NE]), sb("starts", [P, NE]), sb("ntile", [P, NE])
        nti, zero = sb("nti", [P, NE], I32), sb("zero", [P, NE])
        index, ind, ind2 = sb("index", [P, 2]), sb("ind", [P, 2, NE]), sb("ind2", [P, 2, NE])
        num, start, tab_i = sb("num", [P, 2]), sb("start", [P, 2]), sb("tab_i", [P, 2, 2], I32)
        tp = [ps(f"tp{i}", [P, S]) for i in range(EC)]
        lp = ps("l", [P, 4, TB, NE])
        up = [ps(f"up{i}", [P, 2, SI]) for i in range(2)]
        hp = ps("h", [P, 2 * SI // P, P])
        dp = [ps(f"d{i}", [P, 2 * E]) for i in range(2)]
        block = es.enter_context(nc.Block())

        def loop(eng, body):
            for u in range(2):
                body(u, u, 0, u == 0, False)
            with eng.Fori(1, B // 2 - 1) as it:
                for u in range(2):
                    body(it * 2 + u, u, it, False, False)
            for u in range(2):
                body(B - 2 + u, u, B // 2 - 1, False, True)

        def pad(eng, experts):
            with eng.Fori(experts.start // 4, experts.stop // 4) as e4:
                for e in range(4):
                    at = eng.value_load(padidx[0:1, bass.ds(e4 * 4 + e, 1)], min_val=0, max_val=PADS - P)
                    eng.dma_start(sc["slots"][bass.ds(at, P), :], padrow[:, :]).then_inc(c["pads"], 16)

        @block.sync
        def _(sp):
            def load(n, u):
                sp.dma_start(x[u][:, :, :], sc["x1"][bass.ds(n, 1)].rearrange("o p t e -> (o p) t e")).then_inc(c["x_in"][u].sem, 16)

            load(0, 0)
            for dst_, src in ((gate, a["gateT"].rearrange("(c p) e -> p c e", p=P)), (wsh, a["shared"]), (wsd, a["shared_dn"]),
                              (ebias, a["ebias"].to_broadcast([P, NE])), (earlier, a["earlier"].rearrange("p (i j) -> p i j", j=NG)),
                              (regions, a["regions"]), (before32, a["before"])):
                sp.dma_start(dst_[tuple(slice(None) for _ in dst_.shape)], src).then_inc(c["once"], 16)

            def load_base(n, u):
                sp.dma_start(base[u][:, :, :], sc["x1"][bass.ds(n, 1)].rearrange("o p t e -> (o p) t e")).then_inc(c["base_in"][u].sem, 16)

            def store_base(n, u, it):
                sp.wait_ge(c["base"].sem, c["base"].value(n))
                sp.dma_start(sc["base"][bass.ds(n, 1)].rearrange("o p t e -> (o p) t e"), base[u][:, :, :]).then_inc(c["base_out"][u].sem, 16)

            def body(n, u, it, first, last):
                if not last:
                    sp.wait_ge(c["xn"].sem, c["xn"].value(n))
                    load(n + 2, u)
                if not first:
                    store_base(n - 1, 1 - u, it + u - 1)
                    sp.wait_ge(c["base_out"][1 - u].sem, c["base_out"][1 - u].value(it + u - 1))
                    if not (last and u):
                        load_base(n + 1, 1 - u)
                part = bass.ds(n * (NE // B * WE), NE // B * WE)
                sp.dma_start(weights[:, part], a["experts"][:, part]).then_inc(weights_in, 16)

            load(1, 1)
            for u in range(2):
                load_base(u, u)
            loop(sp, body)
            sp.wait_ge(c["end"], T_LAST)
            sp.dma_start(sc["tiletab"].rearrange("w p c -> p w c"), tab_i[:, :, :]).then_inc(c["tab"], 16)
            sp.wait_ge(c["padrow"], 1)
            sp.dma_start(sc["slots"][PADS:PADS + P, :], padrow[:, :]).then_inc(c["dummy"], 16)
            pad(sp, range(NE * 3 // 8, NE))
            sp.wait_ge(c["tab"], 16)
            sp.dma_start(tiles[:, :, :], sc["tiletab"].rearrange("w p c -> (w p c)").rearrange("(o w i) -> o w i", o=1, w=2)).then_inc(c["tiles"], 16)
            store_base(B - 1, 1, B // 2 - 1)
            for u in range(2):
                sp.wait_ge(c["base_out"][u].sem, c["base_out"][u].value(B // 2 - 1))
            sp.wait_ge(c["tiles"], 16)
            sp.wait_ge(c["dummy"], 16)
            sp.wait_ge(c["pads"], 16 * NE)

        @block.gpsimd
        def _(g):
            init = c["init"]
            g.memset(half[:, :], -0.5).then_inc(init, 1)
            g.memset(ones[:, :], 1.0).then_inc(init, 1)
            g.memset(cand[:, :, :], SENT).then_inc(init, 1)
            g.memset(cnt[:, :, :], 0.0).then_inc(init, 1)
            g.memset(zero[:, :], 0.0).then_inc(init, 1)
            for u in range(2):
                g.memset(rows[u][:, :, :, E + 2:ROWW], 0.0).then_inc(init, 1)
            g.memset(padrow[:, :], 0.0).then_inc(init, 1)
            g.iota(dst[:, :, :], [[P * TOPK, TB], [1, TOPK]], base=0, channel_multiplier=TOPK).then_inc(init, 1)
            g.iota(index[:, :], [[1, 2]], base=0, channel_multiplier=2, allow_small_or_imprecise_dtypes=True).then_inc(init, 1)
            g.wait_ge(init, 10)
            g.memset(padrow[:, E + 1:E + 2].bitcast(I32), 1 << 20).then_inc(c["padrow"], 1)

            def norm(n, u):
                g.wait_ge(c["stats"].sem, c["stats"].value(n))
                stand_alone(g, passed)
                g.tensor_scalar(var[u][:, :], mv[u][:, :, 1], EPS, None, ALU.add).then_inc(c["rstd"].sem, 1)
                g.wait_ge(c["rstd"].sem, c["rstd"].value(n, 1))
                g.tensor_tensor(rstd[u][:, :], var[u][:, :], half[:, :], ALU.pow).then_inc(c["rstd"].sem, 1)

            def body(n, u, it, first, last):
                g.wait_ge(c["r"].sem, c["r"].value(n))
                g.wait_ge(c["rows"].sem, c["rows"].value(n))
                stand_alone(g, passed)
                for t in range(TB):
                    for j in range(TOPK):
                        g.indirect_dma_start(sc["slots"], bass.IndirectOffsetOnAxis(ap=slots[u][:, t, j:j + 1], axis=0),
                                             rows[u][:, t, j, :], None).then_inc(c["scat"][u].sem, 16)
                    if t == 0 and not last:
                        norm(n + 2, u)

            norm(0, 0)
            norm(1, 1)
            loop(g, body)
            for u in range(2):
                g.wait_ge(c["scat"][u].sem, c["scat"][u].value(B // 2 - 1))

        @block.vector
        def _(v):
            def scattered(u, it):
                if not isinstance(it, int) or it:
                    v.wait_ge(c["scat"][u].sem, c["scat"][u].value(it - 1))

            def stats(n, u, it):
                v.wait_ge(c["x_in"][u].sem, c["x_in"][u].value(it))
                v.wait_ge(c["xn"].sem, c["xn"].value(n - 2))
                for t in range(TB):
                    v.bn_stats(st[u][:, t, :], x[u][:, t, :]).then_inc(c["stats"].sem, 1)
                v.wait_ge(c["stats"].sem, c["stats"].value(n, TB))
                stand_alone(v, passed)
                for t in range(TB):
                    v.bn_aggr(mv[u][:, t, :], st[u][:, t, :]).then_inc(c["stats"].sem, 1)

            def normalise(n, u):
                v.wait_ge(c["rstd"].sem, c["rstd"].value(n))
                v.wait_ge(c["rows"].sem, c["rows"].value(n - 2))
                v.wait_ge(c["tp"].sem, c["tp"].value(n - 2))
                for t in range(TB):
                    v.tensor_scalar(xn[u][:, t, :], x[u][:, t, :], mv[u][:, t, 0:1],
                                    rstd[u][:, t:t + 1], ALU.subtract, ALU.mult).then_inc(c["xn"].sem, 1)

            def gate_hidden(n, t):
                v.wait_ge(c["silu"].sem, c["silu"].value(n, t + 1))
                v.wait_ge(c["ht"].sem, c["ht"].value(n, t - 1))
                v.tensor_tensor(h[t % 2][:, :], sg[t % 2][:, :], up[t % 2][:, 1, :], ALU.mult).then_inc(c["h"].sem, 1)

            def add_shared(n, u, it, t):
                if t == 0:
                    v.wait_ge(c["base_in"][u].sem, c["base_in"][u].value(it))
                v.wait_ge(c["dn"].sem, c["dn"].value(n, t + 1))
                v.tensor_tensor(base[u][:, t, :], dp[t % 2][:, 0:E], base[u][:, t, :], ALU.add).then_inc(c["base"].sem, 1)

            def choose(n, u, it, between):
                k = c["r"]
                done, calls = [0], [0]

                def step(*ops):
                    if done[0]:
                        v.wait_ge(k.sem, k.value(n, done[0]))
                    if len(ops) == TB:
                        stand_alone(v, passed)
                    for op in ops:
                        op().then_inc(k.sem, 1)
                        done[0] += 1
                    calls[0] += 1
                    between.get(calls[0], lambda: None)()

                v.wait_ge(k.sem, k.value(n - 1))
                v.wait_ge(c["ex"].sem, c["ex"].value(n))
                groups = lambda ap: ap.rearrange("p t (g s) -> p t g s", s=GS)
                last1 = lambda ap: ap.rearrange("p t (g o) -> p t g o", o=1)
                step(lambda: v.tensor_scalar(sig[:, :, :], ex[:, :, :], 1.0, None, ALU.add))
                step(lambda: v.reciprocal(sig[:, :, :], sig[:, :, :]))
                step(lambda: v.tensor_tensor(sfc[:, :, :], sig[:, :, :],
                                             ebias[:, :].rearrange("p (o e) -> p o e", o=1).to_broadcast([P, TB, NE]), ALU.add))
                step(lambda: v.tensor_reduce(gmax[:, :, :], groups(sfc[:, :, :]), X, ALU.max))
                gi = last1(gmax[:, :, :]).to_broadcast([P, TB, NG, NG])
                gj = gmax[:, :, :].rearrange("p t (o g) -> p t o g", o=1).to_broadcast([P, TB, NG, NG])
                step(lambda: v.tensor_tensor(gcmp[:, :, :, :], gj, gi, ALU.is_gt),
                     lambda: v.tensor_tensor(geq[:, :, :, :], gj, gi, ALU.is_equal))
                step(lambda: v.tensor_tensor(geq[:, :, :, :], geq[:, :, :, :],
                                             earlier[:, :, :].rearrange("p (o i) j -> p o i j", o=1).to_broadcast([P, TB, NG, NG]), ALU.mult))
                step(lambda: v.tensor_tensor(gcmp[:, :, :, :], gcmp[:, :, :, :], geq[:, :, :, :], ALU.add))
                step(lambda: v.tensor_reduce(rank[:, :, :], gcmp[:, :, :, :], X, ALU.add))
                step(lambda: v.tensor_scalar(rank[:, :, :], rank[:, :, :], float(TOPG), None, ALU.is_lt))
                step(lambda: v.tensor_tensor(cand[:, :, 0:NE].rearrange("p t (g s) -> p t g s", s=GS), groups(sfc[:, :, :]),
                                             last1(rank[:, :, :]).to_broadcast([P, TB, NG, GS]), ALU.mult))
                step(*[lambda t=t: v.max(top[:, t, :], cand[:, t, :]) for t in range(TB)])
                step(lambda: v.memset(top[:, :, TOPK:8], SENT))
                step(*[lambda t=t: v.match_replace(left[:, t, :], top[:, t, :], cand[:, t, :], 2 * SENT) for t in range(TB)])
                step(lambda: v.tensor_scalar(sel[:, :, :], left[:, :, 0:NE], 1.5 * SENT, None, ALU.is_lt))
                step(lambda: v.tensor_copy(selb[:, :, :], sel[:, :, :]),
                     lambda: v.tensor_tensor(wgt[:, :, :], sel[:, :, :], sig[:, :, :], ALU.mult))
                step(lambda: v.tensor_reduce(wsum[:, :], wgt[:, :, :], X, ALU.add))
                step(lambda: v.tensor_scalar(wsum[:, :], wsum[:, :], 1e-20, None, ALU.add))
                step(lambda: v.reciprocal(winv[:, :], wsum[:, :]))
                step(lambda: v.tensor_scalar(winv[:, :], winv[:, :], SCALE, None, ALU.mult))
                step(lambda: v.tensor_tensor(wgt[:, :, :], wgt[:, :, :],
                                             winv[:, :].rearrange("p (t o) -> p t o", o=1).to_broadcast([P, TB, NE]), ALU.mult),
                     lambda: v.tensor_copy(cnt[:, 0, :], cnt[:, TB, :]))
                v.wait_ge(c["cnt"].sem, c["cnt"].value(n))
                for t in range(TB):
                    step(lambda: v.tensor_tensor(cnt[:, t + 1, :], cnt[:, t, :], lp[:, 2, t, :], ALU.add))
                step(lambda: v.tensor_tensor(key[:, :, :], lp[:, 1, :, :], cnt[:, 0:TB, :], ALU.add))
                step(lambda: v.scalar_tensor_tensor(key[:, :, :], key[:, :, :], 1.0,
                                                    regions[:, :].rearrange("p (o e) -> p o e", o=1).to_broadcast([P, TB, NE]), ALU.add, ALU.add))
                step(lambda: v.tensor_tensor(key[:, :, :], key[:, :, :], sel[:, :, :], ALU.mult))
                step(*[lambda t=t: v.max(ktop[:, t, :], key[:, t, :]) for t in range(TB)])
                scattered(u, it)
                step(lambda: v.tensor_scalar(slots[u][:, :, :], ktop[:, :, 0:TOPK], -1.0, None, ALU.add),
                     lambda: v.tensor_tensor(hit[:, :, :, :], key[:, :, :].rearrange("p t (o e) -> p t o e", o=1).to_broadcast([P, TB, TOPK, NE]),
                                             last1(ktop[:, :, 0:TOPK]).to_broadcast([P, TB, TOPK, NE]), ALU.is_equal),
                     lambda: v.tensor_copy(rows[u][:, :, :, E + 1].bitcast(I32), dst[:, :, :]))
                step(lambda: v.tensor_tensor(hit[:, :, :, :], hit[:, :, :, :],
                                             wgt[:, :, :].rearrange("p t (o e) -> p t o e", o=1).to_broadcast([P, TB, TOPK, NE]), ALU.mult),
                     lambda: v.tensor_scalar(dst[:, :, :], dst[:, :, :], float(S * TOPK), None, ALU.add))
                step(lambda: v.tensor_reduce(rows[u][:, :, :, E], hit[:, :, :, :], X, ALU.add))
                assert done[0] == R_STEPS and all(i <= calls[0] for i in between), (done, calls)

            stats(0, 0, 0)
            normalise(0, 0)
            v.wait_ge(c["init"], 10)
            v.wait_ge(c["once"], 7 * 16)
            v.tensor_copy(before[:, :], before32[:, :]).then_inc(c["init"], 1)

            def body(n, u, it, first, last):
                between = {}
                if not first:
                    m = (n - 1, 1 - u, it + u - 1)
                    for t in range(TB):
                        between[HIDDEN_AT[t]] = lambda t=t: gate_hidden(m[0], t)
                        between[SHARED_AT[t]] = lambda t=t: add_shared(*m, t)
                if not (last and u):
                    stats(n + 1, 1 - u, it + u)
                    between[XN_AT] = lambda: normalise(n + 1, 1 - u)
                choose(n, u, it, between)

            loop(v, body)
            end = c["end"]
            last = cnt[:, TB, :]
            v.wait_ge(c["r"].sem, c["r"].value(B - 1))
            done = [0]

            def step(op):
                if done[0]:
                    v.wait_ge(end, done[0])
                op().then_inc(end, 1)
                done[0] += 1

            v.tensor_scalar(num[:, :], index[:, :], 0.5, None, ALU.mult).then_inc(c["init"], 1)
            v.wait_ge(c["init"], 12)
            step(lambda: v.scalar_tensor_tensor(padidx[:, :], last, num[:, 0:1], regions[:, :], ALU.add, ALU.add))
            step(lambda: v.tensor_scalar(nti[:, :], last, float(P - 1), None, ALU.add))
            step(lambda: v.tensor_scalar(nti[:, :], nti[:, :], 7, None, ALU.logical_shift_right))
            step(lambda: v.tensor_copy(ntile[:, :], nti[:, :]))
            step(lambda: v.tensor_tensor_scan(ends[:, :], ntile[:, :], zero[:, :], 0.0, ALU.add, ALU.add))
            e3 = lambda ap: ap.rearrange("p (o e) -> p o e", o=1).to_broadcast([P, 2, NE])
            i3 = lambda ap: ap.rearrange("p (c o) -> p c o", o=1).to_broadcast([P, 2, NE])
            step(lambda: v.tensor_tensor(ind[:, :, :], i3(index[:, :]), e3(ends[:, :]), ALU.is_ge))
            step(lambda: v.tensor_reduce(num[:, :], ind[:, :, :], X, ALU.add))
            step(lambda: v.tensor_tensor(ind2[:, :, :], ind[:, :, :], e3(ntile[:, :]), ALU.mult))
            step(lambda: v.tensor_reduce(start[:, :], ind2[:, :, :], X, ALU.add))
            step(lambda: v.tensor_scalar(tab_i[:, 1, :], num[:, :], float(NE - 1), float(WE), ALU.min, ALU.mult))
            step(lambda: v.tensor_sub(start[:, :], index[:, :], start[:, :]))
            step(lambda: v.tensor_scalar(start[:, :], start[:, :], float(P), None, ALU.mult))
            step(lambda: v.scalar_tensor_tensor(start[:, :], num[:, :], float(REG), start[:, :], ALU.mult, ALU.add))
            step(lambda: v.tensor_scalar(tab_i[:, 0, :], start[:, :], float(PADS), None, ALU.min))
            assert done[0] == T_LAST
            for t in range(TB + 1):
                if t < TB:
                    gate_hidden(B - 1, t)
                if t:
                    add_shared(B - 1, 1, B // 2 - 1, t - 1)

        @block.scalar
        def _(s):
            def xT_out(n, u):
                for i in range(EC):
                    s.wait_ge(c["tp"].sem, c["tp"].value(n, i + 1))
                    s.wait_ge(c["up"].sem, c["up"].value(n - 2))
                    s.copy(xT[u][:, i, :], tp[i][:, :]).then_inc(c["xT"].sem, 1)

            def copy_rows(n, u, it, t):
                if t == 0 and not (isinstance(it, int) and it == 0):
                    s.wait_ge(c["scat"][u].sem, c["scat"][u].value(it - 1))
                if t == 0:
                    s.wait_ge(c["xn"].sem, c["xn"].value(n))
                s.copy(rows[u][:, t, :, 0:E], xn[u][:, t:t + 1, :].to_broadcast([P, TOPK, E])).then_inc(c["rows"].sem, 1)

            def shared(n, t):
                if t < TB:
                    s.wait_ge(c["up"].sem, c["up"].value(n, t + 1))
                    s.wait_ge(c["h"].sem, c["h"].value(n, t - 1))
                    s.activation(sg[t % 2][:, :], up[t % 2][:, 0, :], ACT.Silu).then_inc(c["silu"].sem, 1)
                if t:
                    s.wait_ge(c["ht"].sem, c["ht"].value(n, t))
                    s.wait_ge(c["dn"].sem, c["dn"].value(n, t - 2))
                    s.copy(hT[(t - 1) % 2][:, :, :], hp[:, 0:SI // P, :]).then_inc(c["hT"].sem, 1)

            def body(n, u, it, first, last):
                s.wait_ge(c["lg"].sem, c["lg"].value(n))
                s.activation(ex[:, :, :], lp[:, 0, :, :], ACT.Exp, scale=-1.0).then_inc(c["ex"].sem, 1)
                for t in range(TB + 1):
                    if not first:
                        shared(n - 1, t)
                    if t:
                        copy_rows(n, u, it, t - 1)
                if not (last and u):
                    xT_out(n + 1, 1 - u)

            xT_out(0, 0)
            loop(s, body)
            for t in range(TB + 1):
                shared(B - 1, t)
            s.wait_ge(c["end"], 1)
            s.wait_ge(c["padrow"], 1)
            pad(s, range(NE * 3 // 8))

        @block.tensor
        def _(t_):
            def transposes(n, u):
                t_.wait_ge(c["xn"].sem, c["xn"].value(n))
                for i in range(EC):
                    t_.wait_ge(c["xT"].sem, c["xT"].value(n - 1, i + 1))
                    for t in range(TB):
                        last = t_.transpose(tp[i][:, t * P:(t + 1) * P], xn[u][:, t, i * P:(i + 1) * P], ident[:, :])
                    last.then_inc(c["tp"].sem, 1)

            def logits(n, u):
                t_.wait_ge(c["xT"].sem, c["xT"].value(n))
                t_.wait_ge(c["r"].sem, c["r"].value(n - 1, R_COUNTED))
                for t in range(TB):
                    for i in range(EC):
                        last = t_.matmul(lp[:, 0, t, :], xT[u][:, i, t * P:(t + 1) * P], gate[:, i, :], start=(i == 0), stop=(i == EC - 1))
                last.then_inc(c["lg"].sem, 1)

            def shared_up(n, u, t):
                t_.wait_ge(c["h"].sem, c["h"].value(n, t - 1))
                for i in range(EC):
                    last = t_.matmul(up[t % 2][:, :, :].rearrange("p a b -> p (a b)"), xT[u][:, i, t * P:(t + 1) * P], wsh[:, i, :],
                                     start=(i == 0), stop=(i == EC - 1))
                last.then_inc(c["up"].sem, 1)

            def hidden_back(n, t):
                t_.wait_ge(c["h"].sem, c["h"].value(n, t + 1))
                t_.wait_ge(c["hT"].sem, c["hT"].value(n, t))
                for i in range(SI // P):
                    last = t_.transpose(hp[:, i, :], h[t % 2][:, i * P:(i + 1) * P], ident[:, :])
                last.then_inc(c["ht"].sem, 1)

            def shared_down(n, t):
                t_.wait_ge(c["hT"].sem, c["hT"].value(n, t + 1))
                t_.wait_ge(c["base"].sem, c["base"].value(n, t - 1))
                for i in range(SI // P):
                    last = t_.matmul(dp[t % 2][:, 0:E], hT[t % 2][:, i, :], wsd[:, i, :], start=(i == 0), stop=(i == SI // P - 1))
                last.then_inc(c["dn"].sem, 1)

            def counts(n):
                t_.wait_ge(c["r"].sem, c["r"].value(n, R_SELECTED))
                flat = selb[:, :, :].rearrange("p t e -> p (t e)")
                t_.matmul(lp[:, 1, :, :].rearrange("p t e -> p (t e)"), before[:, :], flat, start=True, stop=True)
                t_.matmul(lp[:, 2, :, :].rearrange("p t e -> p (t e)"), ones[:, :], flat, start=True, stop=True).then_inc(c["cnt"].sem, 1)

            def body(n, u, it, first, last):
                for t in range(TB):
                    if not first:
                        shared_up(n - 1, 1 - u, t)
                        if t:
                            hidden_back(n - 1, t - 1)
                            shared_down(n - 1, t - 1)
                    if t == 2:
                        counts(n)
                if not first:
                    hidden_back(n - 1, TB - 1)
                    shared_down(n - 1, TB - 1)
                if not (last and u):
                    transposes(n + 1, 1 - u)
                    logits(n + 1, 1 - u)

            transposes(0, 0)
            t_.wait_ge(c["once"], 7 * 16)
            t_.wait_ge(c["init"], 11)
            logits(0, 0)
            loop(t_, body)
            for t in range(TB):
                shared_up(B - 1, 1, t)
                if t:
                    hidden_back(B - 1, t - 1)
                    shared_down(B - 1, t - 1)
            hidden_back(B - 1, TB - 1)
            shared_down(B - 1, TB - 1)


R_SELECTED = 22
T_LAST = 14
R_COUNTED = 34
HIDDEN_AT, SHARED_AT, XN_AT = [4, 9, 16, 24], [8, 14, 20, 28], 19


XR = 16
YR = 8
WE = (EC * 2 * FI) + E


def expert_counts(count, sem):
    def each(name, per=1, ahead=2, ring=2):
        return [count(f"ex_{name}{u}", per, ahead) for u in range(ring)]

    return dict(
        weights=sem("ex_weights"), x_in=each("x_in", 16, ring=XR), y_out=each("y_out", 16, 0, YR),
        tp=each("tp"), xT=each("xT"), up=each("up"), silu=each("silu"), h=each("h"),
        ht=each("ht"), hT=each("hT"), dn=each("dn"), y=each("y"),
    )


def experts(nc, a, sc, c, passed, ident, tiles, weights):
    with ExitStack() as es:
        def ring(k, name, shape, dt=F32):
            return [es.enter_context(nc.sbuf_tensor(f"ex_{name}{u}", shape, dt)) for u in range(k)]

        def banks(name):
            return [es.enter_context(nc.psum_tensor(f"ex_{name}{u}", [P, 512], F32)) for u in range(2)]

        x, xT = ring(XR, "x", [P, ROWW]), ring(2, "xT", [P, EC, P])
        sg, h, hT, y = ring(2, "sg", [P, FI]), ring(2, "h", [P, FI]), ring(2, "hT", [FI, P]), ring(YR, "y", [P, E])
        tp, up, hp, dp = banks("tp"), banks("up"), banks("hp"), banks("dp")
        tp_, up_ = [b[:, 0:E].rearrange("p (c q) -> p c q", c=EC) for b in tp], [b[:, 0:2 * FI].rearrange("p (c i) -> p c i", c=2) for b in up]
        block = es.enter_context(nc.Block())
        U = XR

        def step(name, v):
            return c[name][v % len(c[name])]

        def fixed(it):
            return lambda name, v: step(name, v).value((U * it + v) // len(c[name]))

        def loop(eng, body, peel=1):
            for n in range(peel * U):
                body(n % U, n // U, fixed(n // U), n < U, False)
            with eng.Fori(peel, TILES // U - 1) as it:
                held = {}

                def at(name, v):
                    k, ring = step(name, v), len(c[name])
                    key = (k.per, k.ahead, ring, v // ring)
                    if key not in held:
                        held[key] = eng.snap(k.value(it * (U // ring) + v // ring))
                    return held[key]

                for u in range(U):
                    body(u, it, at, False, False)
            for u in range(U):
                body(u, TILES // U - 1, fixed(TILES // U - 1), False, True)

        def entry(eng, which, n, top):
            return eng.value_load(tiles[0:1, which, bass.ds(n, 1)], min_val=0, max_val=top)

        @block.sync
        def _(sp):
            def load(n, u):
                sp.dma_start(x[u][:, :], sc["slots"][bass.ds(entry(sp, 0, n, PADS), P), :]).then_inc(c["x_in"][u].sem, 16)

            for u in range(U):
                load(u, u)

            def body(u, it, at, first, last):
                if not last:
                    sp.wait_ge(step("y_out", u).sem, at("y_out", u))
                    load(it * U + (U + u), u)

            loop(sp, body)

        @block.gpsimd
        def _(g):
            def body(u, it, at, first, last):
                g.wait_ge(step("y", u).sem, at("y", u))
                stand_alone(g, passed)
                g.indirect_dma_start(sc["y"], bass.IndirectOffsetOnAxis(ap=x[u][:, E + 1:E + 2].bitcast(U32), axis=0),
                                     y[u % YR][:, :], None, bounds_check=NY - 1, oob_is_err=False).then_inc(step("y_out", u).sem, 16)

            loop(g, body)
            for u in range(YR):
                g.wait_ge(c["y_out"][u].sem, c["y_out"][u].value(TILES // YR - 1))

        @block.scalar
        def _(s):
            def hT_out(v, at, first):
                s.wait_ge(step("ht", v).sem, at("ht", v))
                if not (first and v < 2):
                    s.wait_ge(step("dn", v - 2).sem, at("dn", v - 2))
                s.copy(hT[v % 2][:, :], hp[v % 2][:, 0:P]).then_inc(step("hT", v).sem, 1)

            def xT_out(v, at):
                s.wait_ge(step("tp", v).sem, at("tp", v))
                s.copy(xT[v % 2][:, :, :], tp_[v % 2]).then_inc(step("xT", v).sem, 1)

            def body(u, it, at, first, last):
                s.wait_ge(step("up", u).sem, at("up", u))
                s.activation(sg[u % 2][:, :], up_[u % 2][:, 0, :], ACT.Silu).then_inc(step("silu", u).sem, 1)
                if not (last and u >= U - 2):
                    xT_out(u + 2, at)
                if u or not first:
                    hT_out(u - 1, at, first)

            xT_out(0, fixed(0))
            xT_out(1, fixed(0))
            loop(s, body)
            hT_out(U - 1, fixed(TILES // U - 1), False)

        @block.vector
        def _(v):
            def weigh(w, at, used):
                v.wait_ge(step("dn", w).sem, at("dn", w))
                if used:
                    v.wait_ge(step("y_out", w).sem, at("y_out", w - YR))
                v.tensor_scalar(y[w % YR][:, :], dp[w % 2][:, 0:E], x[w % U][:, E:E + 1], None, ALU.mult).then_inc(step("y", w).sem, 1)

            def body(u, it, at, first, last):
                w = u - 2
                v.wait_ge(step("silu", u).sem, at("silu", u))
                v.tensor_tensor(h[u % 2][:, :], sg[u % 2][:, :], up_[u % 2][:, 1, :], ALU.mult).then_inc(step("h", u).sem, 1)
                if w >= 0 or not first:
                    weigh(w, at, not first or w >= YR)

            loop(v, body)
            for w in (U - 2, U - 1):
                weigh(w, fixed(TILES // U - 1), True)

        @block.tensor
        def _(t):
            def x_back(v, at):
                t.wait_ge(step("x_in", v).sem, at("x_in", v))
                for i in range(EC):
                    last = t.transpose(tp_[v % 2][:, i, :], x[v % U][:, i * P:(i + 1) * P], ident[:, :])
                last.then_inc(step("tp", v).sem, 1)

            def weights_of(n):
                return entry(t, 1, n, (NE - 1) * WE)

            def down(v, at, w, first):
                t.wait_ge(step("hT", v).sem, at("hT", v))
                if not (first and v < 2):
                    t.wait_ge(step("y", v - 2).sem, at("y", v - 2))
                t.matmul(dp[v % 2][:, 0:E], hT[v % 2][:, :], weights[:, bass.ds(w + EC * 2 * FI, E)],
                         start=True, stop=True).then_inc(step("dn", v).sem, 1)

            held = {}

            def h_back(v, at):
                t.wait_ge(step("h", v).sem, at("h", v))
                t.transpose(hp[v % 2][:, 0:P], h[v % 2][:, :], ident[:, :]).then_inc(step("ht", v).sem, 1)

            def body(u, it, at, first, last):
                held[u] = weights_of(it * U + u)
                t.wait_ge(step("xT", u).sem, at("xT", u))
                for i in range(EC):
                    mm = t.matmul(up[u % 2][:, 0:2 * FI], xT[u % 2][:, i, :],
                                  weights[:, bass.ds(held[u] + i * 2 * FI, 2 * FI)], start=(i == 0), stop=(i == EC - 1))
                mm.then_inc(step("up", u).sem, 1)
                if not (last and u >= U - 2):
                    x_back(u + 2, at)
                if u or not first:
                    h_back(u - 1, at)
                if u >= 2 or not first:
                    if u < 2:
                        held[u - 2] = weights_of(it * U + (u - 2))
                    down(u - 2, at, held[u - 2], first)

            x_back(0, fixed(0))
            x_back(1, fixed(0))
            t.wait_ge(c["weights"], 16 * B)
            loop(t, body)
            end = fixed(TILES // U - 1)
            h_back(U - 1, end)
            for v in (U - 2, U - 1):
                down(v, end, weights_of(TILES - U + v), False)


CR = 4
CV = 3


def combine_counts(count, sem):
    def each(name):
        return [count(f"co_{name}{u}", 16) for u in range(CR)]

    return dict(base_in=each("base_in"), y_in=each("y_in"), yp_in=each("yp_in"), out=each("out"),
                add=count("co_add", TOPK), addp=count("co_addp", TOPK))


def combine(nc, a, sc, c, out):
    U = CR
    with ExitStack() as es:
        acc = [es.enter_context(nc.sbuf_tensor(f"acc{u}", [P, TB, E], F32)) for u in range(U)]
        y = [es.enter_context(nc.sbuf_tensor(f"yy{u}", [P, TB, TOPK, E], F32)) for u in range(U)]
        block = es.enter_context(nc.Block())
        y_rows = sc["y"].rearrange("(n t p j) e -> n p t (j e)", t=TB, j=TOPK, p=P)
        out_rows = out.rearrange("(n t p) e -> n p t e", t=TB, p=P)

        @block.sync
        def _(sp):
            def load(it, u):
                n = it * U + u
                for k, tiles in ((c["y_in"], slice(0, CV)), (c["yp_in"], slice(CV, TB))):
                    sp.dma_start(y[u][:, tiles, :, :].rearrange("p t j e -> p t (j e)"),
                                 y_rows[bass.ds(n, 1), :, tiles].rearrange("o p t e -> (o p) t e")).then_inc(k[u].sem, 16)

            def load_base(it, u):
                sp.dma_start(acc[u][:, :, :], sc["base"][bass.ds(it * U + u, 1)].rearrange("o p t e -> (o p) t e")).then_inc(c["base_in"][u].sem, 16)

            for u in range(U):
                load_base(0, u)
                load(0, u)
            for it in range(1, B // U):
                for u in range(U):
                    sp.wait_ge(c["out"][u].sem, c["out"][u].value(it - 1))
                    load_base(it, u)
                    load(it, u)

        @block.scalar
        def _(s):
            with s.Fori(0, B // U) as it:
                for u in range(U):
                    for k in (c["add"], c["addp"]):
                        s.wait_ge(k.sem, k.value(it * U + u))
                    s.dma_start(out_rows[bass.ds(it * U + u, 1)].rearrange("o p t e -> (o p) t e"), acc[u][:, :, :]).then_inc(c["out"][u].sem, 16)
            for u in range(U):
                s.wait_ge(c["out"][u].sem, c["out"][u].value(B // U - 1))

        def sums(eng, k, rows_in, tiles):
            with eng.Fori(0, B // U) as it:
                for u in range(U):
                    n = it * U + u
                    eng.wait_ge(c["base_in"][u].sem, c["base_in"][u].value(it))
                    eng.wait_ge(rows_in[u].sem, rows_in[u].value(it))
                    for j in range(TOPK):
                        if j:
                            eng.wait_ge(k.sem, k.value(n, j))
                        eng.tensor_tensor(acc[u][:, tiles, :], acc[u][:, tiles, :], y[u][:, tiles, j, :], ALU.add).then_inc(k.sem, 1)

        @block.vector
        def _(v):
            sums(v, c["add"], c["y_in"], slice(0, CV))

        @block.gpsimd
        def _(g):
            sums(g, c["addp"], c["yp_in"], slice(CV, TB))


def shape_constants():
    bucket = np.searchsorted(BUCKET_STARTS, np.arange(S), side="right") - 1
    rel = P - 1 - NEAR_LO - np.arange(DIAG)
    of = np.where(rel > 0, BUCKETS // 2, 0) + bucket[np.abs(rel)]
    onehot_diag = (of[None, :] == np.arange(BUCKETS)[:, None]).astype(np.float32)
    u = np.arange(S)[None, :] - P * np.arange(TB)[:, None]
    far = np.where(u < NEAR_LO, BUCKETS - 1, np.where(u >= NEAR_LO + NEAR_W, BUCKETS // 2 - 1, -1)).reshape(-1)
    onehot_far = (far[None, :] == np.arange(BUCKETS)[:, None]).astype(np.float32)
    blocks = (np.arange(S)[None, :] // P == np.arange(TB)[:, None]).astype(np.float32)
    krows = np.concatenate([np.ones((3, S), np.float32), blocks, blocks, blocks])
    g = np.arange(NG)
    return dict(
        eye=np.eye(P, dtype=np.float32), onehot_diag=onehot_diag, onehot_far=onehot_far, krows=krows,
        before=np.triu(np.ones((P, P), np.float32), 1),
        earlier=np.broadcast_to((g[None, :] < g[:, None]).astype(np.float32).reshape(1, -1), (P, NG * NG)).copy(),
        regions=np.broadcast_to(np.arange(NE, dtype=np.float32)[None, :] * REG, (P, NE)).copy(),
    )


def arrays_of(i):
    n = lambda k: np.asarray(i[k])
    t = np.ascontiguousarray
    gu = n("L0_ffn_experts_gate_up")
    shared = np.concatenate([n("L0_ffn_shared_gate_w"), n("L0_ffn_shared_up_w")])
    return dict(
        x=t(n("x").reshape(B * S, E)), ctxT=t(n("ctx_1024").reshape(B * S, E).T),
        wq=t(n("L0_xattn_Wq")), wkv=t(n("L0_xattn_Wkv")), wo=t(n("L0_xattn_Wo")),
        rel_bias=t(n("L0_xattn_rel_bias").T), gateT=t(n("L0_ffn_gate_weight").T),
        ebias=t(n("L0_ffn_e_score_correction_bias").reshape(1, NE)),
        experts=t(np.concatenate([gu.reshape(NE, 2 * FI, EC, P).transpose(3, 0, 2, 1).reshape(P, NE, -1),
                                  n("L0_ffn_experts_down").transpose(2, 0, 1)], axis=2).reshape(P, -1)),
        shared=t(shared.reshape(2 * SI, EC, P).transpose(2, 1, 0)),
        shared_dn=t(n("L0_ffn_shared_down_w").reshape(E, SI // P, P).transpose(2, 1, 0)),
        **shape_constants(),
    )


def kernel(**inputs):
    import concourse.bacc as bacc
    from concourse.bass_utils import run_bass_kernel_spmd

    nc = bacc.Bacc("TRN2", target_bir_lowering=False, num_devices=1)
    arrays = arrays_of(inputs)
    a = {k: nc.dram_tensor("in_" + k, v.shape, mybir.dt.from_np(v.dtype), kind="ExternalInput").ap() for k, v in arrays.items()}
    out = nc.dram_tensor("out", (B * S, E), F32, kind="ExternalOutput").ap()
    build(nc, a, out)
    r = run_bass_kernel_spmd(nc, [{"in_" + k: v for k, v in arrays.items()}], core_ids=[0])
    return r.results[0]["out"].reshape(B, S, E)
```

```python
import numpy as np
import concourse.bass as bass
import concourse.mybir as mybir
from contextlib import ExitStack

F32 = mybir.dt.float32
BF16 = mybir.dt.bfloat16
I32 = mybir.dt.int32
U32 = mybir.dt.uint32
ALU = mybir.AluOpType
ACT = mybir.ActivationFunctionType
X = mybir.AxisListType.X

P = 128
B, S, E = 8, 512, 256
H, D = 16, 16
TB = S // P
EC = E // P
NT = B * TB
EPS = 1e-5

BUCKETS = 32
BUCKET_STARTS = [0, 1, 2, 3, 4, 5, 6, 7, 8, 12, 16, 23, 32, 46, 64, 91]
FAR = BUCKET_STARTS[-1]
NEAR_LO = -(FAR - 1)
NEAR_W = P + 2 * (FAR - 1)
DIAG = NEAR_W + P - 1

TERMS = [(0, 0), (0, 1), (1, 0), (1, 1), (0, 2), (2, 0)]
KQ = len(TERMS) * D
ROW_MAX = KQ
ROW_FAR = KQ + 3
KS = ROW_FAR + 3 * TB
VW = 32
CH = 2 * TB * 4
NS = H * TB

NE, TOPK, NG, TOPG, SCALE = 32, 6, 8, 4, 2.5
GS = NE // NG
FI, SI = 128, 256
REG = B * S + P
PADS = NE * REG
ROWW = E + 4
TILES = 224
NY = TOPK * B * S
SENT = -1e30


class Count:

    def __init__(self, sem, per=1, ahead=2):
        self.sem, self.per, self.ahead = sem, per, ahead

    def value(self, n, part=None):
        return (n + self.ahead) * self.per + (self.per if part is None else part)


def stand_alone(eng, passed):
    eng.sem_inc(passed, 1)


def build(nc, a, out):
    ctx = ExitStack()
    counts = []

    def sem(name):
        return ctx.enter_context(nc.semaphore(name))

    def count(name, per=1, ahead=2):
        c = Count(sem(name), per, ahead)
        counts.append(c)
        return c

    def dram(name, shape, dt):
        return nc.dram_tensor(name, shape, dt, kind="Internal").ap()

    with ctx:
        sc = dict(
            parts=dram("parts", [B, 2, E, 3, S], BF16),
            v=dram("v", [B, P, H // 4, TB, 4 * D], F32),
            diag=dram("diag", [H, P, DIAG + P], F32),
            krows=dram("krows", [KS - ROW_MAX, S], BF16),
            far=dram("far", [3, TB, H, S], BF16),
            negmax=dram("negmax", [B, 3, NS, P], BF16),
            x1=dram("x1", [B, P, TB, E], F32),
            base=dram("base", [B, P, TB, E], F32),
            slots=dram("slots", [PADS + P, ROWW], F32),
            tiletab=dram("tiletab", [2, P, 2], I32),
            y=dram("y", [NY, E], F32),
        )
        passed = sem("passed")
        c1, c2 = project_counts(count, sem), attend_counts(count, sem)
        c3, c4, c5 = route_counts(count, sem), expert_counts(count, sem), combine_counts(count, sem)
        with ExitStack() as held:
            ident = held.enter_context(nc.sbuf_tensor("ident", [P, P], F32))
            identb = held.enter_context(nc.sbuf_tensor("identb", [P, P], BF16))
            tiles = held.enter_context(nc.sbuf_tensor("tiles", [1, 2, 2 * P], I32))
            acc = held.enter_context(nc.sbuf_tensor("acc", [P, B, TB, E], F32))
            with (
                nc.sbuf_tensor("near", [P, H, NEAR_W], F32) as near,
                nc.sbuf_tensor("qs", [P, 2, H, S], BF16) as qs,
                nc.sbuf_tensor("ks", [P, 2, H, S], BF16) as ks,
            ):
                project(nc, a, sc, counts, sem, c1, c2, passed, ident, identb, near, qs, ks)
                attend(nc, a, sc, c2, passed, ident, identb, near, qs, ks, acc, c3["x_in"])
            with nc.sbuf_tensor("weights", [P, NE * WE], F32) as weights:
                route(nc, a, sc, c3, passed, ident, tiles, acc, weights, c4["weights"])
                experts(nc, a, sc, c4, passed, ident, tiles, weights, acc, c5["acc_in"])
            combine(nc, a, sc, c5, passed, acc, out)


class Tables:

    def __init__(self, es, nc, a, sc, sem, ident, identb, banks, small, diagonals, rest, parts):
        def sb(name, shape, dt=F32):
            return es.enter_context(nc.sbuf_tensor("tb_" + name, shape, dt))

        self.a, self.sc, self.ident, self.identb = a, sc, ident, identb
        self.loaded, self.dve, self.pe, self.act, self.out = (sem("tb_" + n) for n in ("loaded", "dve", "pe", "act", "out"))
        self.rel, self.relmax, self.relT = sb("rel", [H, BUCKETS]), sb("relmax", [H, 1]), sb("relT", [BUCKETS, H])
        self.oh_diag, self.oh_far = sb("oh_diag", [BUCKETS, DIAG]), sb("oh_far", [BUCKETS, TB * S])
        self.ediag, self.krows32 = sb("ediag", [H, DIAG]), sb("krows32", [KS - ROW_MAX, S])
        self.krows16 = sb("krows16", [KS - ROW_MAX, S], BF16)
        self.frest = rest[0:H].rearrange("p h w -> p (h w)")[:, 0:2 * TB * S].rearrange("p (i s) -> p i s", i=2)
        self.fparts = parts[0:H].rearrange("p h s -> p (h s)")[:, 0:3 * TB * S].rearrange("p (i s) -> p i s", i=3)
        self.pt, self.pd, self.pf = small[0:BUCKETS, 0:H], diagonals[0:H, 0:DIAG], [b[0:H, :] for b in banks]

    def load(self, sp):
        for dst, src in ((self.ident, "eye"), (self.rel, "rel_bias"), (self.oh_diag, "onehot_diag"), (self.oh_far, "onehot_far"),
                         (self.krows32, "krows")):
            sp.dma_start(dst[:, :], self.a[src]).then_inc(self.loaded, 16)

    def store(self, sp):
        sc = self.sc
        sp.wait_ge(self.act, 1)
        skewed = bass.AP(tensor=sc["diag"].tensor, offset=0, ap=[[P * (DIAG + P), H], [DIAG + P + 1, P], [1, DIAG]])
        sp.dma_start(skewed, self.ediag[:, :].rearrange("h (o i) -> h o i", o=1).to_broadcast([H, P, DIAG])).then_inc(self.out, 16)
        sp.wait_ge(self.dve, FAR_SPLIT)
        for p in range(3):
            sp.dma_start(sc["far"][p].rearrange("k h s -> h k s"),
                         self.fparts[:, p, :].rearrange("h (k s) -> h k s", k=TB)).then_inc(self.out, 16)
        sp.dma_start(sc["krows"], self.krows16[:, :]).then_inc(self.out, 16)

    def less_max(self, v):
        dve = self.dve
        v.wait_ge(self.loaded, 80)
        v.tensor_copy(self.identb[:, :], self.ident[:, :]).then_inc(dve, 1)
        v.reduce_max(self.relmax[:, :], self.rel[:, :], X).then_inc(dve, 1)
        v.wait_ge(dve, 2)
        v.tensor_scalar(self.frest[:, 0, 0:BUCKETS], self.rel[:, :], self.relmax[:, 0:1], None, ALU.subtract).then_inc(dve, 1)
        v.wait_ge(self.pe, 1)
        v.tensor_copy(self.relT[:, :], self.pt).then_inc(dve, 1)

    def split_far(self, v):
        dve, fparts, frest = self.dve, self.fparts, self.frest
        v.wait_ge(self.pe, 3)
        for k in range(TB):
            at = slice(k * S, (k + 1) * S)
            v.tensor_copy(fparts[:, 0, at], self.pf[k]).then_inc(dve, 1)
        v.wait_ge(dve, 4 + TB)
        for k in range(TB):
            at = slice(k * S, (k + 1) * S)
            v.tensor_sub(frest[:, 0, at], self.pf[k], fparts[:, 0, at]).then_inc(dve, 1)
        v.wait_ge(dve, FAR_READ)
        v.tensor_copy(fparts[:, 1, :], frest[:, 0, :]).then_inc(dve, 1)
        v.wait_ge(dve, FAR_READ + 1)
        v.tensor_sub(frest[:, 1, :], frest[:, 0, :], fparts[:, 1, :]).then_inc(dve, 1)
        v.wait_ge(dve, FAR_READ + 2)
        v.tensor_copy(fparts[:, 2, :], frest[:, 1, :]).then_inc(dve, 1)
        v.tensor_copy(self.krows16[:, :], self.krows32[:, :]).then_inc(dve, 1)

    def exp_diagonals(self, s):
        s.wait_ge(self.pe, 2)
        s.activation(self.ediag[:, :], self.pd, ACT.Exp).then_inc(self.act, 1)

    def products(self, t):
        t.wait_ge(self.dve, 3)
        t.transpose(self.pt, self.frest[:, 0, 0:BUCKETS], self.ident[0:H, 0:H]).then_inc(self.pe, 1)
        t.wait_ge(self.dve, 4)
        t.matmul(self.pd, self.relT[:, :], self.oh_diag[:, :], start=True, stop=True).then_inc(self.pe, 1)
        for k in range(TB):
            last = t.matmul(self.pf[k], self.relT[:, :], self.oh_far[:, k * S:(k + 1) * S], start=True, stop=True)
        last.then_inc(self.pe, 1)


FAR_READ = 4 + 2 * TB
FAR_SPLIT = FAR_READ + 4


def project_counts(count, sem):
    return dict(
        weights=sem("pr_weights"), near_in=sem("pr_near_in"), half=sem("pr_half"),
        x_in=[count(f"pr_x_in{u}", 16) for u in range(2)], c_in=[count(f"pr_c_in{u}", 16) for u in range(2)],
        parts_out=[count(f"pr_parts_out{u}", 16) for u in range(2)], v_out=[count(f"pr_v_out{u}", 16) for u in range(2)],
        stats=count("pr_stats", 8), rstd=count("pr_rstd", 2), xn=count("pr_xn", TB),
        tp=count("pr_tp", 2), xnT=count("pr_xnT", 2), mm=count("pr_mm", 4), part1=count("pr_part1", 4),
        rest=count("pr_rest", 4), part2=count("pr_part2", 4), part3=count("pr_part3", 4),
        vmm=count("pr_vmm", 2), v=count("pr_v", 2),
    )


def project(nc, a, sc, counts, sem, c, c2, passed, ident, identb, near, qs, ks):
    def pair(name, shape, dt=F32):
        return [es.enter_context(nc.sbuf_tensor(f"pr_{name}{u}", shape, dt)) for u in range(2)]

    with ExitStack() as es:
        wq = es.enter_context(nc.sbuf_tensor("wq", [P, EC, E], F32))
        wkv = es.enter_context(nc.sbuf_tensor("wkv", [P, EC, 2 * E], F32))
        half = es.enter_context(nc.sbuf_tensor("half", [P, TB], F32))
        x, xn, xnT, cT = pair("x", [P, TB, E]), pair("xn", [P, TB, E]), pair("xnT", [P, EC, S]), pair("cT", [P, EC, S])
        st, mv, var, rstd = pair("st", [P, TB, 6]), pair("mv", [P, TB, 2]), pair("var", [P, TB]), pair("rstd", [P, TB])
        parts, vt, rest = pair("parts", [P, 4, 3, S], BF16), pair("vt", [P, H // 4, TB, 4 * D]), pair("rest", [P, S])
        tp = [es.enter_context(nc.psum_tensor(f"pr_tp{i}", [P, S], F32)) for i in range(EC)]
        qk = [es.enter_context(nc.psum_tensor(f"pr_qk{i}", [P, S], F32)) for i in range(4)]
        vp = [es.enter_context(nc.psum_tensor(f"pr_vp{i}", [P, 2, E], F32)) for i in range(2)]
        tables = Tables(es, nc, a, sc, sem, ident, identb, qk, tp[1], tp[0], near, ks[:, 1, :, :])
        block = es.enter_context(nc.Block())
        x_rows = a["x"].rearrange("(b t p) e -> b p t e", b=B, t=TB)
        cT_cols = a["ctxT"].rearrange("(c p) (b s) -> b p c s", p=P, b=B)
        parts_d = sc["parts"].rearrange("b k (m p) t s -> b p (k m) (t s)", p=P)

        @block.sync
        def _(sp):
            def load_x(n, u):
                sp.dma_start(x[u][:, :, :], x_rows[bass.ds(n, 1)].rearrange("o p t e -> (o p) t e")).then_inc(c["x_in"][u].sem, 16)

            def load_c(n, u):
                sp.dma_start(cT[u][:, :, :], cT_cols[bass.ds(n, 1)].rearrange("o p c s -> (o p) c s")).then_inc(c["c_in"][u].sem, 16)

            def step(n, u, last):
                if not last:
                    sp.wait_ge(c["xn"].sem, c["xn"].value(n))
                    load_x(n + 2, u)
                sp.wait_ge(c["part3"].sem, c["part3"].value(n))
                sp.dma_start(parts_d[bass.ds(n, 1)].rearrange("o p w s -> (o p) w s"),
                             parts[u][:, :, :, :].rearrange("p w t s -> p w (t s)")).then_inc(c["parts_out"][u].sem, 16)
                sp.wait_ge(c["v"].sem, c["v"].value(n))
                sp.dma_start(sc["v"][bass.ds(n, 1)].rearrange("o p g k w -> (o p) g k w"), vt[u][:, :, :, :]).then_inc(c["v_out"][u].sem, 16)
                if not last:
                    load_c(n + 2, u)

            for k in counts:
                if k.ahead:
                    sp.sem_inc(k.sem, k.ahead * k.per)
            tables.load(sp)
            load_x(0, 0)
            sp.dma_start(wq[:, :, :], a["wq"].rearrange("(c p) e -> p c e", p=P)).then_inc(c["weights"], 16)
            sp.dma_start(wkv[:, :, :], a["wkv"].rearrange("(c p) e -> p c e", p=P)).then_inc(c["weights"], 16)
            load_c(0, 0)
            load_x(1, 1)
            load_c(1, 1)
            tables.store(sp)
            with sp.Fori(0, B // 2 - 1) as it:
                for u in range(2):
                    step(it * 2 + u, u, False)
            sp.wait_ge(tables.out, 80)
            sp.dma_start(near[:, :, :], sc["diag"][:, :, P - 1:P - 1 + NEAR_W].rearrange("h k j -> k h j")).then_inc(c["near_in"], 16)
            step(B - 2, 0, True)
            sp.wait_ge(c["parts_out"][0].sem, c["parts_out"][0].value(0))
            load_stacks(sp, sc, qs, ks, c2["stack"], 0, 0, 0)
            step(B - 1, 1, True)
            for u in range(2):
                sp.dma_start(ks[ROW_MAX:KS, u, :, :], sc["krows"].rearrange("r (o s) -> r o s", o=1).to_broadcast([KS - ROW_MAX, H, S])).then_inc(c2["rows"], 16)
                sp.dma_start(qs[ROW_FAR:KS, u, :, :], sc["far"].rearrange("p k h s -> (p k) h s")).then_inc(c2["rows"], 16)
            sp.wait_ge(c["near_in"], 16)
            for u in range(2):
                sp.wait_ge(c["parts_out"][u].sem, c["parts_out"][u].value(B // 2 - 1))
                sp.wait_ge(c["v_out"][u].sem, c["v_out"][u].value(B // 2 - 1))

        @block.gpsimd
        def _(g):
            g.memset(half[:, :], -0.5).then_inc(c["half"], 1)
            g.wait_ge(c["half"], 1)

            def body(n, u):
                g.wait_ge(c["stats"].sem, c["stats"].value(n))
                stand_alone(g, passed)
                g.tensor_scalar(var[u][:, :], mv[u][:, :, 1], EPS, None, ALU.add).then_inc(c["rstd"].sem, 1)
                g.wait_ge(c["rstd"].sem, c["rstd"].value(n, 1))
                g.tensor_tensor(rstd[u][:, :], var[u][:, :], half[:, :], ALU.pow).then_inc(c["rstd"].sem, 1)

            with g.Fori(0, B // 2) as it:
                for u in range(2):
                    body(it * 2 + u, u)

        @block.vector
        def _(v):
            def stats(n, u, it):
                v.wait_ge(c["x_in"][u].sem, c["x_in"][u].value(it))
                v.wait_ge(c["rstd"].sem, c["rstd"].value(n - 2))
                v.wait_ge(c["xn"].sem, c["xn"].value(n - 2))
                for t in range(TB):
                    v.bn_stats(st[u][:, t, :], x[u][:, t, :]).then_inc(c["stats"].sem, 1)
                v.wait_ge(c["stats"].sem, c["stats"].value(n, TB))
                stand_alone(v, passed)
                for t in range(TB):
                    v.bn_aggr(mv[u][:, t, :], st[u][:, t, :]).then_inc(c["stats"].sem, 1)

            def normalise(n, u):
                v.wait_ge(c["rstd"].sem, c["rstd"].value(n))
                v.wait_ge(c["tp"].sem, c["tp"].value(n - 2))
                for t in range(TB):
                    v.tensor_scalar(xn[u][:, t, :], x[u][:, t, :], mv[u][:, t, 0:1], rstd[u][:, t:t + 1],
                                    ALU.subtract, ALU.mult).then_inc(c["xn"].sem, 1)

            def split(n, u, it, last):
                v.wait_ge(c["parts_out"][u].sem, c["parts_out"][u].value(it - 1))
                for w in range(4 + 1):
                    if w < 4:
                        v.wait_ge(c["part1"].sem, c["part1"].value(n, w + 1))
                        v.wait_ge(c["part3"].sem, c["part3"].value(n, w - 1))
                        v.tensor_sub(rest[w % 2][:, :], qk[w][:, :], parts[u][:, w, 0, :]).then_inc(c["rest"].sem, 1)
                    if w >= 1:
                        v.wait_ge(c["part2"].sem, c["part2"].value(n, w))
                        v.tensor_sub(parts[u][:, w - 1, 2, :], rest[(w - 1) % 2][:, :], parts[u][:, w - 1, 1, :]).then_inc(c["part3"].sem, 1)
                    if w == 2 and not last:
                        normalise(n + 1, 1 - u)

            tables.less_max(v)
            stats(0, 0, 0)
            normalise(0, 0)
            tables.split_far(v)

            def body(n, u, it, last):
                if not last:
                    stats(n + 1, 1 - u, it + u)
                split(n, u, it, last)

            with v.Fori(0, B // 2 - 1) as it:
                for u in range(2):
                    body(it * 2 + u, u, it, False)
            body(B - 2, 0, B // 2 - 1, False)
            body(B - 1, 1, B // 2 - 1, True)

        @block.scalar
        def _(s):
            def xnT_out(n, u):
                for i in range(EC):
                    s.wait_ge(c["tp"].sem, c["tp"].value(n, i + 1))
                    s.wait_ge(c["mm"].sem, c["mm"].value(n - 2, 2))
                    s.copy(xnT[u][:, i, :], tp[i][:, :]).then_inc(c["xnT"].sem, 1)

            def body(n, u, it, last):
                s.wait_ge(c["parts_out"][u].sem, c["parts_out"][u].value(it - 1))
                for w in range(4 + 1):
                    if w < 4:
                        s.wait_ge(c["mm"].sem, c["mm"].value(n, w + 1))
                        s.copy(parts[u][:, w, 0, :], qk[w][:, :]).then_inc(c["part1"].sem, 1)
                    if w >= 1:
                        s.wait_ge(c["rest"].sem, c["rest"].value(n, w))
                        s.copy(parts[u][:, w - 1, 1, :], rest[(w - 1) % 2][:, :]).then_inc(c["part2"].sem, 1)
                s.wait_ge(c["v_out"][u].sem, c["v_out"][u].value(it - 1))
                for i in range(2):
                    s.wait_ge(c["vmm"].sem, c["vmm"].value(n, i + 1))
                    s.copy(vt[u][:, :, 2 * i:2 * i + 2, :],
                           vp[i][:, :, :].rearrange("p k (g w) -> p g k w", w=4 * D)).then_inc(c["v"].sem, 1)
                if not last:
                    xnT_out(n + 1, 1 - u)

            tables.exp_diagonals(s)
            xnT_out(0, 0)
            with s.Fori(0, B // 2 - 1) as it:
                for u in range(2):
                    body(it * 2 + u, u, it, False)
            body(B - 2, 0, B // 2 - 1, False)
            body(B - 1, 1, B // 2 - 1, True)

        @block.tensor
        def _(t_):
            def transposes(n, u):
                for i in range(EC):
                    t_.wait_ge(c["xn"].sem, c["xn"].value(n))
                    t_.wait_ge(c["xnT"].sem, c["xnT"].value(n - 1, i + 1))
                    for t in range(TB):
                        last = t_.transpose(tp[i][:, t * P:(t + 1) * P], xn[u][:, t, i * P:(i + 1) * P], ident[:, :])
                    last.then_inc(c["tp"].sem, 1)

            def body(n, u, it, last):
                for w in range(4):
                    m = w % 2
                    if w == 0:
                        t_.wait_ge(c["xnT"].sem, c["xnT"].value(n))
                    if w == 2:
                        t_.wait_ge(c["c_in"][u].sem, c["c_in"][u].value(it))
                    t_.wait_ge(c["rest"].sem, c["rest"].value(n - 1, w + 1))
                    for i in range(EC):
                        lhsT = wq[:, i, m * P:(m + 1) * P] if w < 2 else wkv[:, i, m * P:(m + 1) * P]
                        rhs = xnT[u][:, i, :] if w < 2 else cT[u][:, i, :]
                        mm = t_.matmul(qk[w][:, :], lhsT, rhs, start=(i == 0), stop=(i == EC - 1))
                    mm.then_inc(c["mm"].sem, 1)
                for k2 in range(2):
                    t_.wait_ge(c["v"].sem, c["v"].value(n - 1, k2 + 1))
                    for k in range(2):
                        kb = 2 * k2 + k
                        for i in range(EC):
                            mm = t_.matmul(vp[k2][:, k, :], cT[u][:, i, kb * P:(kb + 1) * P], wkv[:, i, E:2 * E],
                                           start=(i == 0), stop=(i == EC - 1))
                    mm.then_inc(c["vmm"].sem, 1)
                if not last:
                    transposes(n + 1, 1 - u)

            tables.products(t_)
            t_.wait_ge(tables.act, 1)
            transposes(0, 0)
            t_.wait_ge(tables.dve, FAR_READ)
            t_.wait_ge(c["weights"], 32)
            with t_.Fori(0, B // 2 - 1) as it:
                for u in range(2):
                    body(it * 2 + u, u, it, False)
            body(B - 2, 0, B // 2 - 1, False)
            body(B - 1, 1, B // 2 - 1, True)


def attend_counts(count, sem):
    return dict(
        once=sem("at_once"), rows=sem("at_rows"),
        stack=[count(f"at_stack{i}", 16 * 2 * len(TERMS)) for i in range(2)], res=count("at_res", 16),
        nm_out=[count(f"at_nm_out{i}", 16) for i in range(2)], nm_in=[count(f"at_nm_in{i}", 16) for i in range(2)], x1_out=count("at_x1_out", 16),
        v_in=count("at_v_in", 16), v=count("at_v", H // 4), v_ones=sem("at_v_ones"),
        s=count("at_s", NS), mx=count("at_mx", NS, 3), nm=count("at_nm", 10), nmp=count("at_nmp", 2), nmT=count("at_nmT", 2),
        st=count("at_st", 2 * CH), ex=count("at_ex", 2 * CH), mul=count("at_mul", CH), pv=count("at_pv", CH // 2),
        o=count("at_o", 4), op=count("at_op", 4), rc=count("at_rc", 4), on=count("at_on", 4),
        onp=count("at_onp", EC), onT=count("at_onT", EC), wo=count("at_wo", 2), x1=count("at_x1", 2),
    )


NH2 = NS // 2
CATCH_UP = 4


def score_tiles(k, first):
    if not first:
        return [(1, 2 * k), (1, 2 * k + 1)]
    if k < CATCH_UP:
        return [(0, NS - 4 * (CATCH_UP - k) + i) for i in range(4)]
    if k < CH // 2:
        return [(1, j) for j in range(*(NH2 * (k + i - CATCH_UP) // (CH // 2 - CATCH_UP) for i in range(2)))]
    return [(1, 2 * k), (1, 2 * k + 1)]


AT_MAX, AT_MAX_BACK = CH // 2 - 1, CH // 2 + 1


def second_half_at(first):
    return (CATCH_UP, CATCH_UP + 1, CATCH_UP + 2) if first else (0, 2, 3)


AT_O_LAST, AT_ON0, AT_ON1, AT_WO0, AT_WO1 = 4, 6, 8, 10, 11
AT_O = [12, 20, 28]


def load_stacks(sp, sc, qs, ks, loaded, n, odd, half):
    heads = slice(H // 2 * half, H // 2 * (half + 1))
    for i, (qi, ki) in enumerate(TERMS):
        for k, dst, part in ((0, qs, qi), (1, ks, ki)):
            src = sc["parts"][bass.ds(n, 1), k, heads.start * D:heads.stop * D, part, :].rearrange("o (h d) s -> (o d) h s", d=D)
            sp.dma_start(dst[i * D:(i + 1) * D, odd, heads, :], src).then_inc(loaded[half].sem, 16)


def near_range(kb):
    lo, hi = kb * P + NEAR_LO, kb * P + NEAR_LO + NEAR_W
    return max(lo, 0), min(hi, S), max(lo, 0) - lo


def attend(nc, a, sc, c, passed, ident, identb, near, qs, ks, acc, acc_in):
    with ExitStack() as es:
        def sb(name, shape, dt=F32):
            return es.enter_context(nc.sbuf_tensor("at_" + name, shape, dt))

        def ps(name, shape, dt=F32):
            return es.enter_context(nc.psum_tensor("at_" + name, shape, dt))

        wo = sb("wo", [P, EC, E])
        vc, vt = sb("vc", [P, H // 4, TB, 4 * D]), sb("vt", [P, TB, H, VW])
        pr = [sb(f"pr{i}", [P, 2, S]) for i in range(4)]
        o_sb = [sb(f"o{i}", [P, S]) for i in range(2)]
        rc = sb("rc", [P, TB, 4])
        on = sb("on", [P, TB, E])
        onT = sb("onT", [P, EC, S])
        res, x1 = sb("res", [P, TB, E]), sb("x1", [P, TB, E])
        nm, nmr, nmb, nmT = sb("nm", [P, NS]), sb("nmr", [P, 2, NS]), sb("nmb", [P, 3, NS], BF16), sb("nmT", [NH2, 2, 3, P], BF16)
        sp_ = [ps(f"s{i}", [P, S]) for i in range(3)]
        st_ = [ps(f"st{i}", [P, S]) for i in range(3)]
        op = ps("o", [P, S])
        mp = ps("m", [P, TB, P])
        mpb = mp[:, :, :].rearrange("p a b -> p (a b)").bitcast(BF16)
        block = es.enter_context(nc.Block())
        x_rows = a["x"].rearrange("(b t p) e -> b p t e", b=B, t=TB)

        @block.sync
        def _(sp):
            def stacks(n, odd, half):
                load_stacks(sp, sc, qs, ks, c["stack"], n, odd, half)

            def maxima(n, odd, i):
                sp.wait_ge(c["nmT"].sem, c["nmT"].value(n, i + 1))
                sp.dma_start(sc["negmax"][bass.ds(n, 1), :, NH2 * i:NH2 * (i + 1)].rearrange("o t c q -> (o c) t q"),
                             nmT[:, i, :, :]).then_inc(c["nm_out"][i].sem, 16)
                sp.wait_ge(c["nm_out"][i].sem, c["nm_out"][i].value(n))
                sp.dma_start(qs[ROW_MAX:ROW_FAR, odd, H // 2 * i:H // 2 * (i + 1), :].rearrange("t h s -> t (h s)"),
                             sc["negmax"][bass.ds(n, 1), :, NH2 * i:NH2 * (i + 1)].rearrange("o t c q -> (o t) (c q)")).then_inc(c["nm_in"][i].sem, 16)

            def values_in(n):
                sp.dma_start(vc[:, :, :, :], sc["v"][bass.ds(n, 1)].rearrange("o p g k w -> (o p) g k w")).then_inc(c["v_in"].sem, 16)

            def store(n):
                sp.wait_ge(c["x1"].sem, c["x1"].value(n))
                sp.dma_start(sc["x1"][bass.ds(n, 1)].rearrange("o p t e -> (o p) t e"), x1[:, :, :]).then_inc(c["x1_out"].sem, 16)

            def residual(n):
                sp.wait_ge(c["x1"].sem, c["x1"].value(n - 1))
                sp.dma_start(res[:, :, :], x_rows[bass.ds(n, 1)].rearrange("o p t e -> (o p) t e")).then_inc(c["res"].sem, 16)

            def batch(n, odd, first, last, before_last=False):
                if not last:
                    sp.wait_ge(c["v"].sem, c["v"].value(n))
                    values_in(n + 1)
                maxima(n, odd, 1)
                if not last:
                    sp.wait_ge(c["st"].sem, c["st"].value(n - 1))
                    stacks(n + 1, 1 - odd, 1)
                if not first:
                    store(n - 1)
                residual(n)
                if not last:
                    if not before_last:
                        sp.wait_ge(c["st"].sem, c["st"].value(n, CH))
                        stacks(n + 2, odd, 0)
                    maxima(n + 1, 1 - odd, 0)

            sp.dma_start(wo[:, :, :], a["wo"].rearrange("(c p) e -> p c e", p=P)).then_inc(c["once"], 16)
            values_in(0)
            stacks(0, 0, 1)
            maxima(0, 0, 0)
            stacks(1, 1, 0)
            batch(0, 0, True, False)
            with sp.Fori(0, B // 2 - 2) as it:
                for u in range(2):
                    batch(it * 2 + (1 + u), 1 - u, False, False)
            batch(B - 3, 1, False, False)
            batch(B - 2, 0, False, False, True)
            batch(B - 1, 1, False, True)
            sp.wait_ge(c["x1_out"].sem, c["x1_out"].value(1))
            for n in range(2):
                sp.dma_start(acc[:, n, :, :], sc["x1"][n]).then_inc(acc_in[n].sem, 16)
            store(B - 1)
            sp.wait_ge(c["x1_out"].sem, c["x1_out"].value(B - 1))

        @block.vector
        def _(v):
            def row_max(n, j):
                v.wait_ge(c["s"].sem, c["s"].value(n, j + 1))
                if j == 0:
                    v.wait_ge(c["nm"].sem, c["nm"].value(n - 1))
                v.reduce_max(nm[:, j:j + 1], sp_[j % 3][:, :], X, negate=True).then_inc(c["mx"].sem, 1)

            def split_max(n, i):
                k, at = c["nm"], slice(NH2 * i, NH2 * (i + 1))
                v.wait_ge(c["mx"].sem, c["mx"].value(n, NH2 * (i + 1)))
                v.wait_ge(c["nmp"].sem, c["nmp"].value(n - 1, i + 1))
                v.tensor_copy(nmb[:, 0, at], nm[:, at]).then_inc(k.sem, 1)
                v.wait_ge(k.sem, k.value(n, 5 * i + 1))
                v.tensor_sub(nmr[:, 0, at], nm[:, at], nmb[:, 0, at]).then_inc(k.sem, 1)
                v.wait_ge(k.sem, k.value(n, 5 * i + 2))
                v.tensor_copy(nmb[:, 1, at], nmr[:, 0, at]).then_inc(k.sem, 1)
                v.wait_ge(k.sem, k.value(n, 5 * i + 3))
                v.tensor_sub(nmr[:, 1, at], nmr[:, 0, at], nmb[:, 1, at]).then_inc(k.sem, 1)
                v.wait_ge(k.sem, k.value(n, 5 * i + 4))
                v.tensor_copy(nmb[:, 2, at], nmr[:, 1, at]).then_inc(k.sem, 1)

            def normalise(n, g):
                v.wait_ge(c["op"].sem, c["op"].value(n, g + 1))
                heads = mp[:, :, :].rearrange("p t (h w) -> p t h w", w=VW)
                v.wait_ge(c["on"].sem, c["on"].value(n, g))
                v.reciprocal(rc[:, :, :], heads[:, :, :, D]).then_inc(c["rc"].sem, 1)
                v.wait_ge(c["rc"].sem, c["rc"].value(n, g + 1))
                v.wait_ge(c["onp"].sem, c["onp"].value(n - 1))
                v.tensor_tensor(on[:, :, 4 * g * D:4 * (g + 1) * D].rearrange("p t (h d) -> p t h d", d=D), heads[:, :, :, 0:D],
                                rc[:, :, :].rearrange("p t (h o) -> p t h o", o=1).to_broadcast([P, TB, 4, D]), ALU.mult).then_inc(c["on"].sem, 1)

            def add_residual(n, i):
                v.wait_ge(c["wo"].sem, c["wo"].value(n, i + 1))
                if i == 0:
                    v.wait_ge(c["res"].sem, c["res"].value(n))
                    v.wait_ge(c["x1_out"].sem, c["x1_out"].value(n - 1))
                v.tensor_add(x1[:, 2 * i:2 * i + 2, :], mp[:, :, :].rearrange("p a b -> p (a b)").rearrange("p (t e) -> p t e", e=E),
                             res[:, 2 * i:2 * i + 2, :]).then_inc(c["x1"].sem, 1)

            def batch(n, first, last):
                for k in range(CH):
                    if k == second_half_at(first)[0]:
                        split_max(n, 1)
                    if not last:
                        for ahead, j in score_tiles(k, first):
                            row_max(n + ahead, j)
                        if k == AT_MAX:
                            split_max(n + 1, 0)
                    if not first and k == AT_O_LAST + 1:
                        normalise(n - 1, 3)
                    if not first and k in (AT_WO0, AT_WO1):
                        add_residual(n - 1, (AT_WO0, AT_WO1).index(k))
                    if k - 1 in AT_O:
                        normalise(n, AT_O.index(k - 1))

            for j in range(NH2):
                row_max(0, j)
            split_max(0, 0)
            for j in range(NH2, NS - 4 * CATCH_UP):
                row_max(0, j)
            batch(0, True, False)
            with v.Fori(1, B - 1) as n:
                batch(n, False, False)
            batch(B - 1, False, True)
            normalise(B - 1, 3)
            for i in range(2):
                add_residual(B - 1, i)

        @block.scalar
        def _(s):
            def exp(n, k):
                s.wait_ge(c["pv"].sem, c["pv"].value(n, (k - 4) // 2 + 1))
                for j in range(2):
                    m = 2 * k + j
                    s.wait_ge(c["st"].sem, c["st"].value(n, m + 1))
                    s.activation(pr[k % 4][:, j, :], st_[m % 3][:, :], ACT.Exp).then_inc(c["ex"].sem, 1)

            def o_out(n, g):
                s.wait_ge(c["pv"].sem, c["pv"].value(n, 4 * g + 4))
                s.wait_ge(c["op"].sem, c["op"].value(n, g - 1))
                s.copy(o_sb[g % 2][:, :], op[:, :]).then_inc(c["o"].sem, 1)

            def v_out(n, g):
                if g == 0:
                    s.wait_ge(c["v_in"].sem, c["v_in"].value(n))
                s.copy(vt[:, :, 4 * g:4 * g + 4, 0:D], vc[:, g, :, :].rearrange("p k (h d) -> p k h d", d=D)).then_inc(c["v"].sem, 1)

            def onT_out(n, i):
                s.wait_ge(c["onp"].sem, c["onp"].value(n, i + 1))
                s.wait_ge(c["wo"].sem, c["wo"].value(n - 1))
                s.copy(onT[:, i, :], mp[:, :, :].rearrange("p a b -> p (a b)")).then_inc(c["onT"].sem, 1)

            def nmT_out(n, i):
                s.wait_ge(c["nmp"].sem, c["nmp"].value(n, i + 1))
                s.wait_ge(c["nm_out"][i].sem, c["nm_out"][i].value(n - 1))
                s.copy(nmT[:, i, :, :].rearrange("c t q -> c (t q)"), mpb[0:NH2, 0:3 * P]).then_inc(c["nmT"].sem, 1)

            def batch(n, first, last):
                for k in range(CH):
                    if not first and k == 2:
                        o_out(n - 1, 3)
                        v_out(n, 3)
                    if not first and k in (AT_ON0 + 1, AT_ON1 + 1):
                        onT_out(n - 1, (AT_ON0 + 1, AT_ON1 + 1).index(k))
                    if k in (10, 18, 26):
                        o_out(n, (10, 18, 26).index(k))
                        if not last:
                            v_out(n + 1, (10, 18, 26).index(k))
                    if k == second_half_at(first)[2]:
                        nmT_out(n, 1)
                    if not last and k == AT_MAX_BACK + 1:
                        nmT_out(n + 1, 0)
                    exp(n, k)

            s.wait_ge(c["v_ones"], 2)
            for g in range(4):
                v_out(0, g)
            nmT_out(0, 0)
            batch(0, True, False)
            with s.Fori(1, B - 1) as n:
                batch(n, False, False)
            batch(B - 1, False, True)
            o_out(B - 1, 3)
            for i in range(EC):
                onT_out(B - 1, i)

        @block.gpsimd
        def _(g_):
            def batch(n):
                for k in range(CH):
                    g, kb, two = k // 8, k // 2 % TB, k % 2
                    lo, hi, at = near_range(kb)
                    h = 4 * g + 2 * two
                    g_.wait_ge(c["ex"].sem, c["ex"].value(n, 2 * k + 2))
                    g_.tensor_tensor(pr[k % 4][:, :, lo:hi], pr[k % 4][:, :, lo:hi], near[:, h:h + 2, at:at + hi - lo],
                                     ALU.mult).then_inc(c["mul"].sem, 1)

            g_.memset(vt[:, :, :, D:VW], 0.0).then_inc(c["v_ones"], 1)
            g_.wait_ge(c["v_ones"], 1)
            g_.memset(vt[:, :, :, D:D + 1], 1.0).then_inc(c["v_ones"], 1)
            with g_.Fori(0, B) as n:
                batch(n)

        @block.tensor
        def _(t):
            def scores(n, odd, j):
                h, qb = j // TB, j % TB
                if j == 0 or j >= 3:
                    t.wait_ge(c["mx"].sem, c["mx"].value(n, max(j - 2, 0)))
                if j in (0, NH2):
                    stack = c["stack"][j // NH2]
                    t.wait_ge(stack.sem, stack.value(n))
                t.matmul(sp_[j % 3][:, :], qs[0:KQ, odd, h, qb * P:(qb + 1) * P], ks[0:KQ, odd, h, :], start=True, stop=True).then_inc(c["s"].sem, 1)

            def chunk(n, odd, k, between):
                g, kb, two = k // 8, k // 2 % TB, k % 2
                if k in (0, CH // 2):
                    nm_in = c["nm_in"][k // (CH // 2)]
                    t.wait_ge(nm_in.sem, nm_in.value(n))
                for j in range(2):
                    h = 4 * g + 2 * two + j
                    if j:
                        between()
                    m = 2 * k + j
                    if m == 0 or m >= 3:
                        t.wait_ge(c["ex"].sem, c["ex"].value(n, max(m - 2, 0)))
                    t.matmul(st_[m % 3][:, :], ks[0:KS, odd, h, kb * P:(kb + 1) * P], qs[0:KS, odd, h, :],
                             start=True, stop=True).then_inc(c["st"].sem, 1)

            def values(n, i):
                g, kb = i // TB, i % TB
                t.wait_ge(c["mul"].sem, c["mul"].value(n, 2 * i + 2))
                if kb == 0:
                    t.wait_ge(c["v"].sem, c["v"].value(n, g + 1))
                    t.wait_ge(c["o"].sem, c["o"].value(n, g))
                for hh in range(4):
                    k = 2 * i + hh // 2
                    last = t.matmul(op[32 * hh:32 * hh + VW, :], vt[:, kb, 4 * g + hh, :], pr[k % 4][:, hh % 2, :],
                                    start=(kb == 0), stop=(kb == TB - 1))
                last.then_inc(c["pv"].sem, 1)

            def o_back(n, g, misc_free):
                t.wait_ge(c["o"].sem, c["o"].value(n, g + 1))
                misc_free()
                for q in range(TB):
                    last = t.transpose(mp[:, q, :], o_sb[g % 2][:, q * P:(q + 1) * P], ident[:, :])
                last.then_inc(c["op"].sem, 1)

            def on_back(n, i):
                if i == 0:
                    t.wait_ge(c["on"].sem, c["on"].value(n))
                else:
                    t.wait_ge(c["onT"].sem, c["onT"].value(n, 1))
                for q in range(TB):
                    last = t.transpose(mp[:, q, :], on[:, q, i * P:(i + 1) * P], ident[:, :])
                last.then_inc(c["onp"].sem, 1)

            def project_out(n, i):
                if i == 0:
                    t.wait_ge(c["onT"].sem, c["onT"].value(n))
                else:
                    t.wait_ge(c["x1"].sem, c["x1"].value(n, 1))
                out = mp[:, :, :].rearrange("p a b -> p (a b)")
                for q in range(2):
                    for i2 in range(EC):
                        last = t.matmul(out[:, q * E:(q + 1) * E], onT[:, i2, (2 * i + q) * P:(2 * i + q + 1) * P], wo[:, i2, :],
                                        start=(i2 == 0), stop=(i2 == EC - 1))
                last.then_inc(c["wo"].sem, 1)

            def maxima_back(n, i, misc_free):
                t.wait_ge(c["nm"].sem, c["nm"].value(n, 5 * (i + 1)))
                misc_free()
                stand_alone(t, passed)
                for p in range(3):
                    last = t.transpose(mpb[0:NH2, p * P:(p + 1) * P], nmb[:, p, NH2 * i:NH2 * (i + 1)], identb[:, :])
                last.then_inc(c["nmp"].sem, 1)

            def batch(n, odd, first, last):
                for k in range(CH):
                    todo = [] if last else score_tiles(k, first)

                    def one():
                        if todo:
                            ahead, j = todo.pop(0)
                            scores(n + ahead, (odd + ahead) % 2, j)

                    chunk(n, odd, k, one)
                    one()
                    if k == 1 and not first:
                        values(n - 1, CH // 2 - 1)
                    if k % 2 and k >= 3:
                        values(n, (k - 3) // 2)
                    while todo:
                        one()
                    if k == second_half_at(first)[1]:
                        maxima_back(n, 1, lambda: t.wait_ge(c["nmT"].sem, c["nmT"].value(n, 1)) if first else
                                    t.wait_ge(c["on"].sem, c["on"].value(n - 1, 3)))
                    if not first:
                        if k == AT_O_LAST:
                            o_back(n - 1, 3, lambda: (t.wait_ge(c["nmT"].sem, c["nmT"].value(n)),
                                                      t.wait_ge(c["on"].sem, c["on"].value(n - 1, 3))))
                        if k in (AT_ON0, AT_ON1):
                            on_back(n - 1, (AT_ON0, AT_ON1).index(k))
                        if k in (AT_WO0, AT_WO1):
                            project_out(n - 1, (AT_WO0, AT_WO1).index(k))
                    if k == AT_MAX_BACK and not last:
                        maxima_back(n + 1, 0, lambda: t.wait_ge(c["on"].sem, c["on"].value(n, 1)))
                    if k in AT_O:
                        g = AT_O.index(k)

                        def read():
                            if g == 0 and first:
                                t.wait_ge(c["nmT"].sem, c["nmT"].value(n))
                            elif g == 0:
                                t.wait_ge(c["x1"].sem, c["x1"].value(n - 1))
                            elif g == 1 and not last:
                                t.wait_ge(c["nmT"].sem, c["nmT"].value(n + 1, 1))
                            else:
                                t.wait_ge(c["on"].sem, c["on"].value(n, g))

                        o_back(n, g, read)

            for j in range(NH2):
                scores(0, 0, j)
            t.wait_ge(c["once"], 16)
            t.wait_ge(c["rows"], 64)
            maxima_back(0, 0, lambda: None)
            for j in range(NH2, NS - 4 * CATCH_UP):
                scores(0, 0, j)
            batch(0, 0, True, False)
            with t.Fori(0, B // 2 - 1) as it:
                for u in range(2):
                    batch(it * 2 + (1 + u), 1 - u, False, False)
            batch(B - 1, 1, False, True)
            values(B - 1, CH // 2 - 1)
            o_back(B - 1, 3, lambda: t.wait_ge(c["on"].sem, c["on"].value(B - 1, 3)))
            for i in range(EC):
                on_back(B - 1, i)
            for i in range(2):
                project_out(B - 1, i)


def route_counts(count, sem):
    return dict(
        once=sem("rt_once"), init=sem("rt_init"), end=sem("rt_end"), pads=sem("rt_pads"), padrow=sem("rt_padrow"),
        tab=sem("rt_tab"), tiles=sem("rt_tiles"), dummy=sem("rt_dummy"),
        x_in=[count(f"rt_x_in{u}", 16) for u in range(2)], base_in=[count(f"rt_base_in{u}", 16) for u in range(2)],
        base_out=[count(f"rt_base_out{u}", 16) for u in range(2)],
        scat=[count(f"rt_scat{u}", 16 * TB * TOPK, 0) for u in range(2)],
        stats=count("rt_stats", 8), rstd=count("rt_rstd", 2), xn=count("rt_xn", TB), tp=count("rt_tp", 2),
        xT=count("rt_xT", 2), lg=count("rt_lg"), ex=count("rt_ex"), r=count("rt_r", R_STEPS),
        cnt=count("rt_cnt"), up=count("rt_up", TB), silu=count("rt_silu", TB), h=count("rt_h", TB),
        ht=count("rt_ht", TB), hT=count("rt_hT", TB), dn=count("rt_dn", TB), base=count("rt_base", TB), rows=count("rt_rows", TB),
    )


R_STEPS = 46


def route(nc, a, sc, c, passed, ident, tiles, acc, weights, weights_in):
    with ExitStack() as es:
        def sb(name, shape, dt=F32):
            return es.enter_context(nc.sbuf_tensor("rt_" + name, shape, dt))

        def pair(name, shape, dt=F32):
            return [sb(f"{name}{u}", shape, dt) for u in range(2)]

        def ps(name, shape, dt=F32):
            return es.enter_context(nc.psum_tensor("rt_" + name, shape, dt))

        gate, wsh, wsd = sb("gate", [P, EC, NE]), sb("wsh", [P, EC, 2 * SI]), sb("wsd", [P, SI // P, E])
        ebias, earlier, regions = sb("ebias", [P, NE]), sb("earlier", [P, NG, NG]), sb("regions", [P, NE])
        before, ones = sb("before", [P, P], BF16), sb("ones", [P, P], BF16)
        before32, half = sb("before32", [P, P]), sb("half", [P, TB])
        rows = pair("rows", [P, TB, TOPK, ROWW])
        x, base, xn, xT = ([acc[:, 2 * i + u, :, :] for u in range(2)] for i in range(4))
        xT = [b.rearrange("p t e -> p (t e)").rearrange("p (c s) -> p c s", c=EC) for b in xT]
        st, mv, var, rstd = pair("st", [P, TB, 6]), pair("mv", [P, TB, 2]), pair("var", [P, TB]), pair("rstd", [P, TB])
        slots = pair("slots", [P, TB, TOPK], U32)
        ex, sig, sfc = sb("ex", [P, TB, NE]), sb("sig", [P, TB, NE]), sb("sfc", [P, TB, NE])
        gmax, gcmp, geq, rank = sb("gmax", [P, TB, NG]), sb("gcmp", [P, TB, NG, NG]), sb("geq", [P, TB, NG, NG]), sb("rank", [P, TB, NG])
        cand, left, top = sb("cand", [P, TB, NE + 8]), sb("left", [P, TB, NE + 8]), sb("top", [P, TB, 8])
        sel, selb, wgt = sb("sel", [P, TB, NE]), sb("selb", [P, TB, NE], BF16), sb("wgt", [P, TB, NE])
        wsum, winv = sb("wsum", [P, TB]), sb("winv", [P, TB])
        cnt, key, ktop = sb("cnt", [P, TB + 1, NE]), sb("key", [P, TB, NE]), sb("ktop", [P, TB, 8])
        hit, dst = sb("hit", [P, TB, TOPK, NE]), sb("dst", [P, TB, TOPK], I32)
        sg, h, hT = pair("sg", [P, SI]), pair("h", [P, SI]), pair("hT", [P, SI // P, P])
        padrow, padidx = sb("padrow", [P, ROWW]), sb("padidx", [P, NE], I32)
        ends, starts, ntile = sb("ends", [P, NE]), sb("starts", [P, NE]), sb("ntile", [P, NE])
        nti, zero = sb("nti", [P, NE], I32), sb("zero", [P, NE])
        index, ind, ind2 = sb("index", [P, 2]), sb("ind", [P, 2, NE]), sb("ind2", [P, 2, NE])
        num, start, tab_i = sb("num", [P, 2]), sb("start", [P, 2]), sb("tab_i", [P, 2, 2], I32)
        tp = [ps(f"tp{i}", [P, S]) for i in range(EC)]
        lp = ps("l", [P, 4, TB, NE])
        up = [ps(f"up{i}", [P, 2, SI]) for i in range(2)]
        hp = ps("h", [P, 2 * SI // P, P])
        dp = [ps(f"d{i}", [P, 2 * E]) for i in range(2)]
        block = es.enter_context(nc.Block())

        def loop(eng, body):
            for u in range(2):
                body(u, u, 0, u == 0, False)
            with eng.Fori(1, B // 2 - 1) as it:
                for u in range(2):
                    body(it * 2 + u, u, it, False, False)
            for u in range(2):
                body(B - 2 + u, u, B // 2 - 1, False, True)

        def pad(eng, experts):
            with eng.Fori(experts.start // 4, experts.stop // 4) as e4:
                for e in range(4):
                    at = eng.value_load(padidx[0:1, bass.ds(e4 * 4 + e, 1)], min_val=0, max_val=PADS - P)
                    eng.dma_start(sc["slots"][bass.ds(at, P), :], padrow[:, :]).then_inc(c["pads"], 16)

        @block.sync
        def _(sp):
            def load(n, u):
                sp.dma_start(x[u][:, :, :], sc["x1"][bass.ds(n, 1)].rearrange("o p t e -> (o p) t e")).then_inc(c["x_in"][u].sem, 16)

            for dst_, src in ((gate, a["gateT"].rearrange("(c p) e -> p c e", p=P)), (wsh, a["shared"]), (wsd, a["shared_dn"]),
                              (ebias, a["ebias"].to_broadcast([P, NE])), (earlier, a["earlier"].rearrange("p (i j) -> p i j", j=NG)),
                              (regions, a["regions"]), (before32, a["before"])):
                sp.dma_start(dst_[tuple(slice(None) for _ in dst_.shape)], src).then_inc(c["once"], 16)

            def load_base(n, u):
                sp.dma_start(base[u][:, :, :], sc["x1"][bass.ds(n, 1)].rearrange("o p t e -> (o p) t e")).then_inc(c["base_in"][u].sem, 16)

            def store_base(n, u, it):
                sp.wait_ge(c["base"].sem, c["base"].value(n))
                sp.dma_start(sc["base"][bass.ds(n, 1)].rearrange("o p t e -> (o p) t e"), base[u][:, :, :]).then_inc(c["base_out"][u].sem, 16)

            def body(n, u, it, first, last):
                if not last:
                    sp.wait_ge(c["xn"].sem, c["xn"].value(n))
                    load(n + 2, u)
                if not first:
                    store_base(n - 1, 1 - u, it + u - 1)
                    sp.wait_ge(c["base_out"][1 - u].sem, c["base_out"][1 - u].value(it + u - 1))
                    if not (last and u):
                        load_base(n + 1, 1 - u)
                part = bass.ds(n * (NE // B * WE), NE // B * WE)
                sp.dma_start(weights[:, part], a["experts"][:, part]).then_inc(weights_in, 16)

            for u in range(2):
                load_base(u, u)
            loop(sp, body)
            sp.wait_ge(c["end"], T_LAST)
            sp.dma_start(sc["tiletab"].rearrange("w p c -> p w c"), tab_i[:, :, :]).then_inc(c["tab"], 16)
            sp.wait_ge(c["padrow"], 1)
            sp.dma_start(sc["slots"][PADS:PADS + P, :], padrow[:, :]).then_inc(c["dummy"], 16)
            pad(sp, range(NE * 3 // 8, NE))
            sp.wait_ge(c["tab"], 16)
            sp.dma_start(tiles[:, :, :], sc["tiletab"].rearrange("w p c -> (w p c)").rearrange("(o w i) -> o w i", o=1, w=2)).then_inc(c["tiles"], 16)
            store_base(B - 1, 1, B // 2 - 1)
            for u in range(2):
                sp.wait_ge(c["base_out"][u].sem, c["base_out"][u].value(B // 2 - 1))
            sp.wait_ge(c["tiles"], 16)
            sp.wait_ge(c["dummy"], 16)
            sp.wait_ge(c["pads"], 16 * NE)

        @block.gpsimd
        def _(g):
            init = c["init"]
            g.memset(half[:, :], -0.5).then_inc(init, 1)
            g.memset(ones[:, :], 1.0).then_inc(init, 1)
            g.memset(cand[:, :, :], SENT).then_inc(init, 1)
            g.memset(cnt[:, :, :], 0.0).then_inc(init, 1)
            g.memset(zero[:, :], 0.0).then_inc(init, 1)
            for u in range(2):
                g.memset(rows[u][:, :, :, E + 2:ROWW], 0.0).then_inc(init, 1)
            g.memset(padrow[:, :], 0.0).then_inc(init, 1)
            g.iota(dst[:, :, :], [[P * TOPK, TB], [1, TOPK]], base=0, channel_multiplier=TOPK).then_inc(init, 1)
            g.iota(index[:, :], [[1, 2]], base=0, channel_multiplier=2, allow_small_or_imprecise_dtypes=True).then_inc(init, 1)
            g.wait_ge(init, 10)
            g.memset(padrow[:, E + 1:E + 2].bitcast(I32), 1 << 20).then_inc(c["padrow"], 1)

            def norm(n, u):
                g.wait_ge(c["stats"].sem, c["stats"].value(n))
                stand_alone(g, passed)
                g.tensor_scalar(var[u][:, :], mv[u][:, :, 1], EPS, None, ALU.add).then_inc(c["rstd"].sem, 1)
                g.wait_ge(c["rstd"].sem, c["rstd"].value(n, 1))
                g.tensor_tensor(rstd[u][:, :], var[u][:, :], half[:, :], ALU.pow).then_inc(c["rstd"].sem, 1)

            def body(n, u, it, first, last):
                g.wait_ge(c["r"].sem, c["r"].value(n))
                g.wait_ge(c["rows"].sem, c["rows"].value(n))
                stand_alone(g, passed)
                for t in range(TB):
                    for j in range(TOPK):
                        g.indirect_dma_start(sc["slots"], bass.IndirectOffsetOnAxis(ap=slots[u][:, t, j:j + 1], axis=0),
                                             rows[u][:, t, j, :], None).then_inc(c["scat"][u].sem, 16)
                    if t == 0 and not last:
                        norm(n + 2, u)

            norm(0, 0)
            norm(1, 1)
            loop(g, body)
            for u in range(2):
                g.wait_ge(c["scat"][u].sem, c["scat"][u].value(B // 2 - 1))

        @block.vector
        def _(v):
            def scattered(u, it):
                if not isinstance(it, int) or it:
                    v.wait_ge(c["scat"][u].sem, c["scat"][u].value(it - 1))

            def stats(n, u, it):
                v.wait_ge(c["x_in"][u].sem, c["x_in"][u].value(it))
                v.wait_ge(c["xn"].sem, c["xn"].value(n - 2))
                for t in range(TB):
                    v.bn_stats(st[u][:, t, :], x[u][:, t, :]).then_inc(c["stats"].sem, 1)
                v.wait_ge(c["stats"].sem, c["stats"].value(n, TB))
                stand_alone(v, passed)
                for t in range(TB):
                    v.bn_aggr(mv[u][:, t, :], st[u][:, t, :]).then_inc(c["stats"].sem, 1)

            def normalise(n, u):
                v.wait_ge(c["rstd"].sem, c["rstd"].value(n))
                v.wait_ge(c["rows"].sem, c["rows"].value(n - 2))
                v.wait_ge(c["tp"].sem, c["tp"].value(n - 2))
                for t in range(TB):
                    v.tensor_scalar(xn[u][:, t, :], x[u][:, t, :], mv[u][:, t, 0:1],
                                    rstd[u][:, t:t + 1], ALU.subtract, ALU.mult).then_inc(c["xn"].sem, 1)

            def gate_hidden(n, t):
                v.wait_ge(c["silu"].sem, c["silu"].value(n, t + 1))
                v.wait_ge(c["ht"].sem, c["ht"].value(n, t - 1))
                v.tensor_tensor(h[t % 2][:, :], sg[t % 2][:, :], up[t % 2][:, 1, :], ALU.mult).then_inc(c["h"].sem, 1)

            def add_shared(n, u, it, t):
                if t == 0:
                    v.wait_ge(c["base_in"][u].sem, c["base_in"][u].value(it))
                v.wait_ge(c["dn"].sem, c["dn"].value(n, t + 1))
                v.tensor_tensor(base[u][:, t, :], dp[t % 2][:, 0:E], base[u][:, t, :], ALU.add).then_inc(c["base"].sem, 1)

            def choose(n, u, it, between):
                k = c["r"]
                done, calls = [0], [0]

                def step(*ops):
                    if done[0]:
                        v.wait_ge(k.sem, k.value(n, done[0]))
                    if len(ops) == TB:
                        stand_alone(v, passed)
                    for op in ops:
                        op().then_inc(k.sem, 1)
                        done[0] += 1
                    calls[0] += 1
                    between.get(calls[0], lambda: None)()

                v.wait_ge(k.sem, k.value(n - 1))
                v.wait_ge(c["ex"].sem, c["ex"].value(n))
                groups = lambda ap: ap.rearrange("p t (g s) -> p t g s", s=GS)
                last1 = lambda ap: ap.rearrange("p t (g o) -> p t g o", o=1)
                step(lambda: v.tensor_scalar(sig[:, :, :], ex[:, :, :], 1.0, None, ALU.add))
                step(lambda: v.reciprocal(sig[:, :, :], sig[:, :, :]))
                step(lambda: v.tensor_tensor(sfc[:, :, :], sig[:, :, :],
                                             ebias[:, :].rearrange("p (o e) -> p o e", o=1).to_broadcast([P, TB, NE]), ALU.add))
                step(lambda: v.tensor_reduce(gmax[:, :, :], groups(sfc[:, :, :]), X, ALU.max))
                gi = last1(gmax[:, :, :]).to_broadcast([P, TB, NG, NG])
                gj = gmax[:, :, :].rearrange("p t (o g) -> p t o g", o=1).to_broadcast([P, TB, NG, NG])
                step(lambda: v.tensor_tensor(gcmp[:, :, :, :], gj, gi, ALU.is_gt),
                     lambda: v.tensor_tensor(geq[:, :, :, :], gj, gi, ALU.is_equal))
                step(lambda: v.tensor_tensor(geq[:, :, :, :], geq[:, :, :, :],
                                             earlier[:, :, :].rearrange("p (o i) j -> p o i j", o=1).to_broadcast([P, TB, NG, NG]), ALU.mult))
                step(lambda: v.tensor_tensor(gcmp[:, :, :, :], gcmp[:, :, :, :], geq[:, :, :, :], ALU.add))
                step(lambda: v.tensor_reduce(rank[:, :, :], gcmp[:, :, :, :], X, ALU.add))
                step(lambda: v.tensor_scalar(rank[:, :, :], rank[:, :, :], float(TOPG), None, ALU.is_lt))
                step(lambda: v.tensor_tensor(cand[:, :, 0:NE].rearrange("p t (g s) -> p t g s", s=GS), groups(sfc[:, :, :]),
                                             last1(rank[:, :, :]).to_broadcast([P, TB, NG, GS]), ALU.mult))
                step(*[lambda t=t: v.max(top[:, t, :], cand[:, t, :]) for t in range(TB)])
                step(lambda: v.memset(top[:, :, TOPK:8], SENT))
                step(*[lambda t=t: v.match_replace(left[:, t, :], top[:, t, :], cand[:, t, :], 2 * SENT) for t in range(TB)])
                step(lambda: v.tensor_scalar(sel[:, :, :], left[:, :, 0:NE], 1.5 * SENT, None, ALU.is_lt))
                step(lambda: v.tensor_copy(selb[:, :, :], sel[:, :, :]),
                     lambda: v.tensor_tensor(wgt[:, :, :], sel[:, :, :], sig[:, :, :], ALU.mult))
                step(lambda: v.tensor_reduce(wsum[:, :], wgt[:, :, :], X, ALU.add))
                step(lambda: v.tensor_scalar(wsum[:, :], wsum[:, :], 1e-20, None, ALU.add))
                step(lambda: v.reciprocal(winv[:, :], wsum[:, :]))
                step(lambda: v.tensor_scalar(winv[:, :], winv[:, :], SCALE, None, ALU.mult))
                step(lambda: v.tensor_tensor(wgt[:, :, :], wgt[:, :, :],
                                             winv[:, :].rearrange("p (t o) -> p t o", o=1).to_broadcast([P, TB, NE]), ALU.mult),
                     lambda: v.tensor_copy(cnt[:, 0, :], cnt[:, TB, :]))
                v.wait_ge(c["cnt"].sem, c["cnt"].value(n))
                for t in range(TB):
                    step(lambda: v.tensor_tensor(cnt[:, t + 1, :], cnt[:, t, :], lp[:, 2, t, :], ALU.add))
                step(lambda: v.tensor_tensor(key[:, :, :], lp[:, 1, :, :], cnt[:, 0:TB, :], ALU.add))
                step(lambda: v.scalar_tensor_tensor(key[:, :, :], key[:, :, :], 1.0,
                                                    regions[:, :].rearrange("p (o e) -> p o e", o=1).to_broadcast([P, TB, NE]), ALU.add, ALU.add))
                step(lambda: v.tensor_tensor(key[:, :, :], key[:, :, :], sel[:, :, :], ALU.mult))
                step(*[lambda t=t: v.max(ktop[:, t, :], key[:, t, :]) for t in range(TB)])
                scattered(u, it)
                step(lambda: v.tensor_scalar(slots[u][:, :, :], ktop[:, :, 0:TOPK], -1.0, None, ALU.add),
                     lambda: v.tensor_tensor(hit[:, :, :, :], key[:, :, :].rearrange("p t (o e) -> p t o e", o=1).to_broadcast([P, TB, TOPK, NE]),
                                             last1(ktop[:, :, 0:TOPK]).to_broadcast([P, TB, TOPK, NE]), ALU.is_equal),
                     lambda: v.tensor_copy(rows[u][:, :, :, E + 1].bitcast(I32), dst[:, :, :]))
                step(lambda: v.tensor_tensor(hit[:, :, :, :], hit[:, :, :, :],
                                             wgt[:, :, :].rearrange("p t (o e) -> p t o e", o=1).to_broadcast([P, TB, TOPK, NE]), ALU.mult),
                     lambda: v.tensor_scalar(dst[:, :, :], dst[:, :, :], float(S * TOPK), None, ALU.add))
                step(lambda: v.tensor_reduce(rows[u][:, :, :, E], hit[:, :, :, :], X, ALU.add))
                assert done[0] == R_STEPS and all(i <= calls[0] for i in between), (done, calls)

            stats(0, 0, 0)
            normalise(0, 0)
            v.wait_ge(c["init"], 10)
            v.wait_ge(c["once"], 7 * 16)
            v.tensor_copy(before[:, :], before32[:, :]).then_inc(c["init"], 1)

            def body(n, u, it, first, last):
                between = {}
                if not first:
                    m = (n - 1, 1 - u, it + u - 1)
                    for t in range(TB):
                        between[HIDDEN_AT[t]] = lambda t=t: gate_hidden(m[0], t)
                        between[SHARED_AT[t]] = lambda t=t: add_shared(*m, t)
                if not (last and u):
                    stats(n + 1, 1 - u, it + u)
                    between[XN_AT] = lambda: normalise(n + 1, 1 - u)
                choose(n, u, it, between)

            loop(v, body)
            end = c["end"]
            last = cnt[:, TB, :]
            v.wait_ge(c["r"].sem, c["r"].value(B - 1))
            done = [0]

            def step(op):
                if done[0]:
                    v.wait_ge(end, done[0])
                op().then_inc(end, 1)
                done[0] += 1

            v.tensor_scalar(num[:, :], index[:, :], 0.5, None, ALU.mult).then_inc(c["init"], 1)
            v.wait_ge(c["init"], 12)
            step(lambda: v.scalar_tensor_tensor(padidx[:, :], last, num[:, 0:1], regions[:, :], ALU.add, ALU.add))
            step(lambda: v.tensor_scalar(nti[:, :], last, float(P - 1), None, ALU.add))
            step(lambda: v.tensor_scalar(nti[:, :], nti[:, :], 7, None, ALU.logical_shift_right))
            step(lambda: v.tensor_copy(ntile[:, :], nti[:, :]))
            step(lambda: v.tensor_tensor_scan(ends[:, :], ntile[:, :], zero[:, :], 0.0, ALU.add, ALU.add))
            e3 = lambda ap: ap.rearrange("p (o e) -> p o e", o=1).to_broadcast([P, 2, NE])
            i3 = lambda ap: ap.rearrange("p (c o) -> p c o", o=1).to_broadcast([P, 2, NE])
            step(lambda: v.tensor_tensor(ind[:, :, :], i3(index[:, :]), e3(ends[:, :]), ALU.is_ge))
            step(lambda: v.tensor_reduce(num[:, :], ind[:, :, :], X, ALU.add))
            step(lambda: v.tensor_tensor(ind2[:, :, :], ind[:, :, :], e3(ntile[:, :]), ALU.mult))
            step(lambda: v.tensor_reduce(start[:, :], ind2[:, :, :], X, ALU.add))
            step(lambda: v.tensor_scalar(tab_i[:, 1, :], num[:, :], float(NE - 1), float(WE), ALU.min, ALU.mult))
            step(lambda: v.tensor_sub(start[:, :], index[:, :], start[:, :]))
            step(lambda: v.tensor_scalar(start[:, :], start[:, :], float(P), None, ALU.mult))
            step(lambda: v.scalar_tensor_tensor(start[:, :], num[:, :], float(REG), start[:, :], ALU.mult, ALU.add))
            step(lambda: v.tensor_scalar(tab_i[:, 0, :], start[:, :], float(PADS), None, ALU.min))
            assert done[0] == T_LAST
            for t in range(TB + 1):
                if t < TB:
                    gate_hidden(B - 1, t)
                if t:
                    add_shared(B - 1, 1, B // 2 - 1, t - 1)

        @block.scalar
        def _(s):
            def xT_out(n, u):
                for i in range(EC):
                    s.wait_ge(c["tp"].sem, c["tp"].value(n, i + 1))
                    s.wait_ge(c["up"].sem, c["up"].value(n - 2))
                    s.copy(xT[u][:, i, :], tp[i][:, :]).then_inc(c["xT"].sem, 1)

            def copy_rows(n, u, it, t):
                if t == 0 and not (isinstance(it, int) and it == 0):
                    s.wait_ge(c["scat"][u].sem, c["scat"][u].value(it - 1))
                if t == 0:
                    s.wait_ge(c["xn"].sem, c["xn"].value(n))
                s.copy(rows[u][:, t, :, 0:E], xn[u][:, t:t + 1, :].to_broadcast([P, TOPK, E])).then_inc(c["rows"].sem, 1)

            def shared(n, t):
                if t < TB:
                    s.wait_ge(c["up"].sem, c["up"].value(n, t + 1))
                    s.wait_ge(c["h"].sem, c["h"].value(n, t - 1))
                    s.activation(sg[t % 2][:, :], up[t % 2][:, 0, :], ACT.Silu).then_inc(c["silu"].sem, 1)
                if t:
                    s.wait_ge(c["ht"].sem, c["ht"].value(n, t))
                    s.wait_ge(c["dn"].sem, c["dn"].value(n, t - 2))
                    s.copy(hT[(t - 1) % 2][:, :, :], hp[:, 0:SI // P, :]).then_inc(c["hT"].sem, 1)

            def body(n, u, it, first, last):
                s.wait_ge(c["lg"].sem, c["lg"].value(n))
                s.activation(ex[:, :, :], lp[:, 0, :, :], ACT.Exp, scale=-1.0).then_inc(c["ex"].sem, 1)
                for t in range(TB + 1):
                    if not first:
                        shared(n - 1, t)
                    if t:
                        copy_rows(n, u, it, t - 1)
                if not (last and u):
                    xT_out(n + 1, 1 - u)

            xT_out(0, 0)
            loop(s, body)
            for t in range(TB + 1):
                shared(B - 1, t)
            s.wait_ge(c["end"], 1)
            s.wait_ge(c["padrow"], 1)
            pad(s, range(NE * 3 // 8))

        @block.tensor
        def _(t_):
            def transposes(n, u):
                t_.wait_ge(c["xn"].sem, c["xn"].value(n))
                for i in range(EC):
                    t_.wait_ge(c["xT"].sem, c["xT"].value(n - 1, i + 1))
                    for t in range(TB):
                        last = t_.transpose(tp[i][:, t * P:(t + 1) * P], xn[u][:, t, i * P:(i + 1) * P], ident[:, :])
                    last.then_inc(c["tp"].sem, 1)

            def logits(n, u):
                t_.wait_ge(c["xT"].sem, c["xT"].value(n))
                t_.wait_ge(c["r"].sem, c["r"].value(n - 1, R_COUNTED))
                for t in range(TB):
                    for i in range(EC):
                        last = t_.matmul(lp[:, 0, t, :], xT[u][:, i, t * P:(t + 1) * P], gate[:, i, :], start=(i == 0), stop=(i == EC - 1))
                last.then_inc(c["lg"].sem, 1)

            def shared_up(n, u, t):
                t_.wait_ge(c["h"].sem, c["h"].value(n, t - 1))
                for i in range(EC):
                    last = t_.matmul(up[t % 2][:, :, :].rearrange("p a b -> p (a b)"), xT[u][:, i, t * P:(t + 1) * P], wsh[:, i, :],
                                     start=(i == 0), stop=(i == EC - 1))
                last.then_inc(c["up"].sem, 1)

            def hidden_back(n, t):
                t_.wait_ge(c["h"].sem, c["h"].value(n, t + 1))
                t_.wait_ge(c["hT"].sem, c["hT"].value(n, t))
                for i in range(SI // P):
                    last = t_.transpose(hp[:, i, :], h[t % 2][:, i * P:(i + 1) * P], ident[:, :])
                last.then_inc(c["ht"].sem, 1)

            def shared_down(n, t):
                t_.wait_ge(c["hT"].sem, c["hT"].value(n, t + 1))
                t_.wait_ge(c["base"].sem, c["base"].value(n, t - 1))
                for i in range(SI // P):
                    last = t_.matmul(dp[t % 2][:, 0:E], hT[t % 2][:, i, :], wsd[:, i, :], start=(i == 0), stop=(i == SI // P - 1))
                last.then_inc(c["dn"].sem, 1)

            def counts(n):
                t_.wait_ge(c["r"].sem, c["r"].value(n, R_SELECTED))
                flat = selb[:, :, :].rearrange("p t e -> p (t e)")
                t_.matmul(lp[:, 1, :, :].rearrange("p t e -> p (t e)"), before[:, :], flat, start=True, stop=True)
                t_.matmul(lp[:, 2, :, :].rearrange("p t e -> p (t e)"), ones[:, :], flat, start=True, stop=True).then_inc(c["cnt"].sem, 1)

            def body(n, u, it, first, last):
                for t in range(TB):
                    if not first:
                        shared_up(n - 1, 1 - u, t)
                        if t:
                            hidden_back(n - 1, t - 1)
                            shared_down(n - 1, t - 1)
                    if t == 2:
                        counts(n)
                if not first:
                    hidden_back(n - 1, TB - 1)
                    shared_down(n - 1, TB - 1)
                if not (last and u):
                    transposes(n + 1, 1 - u)
                    logits(n + 1, 1 - u)

            transposes(0, 0)
            t_.wait_ge(c["once"], 7 * 16)
            t_.wait_ge(c["init"], 11)
            logits(0, 0)
            loop(t_, body)
            for t in range(TB):
                shared_up(B - 1, 1, t)
                if t:
                    hidden_back(B - 1, t - 1)
                    shared_down(B - 1, t - 1)
            hidden_back(B - 1, TB - 1)
            shared_down(B - 1, TB - 1)


R_SELECTED = 22
R_COUNTED = 34
T_LAST = 14
HIDDEN_AT, SHARED_AT, XN_AT = [4, 9, 16, 24], [8, 14, 20, 28], 19


XR = 16
YR = 8
WE = (EC * 2 * FI) + E


def expert_counts(count, sem):
    def each(name, per=1, ahead=2, ring=2):
        return [count(f"ex_{name}{u}", per, ahead) for u in range(ring)]

    return dict(
        weights=sem("ex_weights"), x_in=each("x_in", 16, ring=XR), y_out=each("y_out", 16, 0, YR),
        tp=each("tp"), xT=each("xT"), up=each("up"), silu=each("silu"), h=each("h"),
        ht=each("ht"), hT=each("hT"), dn=each("dn"), y=each("y"),
    )


def experts(nc, a, sc, c, passed, ident, tiles, weights, acc, acc_in):
    with ExitStack() as es:
        def ring(k, name, shape, dt=F32):
            return [es.enter_context(nc.sbuf_tensor(f"ex_{name}{u}", shape, dt)) for u in range(k)]

        def banks(name):
            return [es.enter_context(nc.psum_tensor(f"ex_{name}{u}", [P, 512], F32)) for u in range(2)]

        x, xT = ring(XR, "x", [P, ROWW]), ring(2, "xT", [P, EC, P])
        sg, h, hT, y = ring(2, "sg", [P, FI]), ring(2, "h", [P, FI]), ring(2, "hT", [FI, P]), ring(YR, "y", [P, E])
        tp, up, hp, dp = banks("tp"), banks("up"), banks("hp"), banks("dp")
        tp_, up_ = [b[:, 0:E].rearrange("p (c q) -> p c q", c=EC) for b in tp], [b[:, 0:2 * FI].rearrange("p (c i) -> p c i", c=2) for b in up]
        block = es.enter_context(nc.Block())
        U = XR

        def step(name, v):
            return c[name][v % len(c[name])]

        def fixed(it):
            return lambda name, v: step(name, v).value((U * it + v) // len(c[name]))

        def loop(eng, body, peel=1):
            for n in range(peel * U):
                body(n % U, n // U, fixed(n // U), n < U, False)
            with eng.Fori(peel, TILES // U - 1) as it:
                held = {}

                def at(name, v):
                    k, ring = step(name, v), len(c[name])
                    key = (k.per, k.ahead, ring, v // ring)
                    if key not in held:
                        held[key] = eng.snap(k.value(it * (U // ring) + v // ring))
                    return held[key]

                for u in range(U):
                    body(u, it, at, False, False)
            for u in range(U):
                body(u, TILES // U - 1, fixed(TILES // U - 1), False, True)

        def entry(eng, which, n, top):
            return eng.value_load(tiles[0:1, which, bass.ds(n, 1)], min_val=0, max_val=top)

        @block.sync
        def _(sp):
            def load(n, u):
                sp.dma_start(x[u][:, :], sc["slots"][bass.ds(entry(sp, 0, n, PADS), P), :]).then_inc(c["x_in"][u].sem, 16)

            for u in range(U):
                load(u, u)

            def body(u, it, at, first, last):
                if first and u < B:
                    sp.dma_start(acc[:, u, :, :], sc["base"][u]).then_inc(acc_in, 16)
                if not last:
                    sp.wait_ge(step("y_out", u).sem, at("y_out", u))
                    load(it * U + (U + u), u)

            loop(sp, body)

        @block.gpsimd
        def _(g):
            def body(u, it, at, first, last):
                g.wait_ge(step("y", u).sem, at("y", u))
                stand_alone(g, passed)
                g.indirect_dma_start(sc["y"], bass.IndirectOffsetOnAxis(ap=x[u][:, E + 1:E + 2].bitcast(U32), axis=0),
                                     y[u % YR][:, :], None, bounds_check=NY - 1, oob_is_err=False).then_inc(step("y_out", u).sem, 16)

            loop(g, body)
            for u in range(YR):
                g.wait_ge(c["y_out"][u].sem, c["y_out"][u].value(TILES // YR - 1))

        @block.scalar
        def _(s):
            def hT_out(v, at, first):
                s.wait_ge(step("ht", v).sem, at("ht", v))
                if not (first and v < 2):
                    s.wait_ge(step("dn", v - 2).sem, at("dn", v - 2))
                s.copy(hT[v % 2][:, :], hp[v % 2][:, 0:P]).then_inc(step("hT", v).sem, 1)

            def xT_out(v, at):
                s.wait_ge(step("tp", v).sem, at("tp", v))
                s.copy(xT[v % 2][:, :, :], tp_[v % 2]).then_inc(step("xT", v).sem, 1)

            def body(u, it, at, first, last):
                s.wait_ge(step("up", u).sem, at("up", u))
                s.activation(sg[u % 2][:, :], up_[u % 2][:, 0, :], ACT.Silu).then_inc(step("silu", u).sem, 1)
                if not (last and u >= U - 2):
                    xT_out(u + 2, at)
                if u or not first:
                    hT_out(u - 1, at, first)

            xT_out(0, fixed(0))
            xT_out(1, fixed(0))
            loop(s, body)
            hT_out(U - 1, fixed(TILES // U - 1), False)

        @block.vector
        def _(v):
            def weigh(w, at, used):
                v.wait_ge(step("dn", w).sem, at("dn", w))
                if used:
                    v.wait_ge(step("y_out", w).sem, at("y_out", w - YR))
                v.tensor_scalar(y[w % YR][:, :], dp[w % 2][:, 0:E], x[w % U][:, E:E + 1], None, ALU.mult).then_inc(step("y", w).sem, 1)

            def body(u, it, at, first, last):
                w = u - 2
                v.wait_ge(step("silu", u).sem, at("silu", u))
                v.tensor_tensor(h[u % 2][:, :], sg[u % 2][:, :], up_[u % 2][:, 1, :], ALU.mult).then_inc(step("h", u).sem, 1)
                if w >= 0 or not first:
                    weigh(w, at, not first or w >= YR)

            loop(v, body)
            for w in (U - 2, U - 1):
                weigh(w, fixed(TILES // U - 1), True)

        @block.tensor
        def _(t):
            def x_back(v, at):
                t.wait_ge(step("x_in", v).sem, at("x_in", v))
                for i in range(EC):
                    last = t.transpose(tp_[v % 2][:, i, :], x[v % U][:, i * P:(i + 1) * P], ident[:, :])
                last.then_inc(step("tp", v).sem, 1)

            def weights_of(n):
                return entry(t, 1, n, (NE - 1) * WE)

            def down(v, at, w, first):
                t.wait_ge(step("hT", v).sem, at("hT", v))
                if not (first and v < 2):
                    t.wait_ge(step("y", v - 2).sem, at("y", v - 2))
                t.matmul(dp[v % 2][:, 0:E], hT[v % 2][:, :], weights[:, bass.ds(w + EC * 2 * FI, E)],
                         start=True, stop=True).then_inc(step("dn", v).sem, 1)

            held = {}

            def h_back(v, at):
                t.wait_ge(step("h", v).sem, at("h", v))
                t.transpose(hp[v % 2][:, 0:P], h[v % 2][:, :], ident[:, :]).then_inc(step("ht", v).sem, 1)

            def body(u, it, at, first, last):
                held[u] = weights_of(it * U + u)
                t.wait_ge(step("xT", u).sem, at("xT", u))
                for i in range(EC):
                    mm = t.matmul(up[u % 2][:, 0:2 * FI], xT[u % 2][:, i, :],
                                  weights[:, bass.ds(held[u] + i * 2 * FI, 2 * FI)], start=(i == 0), stop=(i == EC - 1))
                mm.then_inc(step("up", u).sem, 1)
                if not (last and u >= U - 2):
                    x_back(u + 2, at)
                if u or not first:
                    h_back(u - 1, at)
                if u >= 2 or not first:
                    if u < 2:
                        held[u - 2] = weights_of(it * U + (u - 2))
                    down(u - 2, at, held[u - 2], first)

            x_back(0, fixed(0))
            x_back(1, fixed(0))
            t.wait_ge(c["weights"], 16 * B)
            loop(t, body)
            end = fixed(TILES // U - 1)
            h_back(U - 1, end)
            for v in (U - 2, U - 1):
                down(v, end, weights_of(TILES - U + v), False)


CR = 4
CV = 3


def combine_counts(count, sem):
    def each(name):
        return [count(f"co_{name}{u}", 16) for u in range(CR)]

    return dict(acc_in=sem("co_acc_in"), y_in=each("y_in"), yp_in=each("yp_in"), out=sem("co_out"),
                add=count("co_add", TOPK), addp=count("co_addp", TOPK))


def combine(nc, a, sc, c, passed, acc, out):
    U = CR
    with ExitStack() as es:
        y = [es.enter_context(nc.sbuf_tensor(f"yy{u}", [P, TB, TOPK, E], F32)) for u in range(U)]
        block = es.enter_context(nc.Block())
        y_rows = sc["y"].rearrange("(n t p j) e -> n p t (j e)", t=TB, j=TOPK, p=P)
        out_rows = out.rearrange("(n t p) e -> n p t e", t=TB, p=P)

        @block.sync
        def _(sp):
            def load(n, u):
                for k, tiles in ((c["y_in"], slice(0, CV)), (c["yp_in"], slice(CV, TB))):
                    sp.dma_start(y[u][:, tiles, :, :].rearrange("p t j e -> p t (j e)"),
                                 y_rows[n, :, tiles]).then_inc(k[u].sem, 16)

            for n in range(B):
                if n >= U:
                    for k in (c["add"], c["addp"]):
                        sp.wait_ge(k.sem, k.value(n - U))
                load(n, n % U)

        @block.scalar
        def _(s):
            with s.Fori(0, B) as n:
                for k in (c["add"], c["addp"]):
                    s.wait_ge(k.sem, k.value(n))
                s.dma_start(out_rows[bass.ds(n, 1)].rearrange("o p t e -> (o p) t e"),
                            acc[:, bass.ds(n, 1), :, :].rearrange("p o t e -> p (o t) e")).then_inc(c["out"], 16)
            s.wait_ge(c["out"], 16 * B)

        def sums(eng, k, rows_in, tiles):
            eng.wait_ge(c["acc_in"], 16 * B)
            with eng.Fori(0, B // U) as it:
                for u in range(U):
                    n = it * U + u
                    eng.wait_ge(rows_in[u].sem, rows_in[u].value(it))
                    for j in range(TOPK):
                        if j:
                            eng.wait_ge(k.sem, k.value(n, j))
                        stand_alone(eng, passed)
                        total = acc[:, bass.ds(n, 1), tiles, :].rearrange("p o t e -> p (o t) e")
                        eng.tensor_tensor(total, total, y[u][:, tiles, j, :], ALU.add).then_inc(k.sem, 1)

        @block.vector
        def _(v):
            sums(v, c["add"], c["y_in"], slice(0, CV))

        @block.gpsimd
        def _(g):
            sums(g, c["addp"], c["yp_in"], slice(CV, TB))


def shape_constants():
    bucket = np.searchsorted(BUCKET_STARTS, np.arange(S), side="right") - 1
    rel = P - 1 - NEAR_LO - np.arange(DIAG)
    of = np.where(rel > 0, BUCKETS // 2, 0) + bucket[np.abs(rel)]
    onehot_diag = (of[None, :] == np.arange(BUCKETS)[:, None]).astype(np.float32)
    u = np.arange(S)[None, :] - P * np.arange(TB)[:, None]
    far = np.where(u < NEAR_LO, BUCKETS - 1, np.where(u >= NEAR_LO + NEAR_W, BUCKETS // 2 - 1, -1)).reshape(-1)
    onehot_far = (far[None, :] == np.arange(BUCKETS)[:, None]).astype(np.float32)
    blocks = (np.arange(S)[None, :] // P == np.arange(TB)[:, None]).astype(np.float32)
    krows = np.concatenate([np.ones((3, S), np.float32), blocks, blocks, blocks])
    g = np.arange(NG)
    return dict(
        eye=np.eye(P, dtype=np.float32), onehot_diag=onehot_diag, onehot_far=onehot_far, krows=krows,
        before=np.triu(np.ones((P, P), np.float32), 1),
        earlier=np.broadcast_to((g[None, :] < g[:, None]).astype(np.float32).reshape(1, -1), (P, NG * NG)).copy(),
        regions=np.broadcast_to(np.arange(NE, dtype=np.float32)[None, :] * REG, (P, NE)).copy(),
    )


def arrays_of(i):
    n = lambda k: np.asarray(i[k])
    t = np.ascontiguousarray
    gu = n("L0_ffn_experts_gate_up")
    shared = np.concatenate([n("L0_ffn_shared_gate_w"), n("L0_ffn_shared_up_w")])
    return dict(
        x=t(n("x").reshape(B * S, E)), ctxT=t(n("ctx_1024").reshape(B * S, E).T),
        wq=t(n("L0_xattn_Wq")), wkv=t(n("L0_xattn_Wkv")), wo=t(n("L0_xattn_Wo")),
        rel_bias=t(n("L0_xattn_rel_bias").T), gateT=t(n("L0_ffn_gate_weight").T),
        ebias=t(n("L0_ffn_e_score_correction_bias").reshape(1, NE)),
        experts=t(np.concatenate([gu.reshape(NE, 2 * FI, EC, P).transpose(3, 0, 2, 1).reshape(P, NE, -1),
                                  n("L0_ffn_experts_down").transpose(2, 0, 1)], axis=2).reshape(P, -1)),
        shared=t(shared.reshape(2 * SI, EC, P).transpose(2, 1, 0)),
        shared_dn=t(n("L0_ffn_shared_down_w").reshape(E, SI // P, P).transpose(2, 1, 0)),
        **shape_constants(),
    )


def kernel(**inputs):
    import concourse.bacc as bacc
    from concourse.bass_utils import run_bass_kernel_spmd

    nc = bacc.Bacc("TRN2", target_bir_lowering=False, num_devices=1)
    arrays = arrays_of(inputs)
    a = {k: nc.dram_tensor("in_" + k, v.shape, mybir.dt.from_np(v.dtype), kind="ExternalInput").ap() for k, v in arrays.items()}
    out = nc.dram_tensor("out", (B * S, E), F32, kind="ExternalOutput").ap()
    build(nc, a, out)
    r = run_bass_kernel_spmd(nc, [{"in_" + k: v for k, v in arrays.items()}], core_ids=[0])
    return r.results[0]["out"].reshape(B, S, E)
```
